# Optimizing a Trainium2 kernel written in Bass

```python
import numpy as np
import jax
import jax.numpy as jnp

def _softmax(x, axis=-1):
    return jax.nn.softmax(x, axis=axis)

def _gelu(x):
    return jax.nn.gelu(x, approximate=True)

def _silu(x):
    return jax.nn.silu(x)

def _sigmoid(x):
    return jax.nn.sigmoid(x)

def _layernorm(x, axis=-1, eps=1e-05):
    m = jnp.mean(x, axis=axis, keepdims=True)
    v = jnp.var(x, axis=axis, keepdims=True)
    return (x - m) / jnp.sqrt(v + eps)

def _scatter_add(tgt, idx, src, axis=0):
    return tgt.at[idx].add(src)

def _segment_sum(src, seg, n):
    return jax.ops.segment_sum(src, seg, n)
kernel_name = 'mk_gnn_preln_d4_gnn_r8_634df8'

def setup_inputs(seed: int=0):
    np.random.seed(seed)
    _w = jnp.asarray

    def _rec_inputs():
        import jax
        import jax.numpy as jnp
        _gk = jax.random.key(seed)
        x = -0.0005121 + 1.001 * jax.random.normal(jax.random.fold_in(_gk, 1), (6250, 64), jnp.float32)
        src = jax.random.randint(jax.random.fold_in(_gk, 2), (200000,), 0, 6250, jnp.int32)
        dst = jax.random.randint(jax.random.fold_in(_gk, 3), (200000,), 0, 6250, jnp.int32)
        _o = jnp.argsort(dst, stable=True)
        src = src[_o]
        dst = dst[_o]
        edge_attr_48 = 5.93493e-05 + 1.00006 * jax.random.normal(jax.random.fold_in(_gk, 13), (200000, 48), jnp.float32)
        edge_attr_64 = -8.62073e-06 + 0.999901 * jax.random.normal(jax.random.fold_in(_gk, 14), (200000, 64), jnp.float32)
        edge_type_16 = jax.random.randint(jax.random.fold_in(_gk, 16), (200000,), 0, 16, jnp.int32)
        return (x, src, dst, edge_attr_48, edge_attr_64, edge_type_16)
    x, src, dst, edge_attr_48, edge_attr_64, edge_type_16 = _rec_inputs()

    def _L0_gnn_setup():
        import jax, jax.numpy as jnp
        import numpy as np
        N_NODES = 6250
        N_EDGES = 62500
        IN_DIM = 64
        OUT_DIM = 64
        NUM_RELS = 16
        key = jax.random.key(seed)
        ks = jax.random.split(key, 8)
        h = jax.random.normal(ks[0], (N_NODES, IN_DIM), dtype=jnp.float32)
        he = jax.random.normal(ks[1], (N_EDGES, IN_DIM), dtype=jnp.float32)
        src = jax.random.randint(ks[2], (N_EDGES,), 0, N_NODES)
        dst = jax.random.randint(ks[3], (N_EDGES,), 0, N_NODES)
        rel = jax.random.randint(ks[4], (N_EDGES,), 0, NUM_RELS)
        W_shared = jax.random.normal(ks[5], (OUT_DIM, IN_DIM), dtype=jnp.float32) * (2.0 / (IN_DIM + OUT_DIM)) ** 0.5
        W_attn = jax.random.normal(ks[6], (1, 3 * OUT_DIM), dtype=jnp.float32) * (2.0 / (3 * OUT_DIM + 1)) ** 0.5
        W_rel = jax.random.normal(ks[7], (NUM_RELS, IN_DIM, OUT_DIM), dtype=jnp.float32) * (2.0 / (IN_DIM + OUT_DIM)) ** 0.5
        return {'h': h, 'he': he, 'src': src, 'dst': dst, 'rel': rel, 'W_shared': W_shared, 'W_attn': W_attn, 'W_rel': W_rel}
    _L0_gnn_all = _L0_gnn_setup()
    _L0_gnn_in = {k: v for k, v in _L0_gnn_all.items() if k in ('W_shared', 'W_attn', 'W_rel')}
    del _L0_gnn_all

    def _L1_gnn_setup():
        import jax, jax.numpy as jnp
        import numpy as np
        N_NODES = 12500
        N_EDGES = 156250
        D_FEAT = 64

        def _aggregate(x, src, dst, num_nodes):
            return jax.ops.segment_sum(x[src], dst, num_segments=num_nodes)
        key = jax.random.key(seed)
        kx, ke = jax.random.split(key)
        x = jax.random.normal(kx, (N_NODES, D_FEAT), dtype=jnp.float32)
        edge_index = jax.random.randint(ke, (2, N_EDGES), 0, N_NODES, dtype=jnp.int64)
        return {'x': x, 'edge_index': edge_index}
    _L1_gnn_all = _L1_gnn_setup()
    _L1_gnn_in = {k: v for k, v in _L1_gnn_all.items() if k in ()}
    del _L1_gnn_all

    def _L2_gnn_setup():
        import jax, jax.numpy as jnp
        import numpy as np
        N_NODES = 6250

        def _gcn_conv(x, W, b, src, dst, dinv, n):
            h = x @ W
            norm = dinv[src] * dinv[dst]
            msg = h[src] * norm[:, None]
            out = jax.ops.segment_sum(msg, dst, num_segments=n)
            return out + b
        key = jax.random.key(seed)
        ks = jax.random.split(key, 10)
        n, e, cin, chid = (N_NODES, 75000, 64, 128)
        x = jax.random.normal(ks[0], (n, cin), dtype=jnp.float32)
        edge_index = jax.random.randint(ks[1], (2, e), 0, n, dtype=jnp.int64)

        def glorot(k, fi, fo):
            s = jnp.sqrt(6.0 / (fi + fo)).astype(jnp.float32)
            return jax.random.uniform(k, (fi, fo), jnp.float32, -s, s)
        return {'x': x, 'edge_index': edge_index, 'W1': glorot(ks[2], cin, chid), 'b1': jnp.zeros((chid,), jnp.float32), 'W2': glorot(ks[3], chid, cin), 'b2': jnp.zeros((cin,), jnp.float32), 'W3': glorot(ks[4], cin, chid), 'b3': jnp.zeros((chid,), jnp.float32), 'W4': glorot(ks[5], chid, cin), 'b4': jnp.zeros((cin,), jnp.float32)}
    _L2_gnn_all = _L2_gnn_setup()
    _L2_gnn_in = {k: v for k, v in _L2_gnn_all.items() if k in ('W1', 'b1', 'W2', 'b2', 'W3', 'b3', 'W4', 'b4')}
    del _L2_gnn_all

    def _L3_gnn_setup():
        import jax, jax.numpy as jnp
        import numpy as np
        N_NODES = 12500
        N_EDGES = 200000
        NODE_D = 64
        EDGE_D = 48
        U_D = 32
        N_GRAPHS = 64
        HIDDEN = 128
        OUT_D = 64
        IN_D = NODE_D + EDGE_D + U_D
        key = jax.random.key(seed)
        ks = jax.random.split(key, 10)
        x = jax.random.normal(ks[0], (N_NODES, NODE_D), dtype=jnp.float32)
        edge_index = jax.random.randint(ks[1], (2, N_EDGES), 0, N_NODES, dtype=jnp.int64)
        edge_attr = jax.random.normal(ks[2], (N_EDGES, EDGE_D), dtype=jnp.float32)
        u = jax.random.normal(ks[3], (N_GRAPHS, U_D), dtype=jnp.float32)
        batch = jnp.sort(jax.random.randint(ks[4], (N_NODES,), 0, N_GRAPHS, dtype=jnp.int64))
        W1 = jax.random.normal(ks[5], (IN_D, HIDDEN), dtype=jnp.float32) / np.sqrt(IN_D)
        b1 = jnp.zeros((HIDDEN,), dtype=jnp.float32)
        W2 = jax.random.normal(ks[6], (HIDDEN, HIDDEN), dtype=jnp.float32) / np.sqrt(HIDDEN)
        b2 = jnp.zeros((HIDDEN,), dtype=jnp.float32)
        W3 = jax.random.normal(ks[7], (HIDDEN, OUT_D), dtype=jnp.float32) / np.sqrt(HIDDEN)
        b3 = jnp.zeros((OUT_D,), dtype=jnp.float32)
        return {'x': x, 'edge_index': edge_index, 'edge_attr': edge_attr, 'u': u, 'batch': batch, 'W1': W1, 'b1': b1, 'W2': W2, 'b2': b2, 'W3': W3, 'b3': b3}
    _L3_gnn_all = _L3_gnn_setup()
    _L3_gnn_in = {k: v for k, v in _L3_gnn_all.items() if k in ('u', 'W1', 'b1', 'W2', 'b2', 'W3', 'b3')}
    del _L3_gnn_all
    return {'x': x, 'src': src, 'dst': dst, 'edge_attr_48': edge_attr_48, 'edge_attr_64': edge_attr_64, 'edge_type_16': edge_type_16, 'L0_gnn_W_shared': _L0_gnn_in['W_shared'], 'L0_gnn_W_attn': _L0_gnn_in['W_attn'], 'L0_gnn_W_rel': _L0_gnn_in['W_rel'], 'L2_gnn_W1': _L2_gnn_in['W1'], 'L2_gnn_b1': _L2_gnn_in['b1'], 'L2_gnn_W2': _L2_gnn_in['W2'], 'L2_gnn_b2': _L2_gnn_in['b2'], 'L2_gnn_W3': _L2_gnn_in['W3'], 'L2_gnn_b3': _L2_gnn_in['b3'], 'L2_gnn_W4': _L2_gnn_in['W4'], 'L2_gnn_b4': _L2_gnn_in['b4'], 'L3_gnn_u': _L3_gnn_in['u'], 'L3_gnn_W1': _L3_gnn_in['W1'], 'L3_gnn_b1': _L3_gnn_in['b1'], 'L3_gnn_W2': _L3_gnn_in['W2'], 'L3_gnn_b2': _L3_gnn_in['b2'], 'L3_gnn_W3': _L3_gnn_in['W3'], 'L3_gnn_b3': _L3_gnn_in['b3']}

def reference(x, src, dst, edge_attr_48, edge_attr_64, edge_type_16, L0_gnn_W_shared, L0_gnn_W_attn, L0_gnn_W_rel, L2_gnn_W1, L2_gnn_b1, L2_gnn_W2, L2_gnn_b2, L2_gnn_W3, L2_gnn_b3, L2_gnn_W4, L2_gnn_b4, L3_gnn_u, L3_gnn_W1, L3_gnn_b1, L3_gnn_W2, L3_gnn_b2, L3_gnn_W3, L3_gnn_b3):
    import jax
    import jax.numpy as jnp

    def _L0_gnn_ref(h, he, src, dst, rel, W_shared, W_attn, W_rel):
        import jax, jax.numpy as jnp
        import numpy as np
        N_NODES = 6250
        N_EDGES = 62500
        IN_DIM = 64
        OUT_DIM = 64
        NUM_RELS = 16
        Z = h @ W_shared.T
        ze = he @ W_shared.T
        Wa_s, Wa_e, Wa_d = jnp.split(W_attn, 3, axis=1)
        a = Z[src] @ Wa_s.T + ze @ Wa_e.T + Z[dst] @ Wa_d.T
        H_all = jnp.einsum('ni,rio->nro', h, W_rel)
        msg = H_all[src, rel] * a
        out = jax.ops.segment_sum(msg, dst, num_segments=N_NODES)
        return jax.nn.relu(out)

    def _L1_gnn_ref(x, edge_index):
        import jax, jax.numpy as jnp
        import numpy as np
        N_NODES = 12500
        N_EDGES = 156250
        D_FEAT = 64

        def _aggregate(x, src, dst, num_nodes):
            return jax.ops.segment_sum(x[src], dst, num_segments=num_nodes)
        num_nodes = x.shape[0]
        src, dst = (edge_index[0], edge_index[1])
        h = _aggregate(x, src, dst, num_nodes)
        h = jax.nn.relu(h)
        h = _aggregate(h, src, dst, num_nodes)
        return h

    def _L2_gnn_ref(x, edge_index, W1, b1, W2, b2, W3, b3, W4, b4):
        import jax, jax.numpy as jnp
        import numpy as np
        N_NODES = 6250

        def _gcn_conv(x, W, b, src, dst, dinv, n):
            h = x @ W
            norm = dinv[src] * dinv[dst]
            msg = h[src] * norm[:, None]
            out = jax.ops.segment_sum(msg, dst, num_segments=n)
            return out + b
        n = x.shape[0]
        loop = jnp.arange(n, dtype=edge_index.dtype)
        src = jnp.concatenate([edge_index[0], loop])
        dst = jnp.concatenate([edge_index[1], loop])
        deg = jax.ops.segment_sum(jnp.ones_like(dst, dtype=x.dtype), dst, num_segments=n)
        dinv = jnp.where(deg > 0, jax.lax.rsqrt(deg), 0.0)
        x_l1 = jax.nn.relu(_gcn_conv(x, W1, b1, src, dst, dinv, n))
        x_l2 = jax.nn.relu(_gcn_conv(x_l1, W2, b2, src, dst, dinv, n))
        x_l1_td = jax.nn.relu(_gcn_conv(x_l2, W3, b3, src, dst, dinv, n)) + x_l1
        x_out = jax.nn.relu(_gcn_conv(x_l1_td, W4, b4, src, dst, dinv, n)) + x
        return x_out

    def _L3_gnn_ref(x, edge_index, edge_attr, u, batch, W1, b1, W2, b2, W3, b3):
        import jax, jax.numpy as jnp
        import numpy as np
        N_NODES = 12500
        N_EDGES = 200000
        NODE_D = 64
        EDGE_D = 48
        U_D = 32
        N_GRAPHS = 64
        HIDDEN = 128
        OUT_D = 64
        IN_D = NODE_D + EDGE_D + U_D
        n = x.shape[0]
        seg = edge_index[0]
        sums = jax.ops.segment_sum(edge_attr, seg, num_segments=n)
        cnt = jax.ops.segment_sum(jnp.ones((edge_attr.shape[0],), edge_attr.dtype), seg, num_segments=n)
        v_e = sums / jnp.maximum(cnt, 1.0)[:, None]
        comb = jnp.concatenate([x, v_e, u[batch]], axis=1)
        h = jax.nn.relu(comb @ W1 + b1)
        h = jax.nn.relu(h @ W2 + b2)
        return h @ W3 + b3
    edge_index = jnp.stack([src, dst])
    batch0 = jnp.zeros((6250,), jnp.int32)
    h = jnp.maximum(_layernorm(x, axis=-1), 0.0)
    x = x + _L0_gnn_ref(h, edge_attr_64, src, dst, edge_type_16, L0_gnn_W_shared, L0_gnn_W_attn, L0_gnn_W_rel)
    h = jnp.maximum(_layernorm(x, axis=-1), 0.0)
    x = x + _L1_gnn_ref(h, edge_index)
    h = jnp.maximum(_layernorm(x, axis=-1), 0.0)
    x = x + _L2_gnn_ref(h, edge_index, L2_gnn_W1, L2_gnn_b1, L2_gnn_W2, L2_gnn_b2, L2_gnn_W3, L2_gnn_b3, L2_gnn_W4, L2_gnn_b4)
    h = jnp.maximum(_layernorm(x, axis=-1), 0.0)
    x = x + _L3_gnn_ref(h, edge_index, edge_attr_48, L3_gnn_u, batch0, L3_gnn_W1, L3_gnn_b1, L3_gnn_W2, L3_gnn_b2, L3_gnn_W3, L3_gnn_b3)
    return x

_drawn_inputs = setup_inputs


def setup_inputs(seed=0):
    import zlib

    import numpy as np

    out = dict(_drawn_inputs(seed))
    spreads = {'L2_gnn_b1': (0.0, 0.8),
     'L2_gnn_b2': (0.0, 2.0),
     'L2_gnn_b3': (0.0, 2.0),
     'L2_gnn_b4': (0.0, 2.0),
     'L3_gnn_b1': (0.0, 2.0),
     'L3_gnn_b2': (0.0, 2.0),
     'L3_gnn_b3': (0.0, 2.0)}
    factors = {'edge_attr_48': 8.0,
     'L2_gnn_W1': 8.0,
     'L2_gnn_W2': 8.0,
     'L2_gnn_W3': 8.0,
     'L2_gnn_W4': 8.0,
     'L3_gnn_u': 8.0,
     'L3_gnn_W1': 8.0,
     'L3_gnn_W2': 8.0,
     'L3_gnn_W3': 8.0}
    for name, (base, spread) in spreads.items():
        noise = np.random.default_rng([zlib.crc32(name.encode()), seed]).standard_normal(out[name].shape)
        drawn = base * np.exp(spread * noise) if base else spread * noise
        out[name] = jnp.asarray(drawn.astype(out[name].dtype))
    for name, factor in factors.items():
        out[name] = (out[name] * factor).astype(out[name].dtype)
    return out
```

```python
import concourse.bass as bass
from concourse import mybir
from contextlib import ExitStack, contextmanager

N = 6250
E = 200000
D = 64
D48 = 48
R = 16
HID = 128
P = 128
BT = 4
NB = -(-N // (BT * P))
NT = NB * BT
NP = NT * P
NROW = NP + P
PAD_NODE = N + 50
K = 4
NC = -(-E // (P * K)) * K
ROUNDS = NC // K
ET = -(-NC // P)
NCT = ET * P
FULL = E // P
TAIL = E - FULL * P
EPS = 1e-5


class Chain:

    def __init__(self, eng, sem):
        self.eng, self.sem = eng, sem
        self.base, self.i, self.per, self.k = 0, None, 0, 0

    def link(self, ins):
        ins.then_inc(self.sem, 1)
        self.k += 1
        at = self.base + self.k
        self.eng.wait_ge(self.sem, at if self.i is None else self.i * self.per + at)

    @contextmanager
    def over(self, trips, per):
        self.base, self.k = self.base + self.k, 0
        with self.eng.Fori(0, trips) as i:
            self.i, self.per = i, per
            yield i
        assert self.k == per, (self.k, per)
        self.base, self.i, self.k = self.base + per * trips, None, 0


def build(nc, A, out):
    f32, f16, i32 = mybir.dt.float32, mybir.dt.float16, mybir.dt.int32
    ALU, ACT, AX = mybir.AluOpType, mybir.ActivationFunctionType, mybir.AxisListType
    ctx = ExitStack()
    with ctx:
        def sb(name, shape, dt=f32):
            return ctx.enter_context(nc.sbuf_tensor(name, shape, dt))

        def sem(name):
            return ctx.enter_context(nc.semaphore(name))

        def dram(name, shape, dt=f32):
            return nc.dram_tensor(name, shape, dt, kind="Internal").ap()

        bank = [ctx.enter_context(nc.psum_tensor(f"bank{i}", [P, 512], f32)) for i in range(8)]

        rel_table = dram("rel_table", [NP * R, 2 * D])
        x_table = dram("x_table", [NP, D])
        l0_sums = [dram(f"l0_sums{k}", [NROW, 2 * D + 1]) for k in range(K)]
        agg_sums = [[dram(f"agg_sums{s}_{k}", [NROW, D]) for k in range(K)] for s in range(2)]
        l3_sums = [dram(f"l3_sums{k}", [NROW, D48 + 1]) for k in range(K)]

        ident = sb("ident", [P, P])
        ident16 = sb("ident16", [P, P], f16)
        before = sb("before", [P, P])
        discard_row = sb("discard_row", [P, 1])
        zeros = sb("zeros", [P, 848])
        w_shared = sb("w_shared", [D, D])
        w_attn = sb("w_attn", [D, 3])
        w_rel = sb("w_rel", [D, R, D])
        v_cols = sb("v_cols", [D, 3])
        v_sd = sb("v_sd", [D, 2])
        ve_row = sb("ve_row", [P, D])
        g_w1, g_w2 = sb("g_w1", [D, HID]), sb("g_w2", [HID, D])
        g_w3, g_w4 = sb("g_w3", [D, HID]), sb("g_w4", [HID, D])
        g_b1, g_b3 = sb("g_b1", [HID, 1]), sb("g_b3", [HID, 1])
        g_b2, g_b4 = sb("g_b2", [P, D]), sb("g_b4", [P, D])
        m_w1x, m_w1e, m_w1u = sb("m_w1x", [D, HID]), sb("m_w1e", [D48, HID]), sb("m_w1u", [32, HID])
        m_u = sb("m_u", [32, 1])
        m_w2, m_w3 = sb("m_w2", [HID, HID]), sb("m_w3", [HID, D])
        m_b1, m_b2, m_b3 = sb("m_b1", [HID, 1]), sb("m_b2", [HID, 1]), sb("m_b3", [P, D])
        m_c1 = sb("m_c1", [HID, 1])
        x = sb("x", [P, NT, D])
        h = sb("h", [P, NT, D])
        U = sb("U", [P, NT, D])
        G = sb("G", [P, NT, D])
        ld = [sb(f"ld{i}", [P, NT, D]) for i in range(2)]
        hid_T = sb("hid_T", [HID, NP])
        mean, var, dinv, cnt = (sb(n, [P, NT]) for n in ("mean", "var", "dinv", "cnt"))
        ldc = sb("ldc", [P, NT])
        s12 = sb("s12", [P, NT, 2])
        eps = sb("eps", [P, 1])
        early = [hid_T[:, q * NCT:(q + 1) * NCT] for q in range(4)]
        idx_stage = early[0].bitcast(i32).rearrange("p (t c) -> p t c", c=P)
        idx_f = early[1].rearrange("p (t c) -> p t c", c=P)
        rel_f = sb("rel_f", [P, NCT])
        src_f, dst_f = (sb(n, [P, NCT]) for n in ("src_f", "dst_f"))
        src_first, dst_first = sb("src_first", [P, NCT]), sb("dst_first", [P, NCT])
        key16 = {k: (sb(f"{k}_hi16", [P, NCT], f16), sb(f"{k}_lo16", [P, NCT], f16)) for k in ("src", "dst")}
        dup = {"src": early[2], "dst": early[3]}
        z = sb("z", [P, NCT])
        he = [sb(f"he{i}", [P, 8, D]) for i in range(2)]
        prod = [sb(f"prod{i}", [P, 8, D]) for i in range(2)]
        scratch = [sb(f"scratch{i}", [P, P]) for i in range(2)]
        gather_idx = [sb(f"gather_idx{k}", [P, 1], i32) for k in range(K)]
        scatter_idx = [sb(f"scatter_idx{k}", [P, 1], i32) for k in range(K)]
        raw = [sb(f"raw{k}", [P, 2 * D + 1]) for k in range(K)]
        raw3 = [sb(f"raw3_{k}", [P, D48 + 1]) for k in range(K)]
        same = [sb(f"same{k}", [P, P]) for k in range(K)]
        comb = [sb(f"comb{k}", [P, 2 * D + 1]) for k in range(K)]
        hT = sb("hT", [D, 512])
        rel_stage = [ld[i][:].rearrange("p t d -> p (t d)")[:, 0:R * 2 * D].rearrange("p (r d) -> p r d", r=R) for i in range(2)]
        stg = sb("stg", [P, BT, D])
        stgh = sb("stgh", [P, BT, D])
        stg_e = sb("stg_e", [P, BT, D48])
        vT, veT = sb("vT", [D, 512]), sb("veT", [D48, 512])
        xs, xs2 = sb("xs", [HID, 512]), sb("xs2", [HID, 512])

        S = {}

        def s(name):
            if name not in S:
                S[name] = sem(name)
            return S[name]

        block = ctx.enter_context(nc.Block())

        col1 = lambda v: v.rearrange("(k a) -> k a", a=1)
        small = [(w_shared[:], A["L0_gnn_W_shared"]), (w_attn[:], A["L0_gnn_W_attn"].rearrange("a (k o) -> o (a k)", o=D)),
                 (w_rel[:], A["L0_gnn_W_rel"].rearrange("r i o -> i r o")),
                 (g_w1[:], A["L2_gnn_W1"]), (g_w2[:], A["L2_gnn_W2"]), (g_w3[:], A["L2_gnn_W3"]), (g_w4[:], A["L2_gnn_W4"]),
                 (g_b1[:], col1(A["L2_gnn_b1"])), (g_b3[:], col1(A["L2_gnn_b3"])),
                 (g_b2[:], A["L2_gnn_b2"].partition_broadcast(P)), (g_b4[:], A["L2_gnn_b4"].partition_broadcast(P)),
                 (m_w1x[:], A["L3_gnn_W1"][0:D, :]), (m_w1e[:], A["L3_gnn_W1"][D:D + D48, :]),
                 (m_w1u[:], A["L3_gnn_W1"][D + D48:D + D48 + 32, :]), (m_u[:], A["L3_gnn_u"][0:1, :].rearrange("a k -> k a")),
                 (m_w2[:], A["L3_gnn_W2"]), (m_w3[:], A["L3_gnn_W3"]),
                 (m_b1[:], col1(A["L3_gnn_b1"])), (m_b2[:], col1(A["L3_gnn_b2"])), (m_b3[:], A["L3_gnn_b3"].partition_broadcast(P))]

        def he_piece(c0, n):
            return A["edge_attr_64"][c0 * P:(c0 + n) * P, :].rearrange("(c p) d -> p c d", p=P)

        HE_ROUNDS = FULL // 16
        HE_REST = FULL - HE_ROUNDS * 16
        NODE_TAIL = N - (N // P) * P
        WHOLE = N // P

        def zero_table(eng, table, width, signal):
            flat = table.rearrange("(p a) d -> p (a d)", p=P)
            total, at, n = (NROW // P) * width, 0, 0
            while at < total:
                w = min(848, total - at)
                eng.dma_start(flat[:, at:at + w], zeros[:, 0:w]).then_inc(signal, 16)
                at, n = at + w, n + 1
            return n

        def node_rows(table):
            return table[0:NP, :].rearrange("(t p) d -> p t d", p=P)

        PASSES = [("l0", 2 * D + 1, "dst")] + [(f"agg{j}", D, "dst") for j in range(6)] + [("l3", D48 + 1, "src")]

        def sums(j):
            name = PASSES[j][0]
            return l0_sums if name == "l0" else l3_sums if name == "l3" else agg_sums[j % 2]

        ld_reads = [K * j for j in range(len(PASSES))]
        ld_counts, upto = [], [0, 0]
        for name, _, _ in PASSES:
            ld_counts.append([])
            for k in range(K):
                upto[k % 2] += {"l0": 3, "l3": 2}.get(name, 1)
                ld_counts[-1].append(upto[k % 2])

        @block.sync
        def _(sp):
            for dst_ap, src_ap in small:
                sp.dma_start(dst_ap, src_ap, allow_slow_non_contiguous=True).then_inc(s("small_loaded"), 16)
            sp.wait_ge(s("memset_done"), 1)
            sp.dma_start(x[:, 0:WHOLE, :], A["x"][0:WHOLE * P, :].rearrange("(t p) d -> p t d", p=P)).then_inc(s("x_loaded"), 16)
            sp.dma_start(x[0:NODE_TAIL, WHOLE, :], A["x"][WHOLE * P:N, :]).then_inc(s("x_loaded"), 16)
            for n, name in enumerate(("src", "dst", "edge_type_16")):
                if n:
                    sp.wait_ge(s("idx_cast"), n)
                a = A[name]
                whole = (ET - 1) * P * P
                rest = FULL - (ET - 1) * P
                sp.dma_start(idx_stage[:, 0:ET - 1, :], a[0:whole].rearrange("(t c p) -> c t p", c=P, p=P)).then_inc(s("idx_loaded"), 16)
                sp.dma_start(idx_stage[0:rest, ET - 1, :], a[whole:FULL * P].rearrange("(c p) -> c p", p=P)).then_inc(s("idx_loaded"), 16)
                sp.dma_start(idx_stage[rest:rest + 1, ET - 1, 0:TAIL], a[FULL * P:E].rearrange("(c p) -> c p", p=TAIL)).then_inc(s("idx_loaded"), 16)
            with sp.Fori(0, HE_ROUNDS) as i:
                for q in range(2):
                    sp.wait_ge(s("he_free"), i * 2 + q + 1)
                    sp.dma_start(he[q][:], A["edge_attr_64"][bass.ds((i * 2 + q) * 8 * P, 8 * P), :].rearrange("(c p) d -> p c d", p=P)).then_inc(s(f"he_loaded{q}"), 16)
            sp.wait_ge(s("he_free"), HE_ROUNDS * 2 + 1)
            sp.dma_start(he[0][:, 0:8, :], he_piece(HE_ROUNDS * 16, 8)).then_inc(s("he_loaded0"), 16)
            sp.wait_ge(s("he_free"), HE_ROUNDS * 2 + 2)
            rest2 = HE_REST - 8
            sp.dma_start(he[1][:, 0:rest2, :], he_piece(HE_ROUNDS * 16 + 8, rest2)).then_inc(s("he_loaded1"), 16)
            sp.dma_start(he[1][0:TAIL, rest2, :], A["edge_attr_64"][FULL * P:E, :]).then_inc(s("he_loaded1"), 16)
            nz = 0
            for t in l0_sums:
                nz += zero_table(sp, t, 2 * D + 1, s("zeroed"))
            for t in agg_sums[1]:
                nz += zero_table(sp, t, D, s("zeroed"))
            for t in l3_sums:
                nz += zero_table(sp, t, D48 + 1, s("zeroed"))
            sp.wait_ge(s("zeroed"), 16 * nz)
            with sp.Fori(0, NB) as b:
                for q in range(BT):
                    sp.wait_ge(s("rel_staged"), b * BT + q + 1)
                    sp.dma_start(rel_table[bass.ds((b * BT + q) * P * R, P * R), :].rearrange("(p r) d -> p r d", r=R),
                                 rel_stage[q % 2]).then_inc(s(f"rel_stored{q % 2}"), 16)
            sp.wait_ge(s("rel_stored0"), 16 * NT // 2)
            sp.wait_ge(s("rel_stored1"), 16 * NT // 2)
            sp.sem_inc(s("table_ready"), 1)

            for j, (name, width, key) in enumerate(PASSES):
                if name == "l3":
                    with sp.Fori(0, ROUNDS - 1) as i:
                        for k in range(K):
                            sp.wait_ge(s("comb_done"), i * K + k + 1 + j * NC)
                            sp.dma_start(raw3[k][:, 0:D48], A["edge_attr_48"][bass.ds((i * K + k) * P, P), :]).then_inc(s(f"edges_loaded{k}"), 16)
                    for k in range(K):
                        c = (ROUNDS - 1) * K + k
                        sp.wait_ge(s("comb_done"), c + 1 + j * NC)
                        n = max(0, min(P, E - c * P))
                        if n:
                            sp.dma_start(raw3[k][0:n, 0:D48], A["edge_attr_48"][c * P:c * P + n, :]).then_inc(s(f"edges_loaded{k}"), 16)
                        else:
                            sp.sem_inc(s(f"edges_loaded{k}"), 16)
                if name.startswith("agg") and PASSES[j + 1][0].startswith("agg"):
                    for t in sums(j + 1):
                        sp_n = zero_table(sp, t, D, s("zeroed"))
                        nz += sp_n
                    sp.wait_ge(s("zeroed"), 16 * nz)
                    sp.sem_inc(s("sums_zero"), 1)
                if name == "l0":
                    sp.sem_inc(s("sums_zero"), 1)
                for k in range(K):
                    sp.wait_ge(s(f"scattered{k}"), 16 * ROUNDS * (j + 1))
                for k in range(K):
                    rows = node_rows(sums(j)[k])
                    if name == "l0":
                        pieces = [(ld[0][:], rows[:, :, 0:D]), (ld[1][:], rows[:, :, D:2 * D]), (ldc[:], rows[:, :, 2 * D])]
                    elif name == "l3":
                        pieces = [(ld[k % 2][:, :, 0:D48], rows[:, :, 0:D48]), (ldc[:], rows[:, :, D48])]
                    else:
                        pieces = [(ld[k % 2][:], rows)]
                    if name in ("l0", "l3"):
                        sp.wait_ge(s("ld_read"), ld_reads[j] + k)
                    elif k >= 2:
                        sp.wait_ge(s("ld_read"), ld_reads[j] + k - 1)
                    for buf, view in pieces:
                        sp.dma_start(buf, view, allow_slow_non_contiguous=True).then_inc(s(f"ld_done{k % 2}"), 16)
                sp.wait_ge(s("ld_read"), ld_reads[j] + K)
                if name != "l3" and j < 6:
                    sp.wait_ge(s("u_ready"), j + 1)
                    sp.dma_start(node_rows(x_table), U[:]).then_inc(s("x_table_stored"), 16)
                    sp.wait_ge(s("x_table_stored"), 16 * (j + 1))
                    sp.sem_inc(s("table_ready"), 1)
            sp.wait_ge(s("out_ready"), 1)
            sp.dma_start(out[0:WHOLE * P, :].rearrange("(t p) d -> p t d", p=P), G[:, 0:WHOLE, :]).then_inc(s("out_stored"), 16)
            sp.dma_start(out[WHOLE * P:N, :], G[0:NODE_TAIL, WHOLE, :]).then_inc(s("out_stored"), 16)
            sp.wait_ge(s("out_stored"), 32)

        @block.gpsimd
        def _(pool):
            ch = Chain(pool, s("pool_chain"))
            ch.link(pool.memset(ident[:], 0.0))
            ch.link(pool.memset(before[:], 1.0))
            ch.link(pool.affine_select(out=ident[:], in_=ident[:], compare_op=ALU.not_equal, fill=1.0, base=0,
                                       pattern=[[-1, P]], channel_multiplier=1))
            ch.link(pool.affine_select(out=before[:], in_=before[:], compare_op=ALU.is_gt, fill=0.0, base=0,
                                       pattern=[[-1, P]], channel_multiplier=1))
            ch.link(pool.iota(discard_row[:], pattern=[[0, 1]], base=NP, channel_multiplier=1, allow_small_or_imprecise_dtypes=True))
            pool.tensor_copy(ident16[:], ident[:]).then_inc(s("const_ready"), 1)

            pool.wait_ge(s("tables_i32"), 1)
            for j, (name, width, key) in enumerate(PASSES):
                if name != "l3":
                    pool.wait_ge(s("table_ready"), j + 1)
                if name.startswith("agg"):
                    pool.wait_ge(s("sums_zero"), j)
                with pool.Fori(0, ROUNDS) as i:
                    c1 = [i * K + k + 1 + j * NC for k in range(K)]
                    if name != "l3":
                        src_ap = rel_table if name == "l0" else x_table
                        for k in range(K):
                            pool.wait_ge(s("gather_idx_ready"), c1[k])
                            pool.wait_ge(s("comb_done"), c1[k])
                            pool.sem_inc(s("pool_turn"), 1)
                            pool.indirect_dma_start(raw[k][:, 0:width - 1 if name == "l0" else width], None, src_ap,
                                                    bass.IndirectOffsetOnAxis(ap=gather_idx[k][:], axis=0)).then_inc(s(f"gathered{k}"), 16)
                    for k in range(K):
                        pool.wait_ge(s("comb_ready"), c1[k] + 2)
                        pool.sem_inc(s("pool_turn"), 1)
                        pool.indirect_dma_start(sums(j)[k], bass.IndirectOffsetOnAxis(ap=scatter_idx[k][:], axis=0),
                                                comb[k][:, 0:width], None, compute_op=ALU.add,
                                                bounds_check=NROW - 1).then_inc(s(f"scattered{k}"), 16)

        @block.scalar
        def _(act):
            ch = Chain(act, s("act_chain"))
            act.sem_inc(s("comb_ready"), 2)
            act.wait_ge(s("memset_done"), 1)

            def rstd(n):
                act.wait_ge(s("var_ready"), n)
                act.activation(var[:], var[:], ACT.Sqrt, bias=eps[:], scale=1.0 / D).then_inc(s("std_ready"), 1)

            def edge_pass(j):
                name, width, key = PASSES[j]
                idx = rel_f if name == "l0" else src_f
                first = dst_first if key == "dst" else src_first
                with act.Fori(0, ROUNDS) as i:
                    dma_free = i * 16 + j * ROUNDS * 16
                    c1 = [i * K + k + 1 + j * NC for k in range(K)]
                    for k in range(K if name != "l3" else 0):
                        act.wait_ge(s(f"gathered{k}"), dma_free)
                        act.copy(gather_idx[k][:], idx[:, bass.ds(i * K + k, 1)]).then_inc(s("gather_idx_ready"), 1)
                    for k in range(K):
                        act.wait_ge(s(f"scattered{k}"), dma_free)
                        act.copy(scatter_idx[k][:], first[:, bass.ds(i * K + k, 1)])
                        act.wait_ge(s("comb_done"), c1[k] + K)
                        act.copy(comb[k][:, 0:width], bank[2 + k % 2][:, 0:width]).then_inc(s("comb_ready"), 1)

            act.wait_ge(s("tables_i32"), 1)
            rstd(1)
            with act.Fori(0, NB) as b:
                act.wait_ge(s("h_T"), b + 1)
                act.copy(hT[:], bank[0][0:D, :]).then_inc(s("hT_ready"), 1)
                for q in range(BT):
                    act.wait_ge(s("rel_mm"), b * BT + q + 1)
                    act.wait_ge(s(f"rel_stored{q % 2}"), (b * 2 + q // 2) * 16)
                    for half in range(2):
                        ins = act.copy(rel_stage[q % 2][:, half * 8:half * 8 + 8, D:2 * D],
                                       bank[1 + half][:, :].rearrange("p (r o) -> p r o", o=D))
                    ins.then_inc(s("rel_h"), 1)
            edge_pass(0)
            rstd(2)
            edge_pass(1)
            edge_pass(2)
            rstd(3)
            act.wait_ge(s("deg_ready"), 1)
            act.activation(dinv[:], cnt[:], ACT.Sqrt).then_inc(s("deg_sqrt"), 1)
            edge_pass(3)

            def dense(n, bias):
                with act.Fori(0, NB) as b:
                    if True:
                        act.wait_ge(s("dense_T"), b + n * NB)
                    act.copy(stg[:], G[:, bass.ds(b * BT, BT), :]).then_inc(s("dense_staged"), 1)
                    act.wait_ge(s("dense_mm1"), b + 1 + n * NB)
                    act.activation(xs[:], bank[1][:], ACT.Relu, bias=bias[:]).then_inc(s("dense_relu"), 1)

            act.wait_ge(s("g_ready"), 1)
            dense(0, g_b1)
            edge_pass(4)
            edge_pass(5)
            act.wait_ge(s("g_ready"), 2)
            dense(1, g_b3)
            edge_pass(6)
            rstd(4)
            edge_pass(7)
            act.wait_ge(s("u_bias_mm"), 1)
            act.activation(m_c1[:], bank[0][:, 0:1], ACT.Identity, bias=m_b1[:]).then_inc(s("c1_ready"), 1)
            act.wait_ge(s("c1_ready"), 1)
            act.wait_ge(s("ve_ready"), 1)
            with act.Fori(0, NB) as b:
                act.wait_ge(s("mlp_T"), b)
                act.copy(stg[:], h[:, bass.ds(b * BT, BT), :])
                act.copy(stg_e[:], ld[0][:, bass.ds(b * BT, BT), 0:D48]).then_inc(s("mlp_staged"), 1)
                act.wait_ge(s("mlp_mm1"), b + 1)
                act.activation(xs[:], bank[2][:], ACT.Relu, bias=m_c1[:]).then_inc(s("mlp_h1"), 1)
                act.wait_ge(s("mlp_mm2"), b + 1)
                act.activation(xs2[:], bank[3][:], ACT.Relu, bias=m_b2[:]).then_inc(s("mlp_h2"), 1)

        @block.vector
        def _(v):
            ch = Chain(v, s("dve_chain"))
            link = ch.link
            v.sem_inc(s("he_free"), 2)
            v.sem_inc(s("dup_done"), 8)
            v.sem_inc(s("same_ready"), 2)
            for t in (zeros[:], x[:], z[:], dup["src"], dup["dst"], he[0][:], he[1][:], idx_stage):
                v.memset(t, 0)
            for k in range(K):
                v.memset(raw[k][:], 1.0)
                v.memset(raw3[k][:], 1.0)
            link(v.memset(eps[:], EPS))
            v.memset(idx_stage[:, ET - 1, :], PAD_NODE).then_inc(s("memset_done"), 1)

            groups = [(g, min(4, ET - g * 4)) for g in range(-(-ET // 4))]
            done = 0
            for n, (tab, pad) in enumerate(((src_f, None), (dst_f, None), (rel_f, None))):
                v.wait_ge(s("idx_loaded"), 48 * (n + 1))
                if n:
                    v.wait_ge(s("idx_T"), len(groups) * n)
                v.tensor_copy(idx_f, idx_stage).then_inc(s("idx_cast"), 1)
                for g, w in groups:
                    v.wait_ge(s("idx_T"), len(groups) * n + g + 1)
                    link(v.tensor_copy(tab[:, g * 512:g * 512 + w * P], bank[g][:, 0:w * P]))
            link(v.tensor_scalar(rel_f[:], rel_f[:], float(R - 1), None, ALU.min))
            link(v.scalar_tensor_tensor(rel_f[:], src_f[:], float(R), rel_f[:], ALU.mult, ALU.add))
            for name, tab in (("src", src_f), ("dst", dst_f)):
                hi, lo = key16[name]
                tmp = idx_stage.rearrange("p t c -> p (t c)")
                tmpf = idx_f.rearrange("p t c -> p (t c)")
                link(v.tensor_copy(tmp, tab[:]))
                link(v.tensor_scalar(tmp, tmp, P - 1, None, ALU.bitwise_and))
                link(v.tensor_copy(tmpf, tmp))
                link(v.tensor_copy(lo[:], tmpf))
                link(v.tensor_tensor(hi[:], tab[:], tmpf, ALU.subtract))
            v.tensor_copy(scratch[0][:, 0:1], dst_f[:, 0:1]).then_inc(s("keys_ready"), 1)

            v.wait_ge(s("ve_mm"), 1)
            link(v.tensor_copy(ve_row[:], bank[5][:, 0:D]))
            v.tensor_copy(v_cols[:], bank[4][0:D, 0:3]).then_inc(s("v_cols_ready"), 1)

            def z_piece(n, q, cols, dst_ap):
                v.wait_ge(s("he_free"), n + 1)
                link(v.tensor_tensor(prod[q][:, 0:cols, :], he[q][:, 0:cols, :],
                                     ve_row[:].unsqueeze(1).to_broadcast([P, cols, D]), ALU.mult))
                v.reduce_sum(dst_ap, prod[q][:, 0:cols, :], axis=AX.X).then_inc(s("he_free"), 1)

            with ch.over(HE_ROUNDS, 2) as i:
                for q in range(2):
                    v.wait_ge(s(f"he_loaded{q}"), i * 16 + 16)
                    z_piece(i * 2 + q, q, 8, z[:, bass.ds((i * 2 + q) * 8, 8)])
            v.wait_ge(s("he_loaded0"), HE_ROUNDS * 16 + 16)
            z_piece(HE_ROUNDS * 2, 0, 8, z[:, HE_ROUNDS * 16:HE_ROUNDS * 16 + 8])
            v.wait_ge(s("he_loaded1"), HE_ROUNDS * 16 + 32)
            z_piece(HE_ROUNDS * 2 + 1, 1, HE_REST - 7, z[:, HE_ROUNDS * 16 + 8:FULL + 1])

            with v.Fori(0, ROUNDS) as i:
                for k in range(K):
                    for m, (name, tab) in enumerate((("src", src_f), ("dst", dst_f))):
                        v.wait_ge(s("dup_row"), i * 8 + 2 * k + m + 1)
                        col = bass.ds(i * K + k, 1)
                        v.wait_ge(s("dup_done"), i * 8 + 2 * k + m + 7)
                        v.scalar_tensor_tensor(scratch[m][:], bank[2 * k + m][:, 0:P], tab[:, col], before[:],
                                               ALU.is_equal, ALU.mult, accum_out=dup[name][:, col]).then_inc(s("dup_done"), 1)
            v.wait_ge(s("dup_done"), 8 + 2 * NC)
            for name, tab, first in (("src", src_f, src_first), ("dst", dst_f, dst_first)):
                tmpf = idx_f.rearrange("p t c -> p (t c)")
                link(v.tensor_scalar(tmpf, tab[:], discard_row[:], None, ALU.subtract))
                link(v.tensor_scalar(dup[name], dup[name], 1.0, None, ALU.min))
                link(v.tensor_tensor(tmpf, tmpf, dup[name], ALU.mult))
                link(v.tensor_tensor(first[:], tab[:], tmpf, ALU.subtract))
            v.tensor_copy(scratch[0][:, 0:1], dst_f[:, 0:1]).then_inc(s("tables_i32"), 1)

            stat = lambda t: t[:].unsqueeze(2).to_broadcast([P, NT, D])

            def layernorm(n):
                link(v.reduce_sum(mean[:], x[:], axis=AX.X))
                link(v.tensor_scalar(mean[:], mean[:], 1.0 / D, None, ALU.mult))
                link(v.tensor_tensor(h[:], x[:], stat(mean), ALU.subtract))
                link(v.tensor_tensor(G[:], h[:], h[:], ALU.mult))
                v.reduce_sum(var[:], G[:], axis=AX.X).then_inc(s("var_ready"), 1)
                v.wait_ge(s("std_ready"), n)
                link(v.reciprocal(var[:], var[:]))
                link(v.tensor_tensor(h[:], h[:], stat(var), ALU.mult))
                ins = v.tensor_scalar(h[:], h[:], 0.0, None, ALU.max)
                return ins

            def edge_pass(j):
                name, width, key = PASSES[j]
                tab = dst_f if key == "dst" else src_f
                with v.Fori(0, ROUNDS) as i:
                    c1 = [i * K + k + 1 + j * NC for k in range(K)]

                    def same_rows(k):
                        v.wait_ge(s("key_row"), c1[k])
                        v.wait_ge(s("comb_done"), c1[k])
                        v.tensor_scalar(same[k][:], bank[k % 2][:, 0:P], tab[:, bass.ds(i * K + k, 1)], None,
                                        ALU.is_equal).then_inc(s("same_ready"), 1)

                    def message(k):
                        if name == "l0":
                            v.wait_ge(s(f"gathered{k}"), i * 16 + 16)
                            v.scalar_tensor_tensor(raw[k][:, 0:D], raw[k][:, D:2 * D], z[:, bass.ds(i * K + k, 1)],
                                                   raw[k][:, 0:D], ALU.mult, ALU.add).then_inc(s("message_ready"), 1)
                    for op, k in ((same_rows, 0), (same_rows, 1), (message, 0), (same_rows, 2), (message, 1),
                                  (same_rows, 3), (message, 2), (message, 3)):
                        op(k)
                for k in range(K):
                    n0 = ld_counts[j][k]
                    v.wait_ge(s(f"ld_done{k % 2}"), 16 * n0)
                    if name == "l0":
                        ops = [(G[:], ld[0][:]), (U[:], ld[1][:]), (cnt[:], ldc[:])]
                    elif name == "l3":
                        ops = [(G[:, :, 0:D48], ld[k % 2][:, :, 0:D48]), (cnt[:], ldc[:])]
                    else:
                        ops = [(G[:], ld[k % 2][:])]
                    for m, (acc, part) in enumerate(ops):
                        ins = v.tensor_copy(acc, part) if k == 0 else v.tensor_tensor(acc, acc, part, ALU.add)
                        if m < len(ops) - 1:
                            link(ins)
                    ins.then_inc(s("ld_read"), 1)
                    v.wait_ge(s("ld_read"), ld_reads[j] + k + 1)

            v.wait_ge(s("x_loaded"), 32)
            layernorm(1).then_inc(s("h_ready"), 1)
            v.wait_ge(s("small_loaded"), 16 * len(small))
            v.wait_ge(s("v_cols_ready"), 1)
            link(v.tensor_copy(v_sd[:, 0:1], v_cols[:, 0:1]))
            v.tensor_copy(v_sd[:, 1:2], v_cols[:, 2:3]).then_inc(s("v_sd_ready"), 1)
            v.wait_ge(s("h_ready"), 1)
            with ch.over(NB, 2 * BT) as b:
                v.wait_ge(s("h_T"), b)
                v.tensor_copy(stgh[:], h[:, bass.ds(b * BT, BT), :]).then_inc(s("h_staged"), 1)
                for q in range(BT):
                    v.wait_ge(s("rel_mm"), b * BT + q + 1)
                    v.wait_ge(s("rel_h"), b * BT + q + 1)
                    link(v.tensor_copy(s12[:, bass.ds(b * BT + q, 1), :], bank[3][:, 0:2].unsqueeze(1)))
                    link(v.tensor_tensor(rel_stage[q % 2][:, :, 0:D], rel_stage[q % 2][:, :, D:2 * D],
                                         s12[:, bass.ds(b * BT + q, 1), 0:1].to_broadcast([P, R, D]), ALU.mult))
                    v.sem_inc(s("rel_staged"), 1)

            edge_pass(0)
            link(v.tensor_tensor(U[:], U[:], s12[:, :, 1:2].to_broadcast([P, NT, D]), ALU.mult))
            link(v.tensor_tensor(G[:], G[:], U[:], ALU.add))
            link(v.tensor_scalar(G[:], G[:], 0.0, None, ALU.max))
            link(v.tensor_tensor(x[:], x[:], G[:], ALU.add))
            link(v.tensor_scalar(cnt[:], cnt[:], 1.0, None, ALU.add))
            link(layernorm(2))
            v.tensor_copy(U[:], h[:]).then_inc(s("u_ready"), 1)
            edge_pass(1)
            v.tensor_scalar(U[:], G[:], 0.0, None, ALU.max).then_inc(s("u_ready"), 1)
            edge_pass(2)
            link(v.tensor_tensor(x[:], x[:], G[:], ALU.add))
            link(layernorm(3))
            v.sem_inc(s("deg_ready"), 1)
            v.wait_ge(s("deg_sqrt"), 1)
            link(v.reciprocal(dinv[:], dinv[:]))
            v.tensor_tensor(U[:], h[:], stat(dinv), ALU.mult).then_inc(s("u_ready"), 1)

            def gcn_sum(j):
                edge_pass(j)
                link(v.tensor_tensor(G[:], G[:], U[:], ALU.add))
                return v.tensor_tensor(G[:], G[:], stat(dinv), ALU.mult)

            def dense(n):
                with ch.over(NB, 1 - n) as b:
                    v.wait_ge(s("dense_T"), b + 1 + n * NB)
                    v.tensor_copy(vT[:], bank[0][0:D, :]).then_inc(s("dense_vT"), 1)
                    v.wait_ge(s("dense_relu"), b + 1 + n * NB)
                    blk = bass.ds(b * 512, 512)
                    if n == 0:
                        link(v.tensor_copy(hid_T[:, blk], xs[:]))
                        v.sem_inc(s("dense_x"), 1)
                    else:
                        v.tensor_tensor(xs[:], xs[:], hid_T[:, blk], ALU.add).then_inc(s("dense_x"), 1)
                    v.wait_ge(s("dense_mm2"), b + 1 + n * NB)
                    v.tensor_tensor(U[:, bass.ds(b * BT, BT), :], bank[2][:, 0:BT * D].rearrange("p (t d) -> p t d", d=D),
                                    dinv[:, bass.ds(b * BT, BT)].unsqueeze(2).to_broadcast([P, BT, D]),
                                    ALU.mult).then_inc(s("dense_u"), 1)
                v.wait_ge(s("dense_u"), (n + 1) * NB)
                v.sem_inc(s("u_ready"), 1)

            gcn_sum(3).then_inc(s("g_ready"), 1)
            dense(0)
            link(gcn_sum(4))
            link(v.tensor_tensor(G[:], G[:], g_b2[:].unsqueeze(1).to_broadcast([P, NT, D]), ALU.add))
            link(v.tensor_scalar(G[:], G[:], 0.0, None, ALU.max))
            v.tensor_tensor(U[:], G[:], stat(dinv), ALU.mult).then_inc(s("u_ready"), 1)
            gcn_sum(5).then_inc(s("g_ready"), 1)
            dense(1)
            link(gcn_sum(6))
            link(v.tensor_tensor(G[:], G[:], g_b4[:].unsqueeze(1).to_broadcast([P, NT, D]), ALU.add))
            link(v.tensor_scalar(G[:], G[:], 0.0, None, ALU.max))
            link(v.tensor_tensor(G[:], G[:], h[:], ALU.add))
            link(v.tensor_tensor(x[:], x[:], G[:], ALU.add))
            link(layernorm(4))
            edge_pass(7)
            link(v.tensor_scalar(cnt[:], cnt[:], 1.0, None, ALU.max))
            link(v.reciprocal(cnt[:], cnt[:]))
            v.tensor_tensor(ld[0][:, :, 0:D48], G[:, :, 0:D48], cnt[:].unsqueeze(2).to_broadcast([P, NT, D48]),
                            ALU.mult).then_inc(s("ve_ready"), 1)
            v.wait_ge(s("ve_ready"), 1)
            with ch.over(NB, 1) as b:
                v.wait_ge(s("mlp_T"), b + 1)
                link(v.tensor_copy(vT[:], bank[0][0:D, :]))
                v.tensor_copy(veT[:], bank[1][0:D48, :]).then_inc(s("mlp_vT"), 1)
                v.wait_ge(s("mlp_mm3"), b + 1)
                blk = bass.ds(b * BT, BT)
                v.tensor_tensor(G[:, blk, :], bank[4][:, 0:BT * D].rearrange("p (t d) -> p t d", d=D), x[:, blk, :],
                                ALU.add).then_inc(s("mlp_y"), 1)
            v.wait_ge(s("mlp_y"), NB)
            v.tensor_tensor(G[:], G[:], m_b3[:].unsqueeze(1).to_broadcast([P, NT, D]), ALU.add).then_inc(s("out_ready"), 1)

        @block.tensor
        def _(pe):
            pe.sem_inc(s("comb_done"), K)
            pe.wait_ge(s("const_ready"), 1)
            pe.wait_ge(s("small_loaded"), 16 * len(small))
            pe.matmul(bank[4][0:D, 0:3], w_shared[:], w_attn[:], start=True, stop=True)
            pe.matmul(bank[5][:, 0:D], w_attn[:, 1:2].to_broadcast([D, P]), w_shared[:], start=True, stop=True).then_inc(s("ve_mm"), 1)
            groups = [(g, min(4, ET - g * 4)) for g in range(-(-ET // 4))]
            for n in range(3):
                pe.wait_ge(s("idx_cast"), n + 1)
                for g, w in groups:
                    for t in range(w):
                        ins = pe.transpose(bank[g][:, t * P:t * P + P], idx_f[:, g * 4 + t, :], ident[:])
                    ins.then_inc(s("idx_T"), 1)
            pe.wait_ge(s("keys_ready"), 1)
            pe.wait_ge(s("v_cols_ready"), 1)

            def key_row(dst_bank, name, col):
                hi, lo = key16[name]
                pe.matmul(dst_bank[:, 0:P], hi[:, col].to_broadcast([P, P]), ident16[:], start=True, stop=False)
                return pe.matmul(dst_bank[:, 0:P], lo[:, col].to_broadcast([P, P]), ident16[:], start=False, stop=True)

            with pe.Fori(0, ROUNDS) as i:
                for k in range(K):
                    for m, name in enumerate(("src", "dst")):
                        pe.wait_ge(s("dup_done"), i * 8 + 2 * k + m + 1)
                        key_row(bank[2 * k + m], name, bass.ds(i * K + k, 1)).then_inc(s("dup_row"), 1)
            pe.wait_ge(s("dup_done"), 8 + 2 * NC)

            pe.wait_ge(s("v_sd_ready"), 1)
            with pe.Fori(0, NB) as b:
                pe.wait_ge(s("h_staged"), b + 1)
                pe.wait_ge(s("hT_ready"), b)
                pe.sem_inc(s("pe_turn"), 1)
                for q in range(BT):
                    ins = pe.transpose(bank[0][0:D, q * P:q * P + P], stgh[:, q, :], ident[:])
                ins.then_inc(s("h_T"), 1)
                pe.wait_ge(s("hT_ready"), b + 1)
                for q in range(BT):
                    pe.wait_ge(s("rel_staged"), b * BT + q)
                    tile = hT[:, q * P:q * P + P]
                    pe.matmul(bank[1][:], tile, w_rel[:, 0:8, :].rearrange("i r o -> i (r o)"), start=True, stop=True)
                    pe.matmul(bank[2][:], tile, w_rel[:, 8:16, :].rearrange("i r o -> i (r o)"), start=True, stop=True)
                    pe.matmul(bank[3][:, 0:2], tile, v_sd[:], start=True, stop=True).then_inc(s("rel_mm"), 1)
            pe.wait_ge(s("rel_staged"), NT)

            def edge_pass(j):
                name, width, key = PASSES[j]
                src_buf = raw3 if name == "l3" else raw
                with pe.Fori(0, ROUNDS) as i:
                    c1 = [i * K + k + 1 + j * NC for k in range(K)]

                    def row(k):
                        pe.wait_ge(s("same_ready"), c1[k])
                        key_row(bank[k % 2], key, bass.ds(i * K + k, 1)).then_inc(s("key_row"), 1)

                    def combine(k):
                        pe.wait_ge(s("same_ready"), c1[k] + 2)
                        if name == "l0":
                            pe.wait_ge(s("message_ready"), c1[k])
                        elif name == "l3":
                            pe.wait_ge(s(f"edges_loaded{k}"), i * 16 + 16)
                        else:
                            pe.wait_ge(s(f"gathered{k}"), i * 16 + 16 * (1 + j * ROUNDS))
                        pe.wait_ge(s("comb_ready"), c1[k])
                        pe.matmul(bank[2 + k % 2][:, 0:width], same[k][:], src_buf[k][:, 0:width],
                                  start=True, stop=True).then_inc(s("comb_done"), 1)
                    for op, k in ((row, 0), (row, 1), (combine, 0), (row, 2), (combine, 1), (row, 3), (combine, 2), (combine, 3)):
                        op(k)

            edge_pass(0)
            edge_pass(1)
            edge_pass(2)
            edge_pass(3)

            def dense(n, wa, wb):
                with pe.Fori(0, NB) as b:
                    at = b + 1 + n * NB
                    pe.wait_ge(s("dense_staged"), at)
                    pe.wait_ge(s("dense_vT"), b + n * NB)
                    pe.sem_inc(s("pe_turn"), 1)
                    for q in range(BT):
                        ins = pe.transpose(bank[0][0:D, q * P:q * P + P], stg[:, q, :], ident[:])
                    ins.then_inc(s("dense_T"), 1)
                    pe.wait_ge(s("dense_vT"), at)
                    pe.matmul(bank[1][:], wa[:], vT[:], start=True, stop=True).then_inc(s("dense_mm1"), 1)
                    pe.wait_ge(s("dense_x"), at)
                    pe.wait_ge(s("dense_u"), b + n * NB)
                    for q in range(BT):
                        ins = pe.matmul(bank[2][:, q * D:q * D + D], xs[:, q * P:q * P + P], wb[:], start=True, stop=True)
                    ins.then_inc(s("dense_mm2"), 1)

            dense(0, g_w1, g_w2)
            edge_pass(4)
            edge_pass(5)
            dense(1, g_w3, g_w4)
            edge_pass(6)
            edge_pass(7)
            pe.matmul(bank[0][:, 0:1], m_w1u[:], m_u[:], start=True, stop=True).then_inc(s("u_bias_mm"), 1)
            pe.wait_ge(s("c1_ready"), 1)
            with pe.Fori(0, NB) as b:
                pe.wait_ge(s("mlp_staged"), b + 1)
                pe.wait_ge(s("mlp_vT"), b)
                pe.sem_inc(s("pe_turn"), 1)
                for q in range(BT):
                    pe.transpose(bank[0][0:D, q * P:q * P + P], stg[:, q, :], ident[:])
                for q in range(BT):
                    ins = pe.transpose(bank[1][0:D48, q * P:q * P + P], stg_e[:, q, :], ident[:])
                ins.then_inc(s("mlp_T"), 1)
                pe.wait_ge(s("mlp_vT"), b + 1)
                pe.matmul(bank[2][:], m_w1x[:], vT[:], start=True, stop=False)
                pe.matmul(bank[2][:], m_w1e[:], veT[:], start=False, stop=True).then_inc(s("mlp_mm1"), 1)
                pe.wait_ge(s("mlp_h1"), b + 1)
                pe.matmul(bank[3][:], m_w2[:], xs[:], start=True, stop=True).then_inc(s("mlp_mm2"), 1)
                pe.wait_ge(s("mlp_h2"), b + 1)
                pe.wait_ge(s("mlp_y"), b)
                for q in range(BT):
                    ins = pe.matmul(bank[4][:, q * D:q * D + D], xs2[:, q * P:q * P + P], m_w3[:], start=True, stop=True)
                ins.then_inc(s("mlp_mm3"), 1)


_INS = ["x", "src", "dst", "edge_attr_48", "edge_attr_64", "edge_type_16", "L0_gnn_W_shared", "L0_gnn_W_attn", "L0_gnn_W_rel",
        "L2_gnn_W1", "L2_gnn_b1", "L2_gnn_W2", "L2_gnn_b2", "L2_gnn_W3", "L2_gnn_b3", "L2_gnn_W4", "L2_gnn_b4",
        "L3_gnn_u", "L3_gnn_W1", "L3_gnn_b1", "L3_gnn_W2", "L3_gnn_b2", "L3_gnn_W3", "L3_gnn_b3"]


def kernel(**inputs):
    import numpy as _np
    import concourse.bacc as _bacc
    from concourse import mybir as _mybir
    from concourse.bass_utils import run_bass_kernel_spmd as _run

    nc = _bacc.Bacc("TRN2", target_bir_lowering=False, num_devices=1)
    arrays, aps = {}, {}
    for name in _INS:
        a = _np.ascontiguousarray(inputs[name])
        arrays[f"in_{name}"] = a
        aps[name] = nc.dram_tensor(f"in_{name}", a.shape, _mybir.dt.from_np(a.dtype), kind="ExternalInput").ap()
    out = nc.dram_tensor("out_0", (N, D), _mybir.dt.float32, kind="ExternalOutput").ap()
    build(nc, aps, out)
    r = _run(nc, [arrays], core_ids=[0])
    return r.results[0]["out_0"]
```

```python
import concourse.bass as bass
from concourse import mybir
from contextlib import ExitStack, contextmanager

N = 6250
E = 200000
D = 64
D48 = 48
R = 16
HID = 128
P = 128
BT = 4
NB = -(-N // (BT * P))
NT = NB * BT
NP = NT * P
NROW = NP + P
PAD_NODE = N + 50
K = 4
NC = -(-E // (P * K)) * K
ROUNDS = NC // K
ET = -(-NC // P)
NCT = ET * P
FULL = E // P
TAIL = E - FULL * P
EPS = 1e-5
SRC_T = -(-N // P)
GN = 16
NG = -(-N // GN)
CG = 6
A_SPLIT = 25
GW = SRC_T * GN
HG = 16
NH = -(-NG // HG)
COUNT_MAX = 16.0
RING = 32
LAG = 3
AHEAD = 5
TG = P // GN
assert NG == ROUNDS and NH % 2 == 1 and RING == TG * K


class Chain:

    def __init__(self, eng, sem):
        self.eng, self.sem = eng, sem
        self.base, self.i, self.per, self.k = 0, None, 0, 0

    def link(self, ins):
        ins.then_inc(self.sem, 1)
        self.k += 1
        at = self.base + self.k
        self.eng.wait_ge(self.sem, at if self.i is None else self.i * self.per + at)

    @contextmanager
    def over(self, trips, per):
        self.base, self.k = self.base + self.k, 0
        with self.eng.Fori(0, trips) as i:
            self.i, self.per = i, per
            yield i
        assert self.k == per, (self.k, per)
        self.base, self.i, self.k = self.base + per * trips, None, 0


def build(nc, A, out):
    f32, f16, i32, i16, f8 = mybir.dt.float32, mybir.dt.float16, mybir.dt.int32, mybir.dt.int16, mybir.dt.float8e4
    ALU, ACT, AX = mybir.AluOpType, mybir.ActivationFunctionType, mybir.AxisListType
    ctx = ExitStack()
    with ctx:
        def sb(name, shape, dt=f32):
            return ctx.enter_context(nc.sbuf_tensor(name, shape, dt))

        def sem(name):
            return ctx.enter_context(nc.semaphore(name))

        def dram(name, shape, dt=f32):
            return nc.dram_tensor(name, shape, dt, kind="Internal").ap()

        bank = [ctx.enter_context(nc.psum_tensor(f"bank{i}", [P, 512], f32)) for i in range(8)]

        rel_table = dram("rel_table", [NP * R, 2 * D])
        x_table = dram("x_table", [NP, D])
        l0_sums = [dram(f"l0_sums{k}", [NROW, 2 * D + 1]) for k in range(K)]
        agg_sums = [[dram(f"agg_sums{s}_{k}", [NROW, D]) for k in range(K)] for s in range(2)]
        l3_sums = [dram(f"l3_sums{k}", [NROW, D48 + 1]) for k in range(K)]

        adjacency = dram("adjacency", [NG * P, GW // 4])
        starts_dram = dram("starts_dram", [4 * P], i32)

        ident = sb("ident", [P, P])
        ident16 = sb("ident16", [P, P], f16)
        before = sb("before", [P, P])
        discard_row = sb("discard_row", [P, 1])
        zeros = sb("zeros", [P, 848])
        w_shared = sb("w_shared", [D, D])
        w_attn = sb("w_attn", [D, 3])
        w_rel = sb("w_rel", [D, R, D])
        v_cols = sb("v_cols", [D, 3])
        v_sd = sb("v_sd", [D, 2])
        ve_row = sb("ve_row", [P, D])
        g_w1, g_w2 = sb("g_w1", [D, HID]), sb("g_w2", [HID, D])
        g_w3, g_w4 = sb("g_w3", [D, HID]), sb("g_w4", [HID, D])
        g_b1, g_b3 = sb("g_b1", [HID, 1]), sb("g_b3", [HID, 1])
        g_b2, g_b4 = sb("g_b2", [P, D]), sb("g_b4", [P, D])
        m_w1x, m_w1e, m_w1u = sb("m_w1x", [D, HID]), sb("m_w1e", [D48, HID]), sb("m_w1u", [32, HID])
        m_u = sb("m_u", [32, 1])
        m_w2, m_w3 = sb("m_w2", [HID, HID]), sb("m_w3", [HID, D])
        m_b1, m_b2, m_b3 = sb("m_b1", [HID, 1]), sb("m_b2", [HID, 1]), sb("m_b3", [P, D])
        m_c1 = sb("m_c1", [HID, 1])
        x = sb("x", [P, NT, D])
        h = sb("h", [P, NT, D])
        U = sb("U", [P, NT, D])
        G = sb("G", [P, NT, D])
        ld_all = sb("ld_all", [P, 2 * NT * D])
        ld = [ld_all[:, i * NT * D:(i + 1) * NT * D].rearrange("p (t d) -> p t d", d=D) for i in range(2)]
        hid_T = sb("hid_T", [HID, NP])
        mean, var, dinv, cnt = (sb(n, [P, NT]) for n in ("mean", "var", "dinv", "cnt"))
        ldc = sb("ldc", [P, NT])
        s12 = sb("s12", [P, NT, 2])
        eps = sb("eps", [P, 1])
        early = [hid_T[:, q * NCT:(q + 1) * NCT] for q in range(4)]
        idx_stage = early[0].bitcast(i32).rearrange("p (t c) -> p t c", c=P)
        idx_f = early[1].rearrange("p (t c) -> p t c", c=P)
        rel_and_z = sb("rel_and_z", [P, 2 * NCT])
        rel_f, z = rel_and_z[:, 0:NCT], rel_and_z[:, NCT:2 * NCT]
        src_f, dst_f = (sb(n, [P, NCT]) for n in ("src_f", "dst_f"))
        src_first, dst_first = sb("src_first", [P, NCT]), sb("dst_first", [P, NCT])
        key16 = {k: (sb(f"{k}_hi16", [P, NCT], f16), sb(f"{k}_lo16", [P, NCT], f16)) for k in ("src", "dst")}
        dup = {"src": early[2], "dst": early[3]}
        he_prod = sb("he_prod", [P, 4 * 8 * D])
        he, prod = ([he_prod[:, i * 8 * D:(i + 1) * 8 * D].rearrange("p (c d) -> p c d", d=D) for i in pair] for pair in ((0, 1), (2, 3)))
        dup4, apart4 = sb("dup4", [P, K]), sb("apart4", [P, K])
        scratch = [sb(f"scratch{i}", [P, P]) for i in range(2)]
        gather_idx4 = sb("gather_idx4", [P, 2 * K], i32)
        gather_idx = [gather_idx4[:, k:k + 1] for k in range(K)]
        scatter_idx = [sb(f"scatter_idx{k}", [P, 1], i32) for k in range(K)]
        raw = [sb(f"raw{k}", [P, 2 * D + 1]) for k in range(K)]
        raw3 = [sb(f"raw3_{k}", [P, D48 + 1]) for k in range(K)]
        same = [sb(f"same{k}", [P, P]) for k in range(K)]
        comb = [sb(f"comb{k}", [P, 2 * D + 1]) for k in range(K)]
        hT = sb("hT", [D, 512])
        rel_stage = [ld_all[:, i * NT * D:i * NT * D + R * 2 * D].rearrange("p (r d) -> p r d", r=R) for i in range(2)]
        stg = sb("stg", [P, BT, D])
        stgh = stg
        stg_e = he[1].rearrange("p c d -> p (c d)")[:, 0:BT * D48].rearrange("p (t d) -> p t d", t=BT)
        veT = he[0][0:D48].rearrange("p c d -> p (c d)")
        xs2 = prod[0].rearrange("p c d -> p (c d)")
        vT, xs = sb("vT", [D, 512]), sb("xs", [HID, 512])

        ones = sb("ones", [P, P])
        twice = sb("twice", [P, D])
        count_key = sb("count_key", [P, SRC_T, GN], i16)
        io128 = sb("io128", [P, P], f16)
        io128f = sb("io128f", [P, P])
        is_group = sb("is_group", [P, 4])
        minus_base = sb("minus_base", [P, NG])
        group_first, group_past = sb("group_first", [P, 4]), sb("group_past", [P, 4])
        first_chunk, last_chunk = sb("first_chunk", [P, 4]), sb("last_chunk", [P, 4])
        first_chunk_i = sb("first_chunk_i", [P, 4], i32)
        starts = sb("starts", [1, 4 * P], i32)
        verdict = sb("verdict", [P, 4])
        flags = sb("flags", [1, 2], i32)
        minus_max = sb("minus_max", [P, 1])
        over_sum = sb("over_sum", [P, 1])
        flat3 = lambda t: t[:].rearrange("p t d -> p (t d)")
        pair_key = flat3(h)[:, 0:NCT]
        minus_group = flat3(h)[:, NCT:2 * NCT]
        RW = 2 * D + 1
        ring = ld_all[:, 0:RING * RW].rearrange("p (c w) -> p c w", w=RW)
        at = RING * RW
        over = ld_all[:, at:at + 2 * NG]
        at += 2 * NG
        count_words = ld_all[:, at:at + GW // 4]
        count_stage = count_words.bitcast(f8)
        at += GW // 4
        over_junk = ld_all[:, at:at + GW // 2].bitcast(f16)
        assert at + GW // 2 <= 2 * NT * D
        at, pair_hot, lo_hot, dst_hot, lo_in, dst_in = 0, [], [], [], [], []
        for q in range(2):
            pair_hot.append(hid_T[:, at:at + CG * GW // 2].bitcast(f16).rearrange("p (c f) -> p c f", c=CG))
            at += CG * GW // 2
            lo_hot.append(hid_T[:, at:at + CG * P // 2].bitcast(f16).rearrange("p (c f) -> p c f", c=CG))
            at += CG * P // 2
            lo_in.append(hid_T[:, at:at + CG])
            dst_in.append(hid_T[:, at + CG:at + 2 * CG])
            at += 2 * CG
            dst_hot.append(he_prod[:, q * CG * P:(q + 1) * CG * P].rearrange("p (c f) -> p c f", c=CG))
        assert at <= NP
        count_bank = [(4, 5), (0, 1)]
        ring_idx = [gather_idx4[:, q * K:(q + 1) * K] for q in range(2)]
        x16 = ld_all[:, 0:SRC_T * P // 2].bitcast(f16).rearrange("p (t f) -> p t f", t=SRC_T)
        half_words = [t[:, 0:HG * GW // 4] for t in (ld_all[:, NT * D:2 * NT * D], rel_and_z[:, :])]
        a_half = [t.bitcast(f8).rearrange("p (g f) -> p g f", g=HG) for t in half_words]
        accT = [sb(f"accT{q}", [P, HG * GN]) for q in range(2)]
        top2, scale_row, unscale, diag = sb("top2", [P, 2, D]), sb("scale_row", [P, D]), sb("unscale", [P, D]), sb("diag", [P, P])
        feature_top, feature_inv = sb("feature_top", [P, 1]), sb("feature_inv", [P, 1])

        S = {}

        def s(name):
            if name not in S:
                S[name] = sem(name)
            return S[name]

        block = ctx.enter_context(nc.Block())

        col1 = lambda v: v.rearrange("(k a) -> k a", a=1)
        small = [(w_shared[:], A["L0_gnn_W_shared"]), (w_attn[:], A["L0_gnn_W_attn"].rearrange("a (k o) -> o (a k)", o=D)),
                 (w_rel[:], A["L0_gnn_W_rel"].rearrange("r i o -> i r o")),
                 (g_w1[:], A["L2_gnn_W1"]), (g_w2[:], A["L2_gnn_W2"]), (g_w3[:], A["L2_gnn_W3"]), (g_w4[:], A["L2_gnn_W4"]),
                 (g_b1[:], col1(A["L2_gnn_b1"])), (g_b3[:], col1(A["L2_gnn_b3"])),
                 (g_b2[:], A["L2_gnn_b2"].partition_broadcast(P)), (g_b4[:], A["L2_gnn_b4"].partition_broadcast(P)),
                 (m_w1x[:], A["L3_gnn_W1"][0:D, :]), (m_w1e[:], A["L3_gnn_W1"][D:D + D48, :]),
                 (m_w1u[:], A["L3_gnn_W1"][D + D48:D + D48 + 32, :]), (m_u[:], A["L3_gnn_u"][0:1, :].rearrange("a k -> k a")),
                 (m_w2[:], A["L3_gnn_W2"]), (m_w3[:], A["L3_gnn_W3"]),
                 (m_b1[:], col1(A["L3_gnn_b1"])), (m_b2[:], col1(A["L3_gnn_b2"])), (m_b3[:], A["L3_gnn_b3"].partition_broadcast(P))]

        def he_piece(c0, n):
            return A["edge_attr_64"][c0 * P:(c0 + n) * P, :].rearrange("(c p) d -> p c d", p=P)

        HE_ROUNDS = FULL // 16
        HE_REST = FULL - HE_ROUNDS * 16
        NODE_TAIL = N - (N // P) * P
        WHOLE = N // P

        def zero_table(eng, table, width, signal):
            flat = table.rearrange("(p a) d -> p (a d)", p=P)
            total, at, n = (NROW // P) * width, 0, 0
            while at < total:
                w = min(848, total - at)
                eng.dma_start(flat[:, at:at + w], zeros[:, 0:w]).then_inc(signal, 16)
                at, n = at + w, n + 1
            return n

        def node_rows(table):
            return table[0:NP, :].rearrange("(t p) d -> p t d", p=P)

        PASSES = [("l0", 2 * D + 1, "dst")] + [(f"agg{j}", D, "dst") for j in range(6)] + [("l3", D48 + 1, "src")]

        FAMILY = ["l0"] + ["agg"] * 6 + ["l3"]
        BEFORE = [0] + list(range(6)) + [0]

        def sums(j):
            name = PASSES[j][0]
            return l0_sums if name == "l0" else l3_sums if name == "l3" else agg_sums[j % 2]

        def loads(j, k):
            per = {"l0": 3, "l3": 2, "agg": 1}[FAMILY[j]]
            return per * (BEFORE[j] * 2 + k // 2 + 1)

        @block.sync
        def _(sp):
            for dst_ap, src_ap in small:
                sp.dma_start(dst_ap, src_ap, allow_slow_non_contiguous=True).then_inc(s("small_loaded"), 16)
            sp.wait_ge(s("memset_done"), 1)
            sp.dma_start(x[:, 0:WHOLE, :], A["x"][0:WHOLE * P, :].rearrange("(t p) d -> p t d", p=P)).then_inc(s("x_loaded"), 16)
            sp.dma_start(x[0:NODE_TAIL, WHOLE, :], A["x"][WHOLE * P:N, :]).then_inc(s("x_loaded"), 16)
            for n, name in enumerate(("src", "dst", "edge_type_16")):
                if n:
                    sp.wait_ge(s("idx_cast"), n)
                a = A[name]
                whole = (ET - 1) * P * P
                rest = FULL - (ET - 1) * P
                sp.dma_start(idx_stage[:, 0:ET - 1, :], a[0:whole].rearrange("(t c p) -> c t p", c=P, p=P)).then_inc(s("idx_loaded"), 16)
                sp.dma_start(idx_stage[0:rest, ET - 1, :], a[whole:FULL * P].rearrange("(c p) -> c p", p=P)).then_inc(s("idx_loaded"), 16)
                sp.dma_start(idx_stage[rest:rest + 1, ET - 1, 0:TAIL], a[FULL * P:E].rearrange("(c p) -> c p", p=TAIL)).then_inc(s("idx_loaded"), 16)
            sp.wait_ge(s("chunks_ready"), 1)
            sp.dma_start(starts_dram.rearrange("(t p) -> p t", p=P), first_chunk_i[:], allow_slow_non_contiguous=True).then_inc(s("starts_out"), 16)
            sp.wait_ge(s("starts_out"), 16)
            sp.dma_start(starts[:], starts_dram.rearrange("(a n) -> a n", a=1)).then_inc(s("starts_in"), 16)
            nz = 0
            for t in l3_sums:
                nz += zero_table(sp, t, D48 + 1, s("l3_zeroed"))
            sp.wait_ge(s("l3_zeroed"), 16 * nz)
            sp.sem_inc(s("l3_go"), 1)

            def l3_edges(r, k):
                sp.wait_ge(s("l3_comb_done"), r * K + (k + 1))
                sp.dma_start(raw3[k][:, 0:D48], A["edge_attr_48"][bass.ds((r * K + k) * P, P), :]).then_inc(s(f"edges_loaded{k}"), 16)

            with sp.Fori(0, HE_ROUNDS) as i:
                for q in range(4):
                    if q % 2 == 0:
                        sp.wait_ge(s("he_free"), i * 2 + q // 2 + 1)
                        sp.dma_start(he[q // 2], A["edge_attr_64"][bass.ds((i * 2 + q // 2) * 8 * P, 8 * P), :].rearrange("(c p) d -> p c d", p=P)).then_inc(s(f"he_loaded{q // 2}"), 16)
                    for k in range(K):
                        l3_edges(i * 4 + q, k)
            sp.wait_ge(s("he_free"), HE_ROUNDS * 2 + 1)
            sp.dma_start(he[0][:, 0:8, :], he_piece(HE_ROUNDS * 16, 8)).then_inc(s("he_loaded0"), 16)
            sp.wait_ge(s("he_free"), HE_ROUNDS * 2 + 2)
            rest2 = HE_REST - 8
            sp.dma_start(he[1][:, 0:rest2, :], he_piece(HE_ROUNDS * 16 + 8, rest2)).then_inc(s("he_loaded1"), 16)
            sp.dma_start(he[1][0:TAIL, rest2, :], A["edge_attr_64"][FULL * P:E, :]).then_inc(s("he_loaded1"), 16)
            for r in range(HE_ROUNDS * 4, ROUNDS):
                for k in range(K):
                    c = r * K + k
                    sp.wait_ge(s("l3_comb_done"), c + 1)
                    n = max(0, min(P, E - c * P))
                    if n:
                        sp.dma_start(raw3[k][0:n, 0:D48], A["edge_attr_48"][c * P:c * P + n, :]).then_inc(s(f"edges_loaded{k}"), 16)
                    else:
                        sp.sem_inc(s(f"edges_loaded{k}"), 16)
            with sp.Fori(0, NB) as b:
                for q in range(BT):
                    sp.wait_ge(s("rel_staged"), b * BT + q + 1)
                    sp.dma_start(rel_table[bass.ds((b * BT + q) * P * R, P * R), :].rearrange("(p r) d -> p r d", r=R),
                                 rel_stage[q % 2]).then_inc(s(f"rel_stored{q % 2}"), 16)
            sp.wait_ge(s("rel_stored0"), 16 * NT // 2)
            sp.wait_ge(s("rel_stored1"), 16 * NT // 2)
            sp.sem_inc(s("rel_ready"), 1)

            def load_sums(j):
                name, fam, b = PASSES[j][0], FAMILY[j], BEFORE[j]
                for k in range(K):
                    sp.wait_ge(s(f"{fam}_scattered{k}"), 16 * ROUNDS * (b + 1))
                for k in range(K):
                    rows = node_rows(sums(j)[k])
                    if name == "l0":
                        pieces = [(ld[0], rows[:, :, 0:D]), (ld[1], rows[:, :, D:2 * D]), (ldc[:], rows[:, :, 2 * D])]
                    elif name == "l3":
                        pieces = [(ld[k % 2][:, :, 0:D48], rows[:, :, 0:D48]), (ldc[:], rows[:, :, D48])]
                    else:
                        pieces = [(ld[k % 2], rows)]
                    if fam in ("l0", "l3"):
                        sp.wait_ge(s(f"{fam}_read"), b * K + k)
                    elif k >= 2:
                        sp.wait_ge(s(f"{fam}_read"), b * K + k - 1)
                    for buf, view in pieces:
                        sp.dma_start(buf, view, allow_slow_non_contiguous=True).then_inc(s(f"{fam}_loaded{k % 2}"), 16)
                sp.wait_ge(s(f"{fam}_read"), b * K + K)

            sp.wait_ge(s("flag1_ready"), 1)
            flag1 = sp.value_load(flags[0:1, 0:1], min_val=0, max_val=1)
            with sp.If(flag1):
                sp.wait_ge(s("adjacency_ready"), 1)
            with sp.Else():
                n = 0
                for t in l0_sums:
                    n += zero_table(sp, t, 2 * D + 1, s("l0_zeroed"))
                sp.wait_ge(s("l0_zeroed"), 16 * n)
                sp.sem_inc(s("l0_go"), 1)
                load_sums(0)
            sp.wait_ge(s("flag2_ready"), 1)
            flag2 = sp.value_load(flags[0:1, 1:2], min_val=0, max_val=1)
            for a in range(6):
                sp.wait_ge(s("u_ready"), a + 1)
                with sp.If(flag2):
                    def half(at_row, slot, used, n=HG):
                        sp.wait_ge(s("half_mm"), used)
                        sp.dma_start(half_words[slot][:, 0:n * GW // 4].rearrange("p (g f) -> p g f", g=n), adjacency[bass.ds(at_row, n * P), :].rearrange("(g p) f -> p g f", p=P)) \
                            .then_inc(s(f"half_in{slot}"), 16)
                    with sp.Fori(0, NH // 2) as i:
                        for q in range(2):
                            half(i * (2 * HG * P) + q * HG * P, q, i * 2 + (q + 1 + NH * a))
                    half((NH - 1) * HG * P, 0, NH * a + NH, n=NG - (NH - 1) * HG)
                with sp.Else():
                    sp.dma_start(node_rows(x_table), U[:]).then_inc(s("x_table_stored"), 16)
                    sp.wait_ge(s("x_table_stored"), 16 * (a + 1))
                    n = 0
                    for t in sums(a + 1):
                        n += zero_table(sp, t, D, s("agg_zeroed"))
                    sp.wait_ge(s("agg_zeroed"), 16 * n * (a + 1))
                    sp.sem_inc(s("table_ready"), 1)
                    load_sums(a + 1)
            sp.wait_ge(s("l3_sums_wanted"), 1)
            load_sums(7)
            sp.wait_ge(s("out_ready"), 1)
            sp.dma_start(out[0:WHOLE * P, :].rearrange("(t p) d -> p t d", p=P), G[:, 0:WHOLE, :]).then_inc(s("out_stored"), 16)
            sp.dma_start(out[WHOLE * P:N, :], G[0:NODE_TAIL, WHOLE, :]).then_inc(s("out_stored"), 16)
            sp.wait_ge(s("out_stored"), 32)

        @block.gpsimd
        def _(pool):
            ch = Chain(pool, s("pool_chain"))
            ch.link(pool.memset(ident[:], 0.0))
            ch.link(pool.memset(before[:], 1.0))
            ch.link(pool.affine_select(out=ident[:], in_=ident[:], compare_op=ALU.not_equal, fill=1.0, base=0,
                                       pattern=[[-1, P]], channel_multiplier=1))
            ch.link(pool.affine_select(out=before[:], in_=before[:], compare_op=ALU.is_gt, fill=0.0, base=0,
                                       pattern=[[-1, P]], channel_multiplier=1))
            ch.link(pool.iota(discard_row[:], pattern=[[0, 1]], base=NP, channel_multiplier=1, allow_small_or_imprecise_dtypes=True))
            exact = dict(allow_small_or_imprecise_dtypes=True)
            ch.link(pool.memset(ones[:], 1.0))
            ch.link(pool.memset(minus_max[:], -COUNT_MAX))
            ch.link(pool.iota(count_key[:], pattern=[[512, SRC_T], [1, GN]], base=0, channel_multiplier=0, **exact))
            ch.link(pool.iota(io128[:], pattern=[[1, P]], base=1, channel_multiplier=0, **exact))
            ch.link(pool.iota(io128f[:], pattern=[[1, P]], base=1, channel_multiplier=0, **exact))
            ch.link(pool.iota(minus_base[:], pattern=[[-GN, NG]], base=0, channel_multiplier=0, **exact))
            ch.link(pool.iota(group_first[:], pattern=[[GN * P, 4]], base=0, channel_multiplier=GN, **exact))
            ch.link(pool.iota(group_past[:], pattern=[[GN * P, 4]], base=GN, channel_multiplier=GN, **exact))
            ch.link(pool.tensor_tensor(twice[:], ident[:, 0:D], ident[:, D:2 * D], ALU.add))
            pool.tensor_copy(ident16[:], ident[:]).then_inc(s("const_ready"), 1)

            def edge_pass(j):
                name, width, key = PASSES[j]
                fam, b = FAMILY[j], BEFORE[j]
                if fam == "agg":
                    pool.wait_ge(s("table_ready"), b + 1)
                with pool.Fori(0, ROUNDS) as i:
                    c1 = [i * K + k + 1 + b * NC for k in range(K)]
                    if name != "l3":
                        src_ap = rel_table if name == "l0" else x_table
                        for k in range(K):
                            pool.wait_ge(s(f"{fam}_gather_idx"), c1[k])
                            pool.wait_ge(s(f"{fam}_comb_done"), c1[k])
                            pool.sem_inc(s("pool_turn"), 1)
                            pool.indirect_dma_start(raw[k][:, 0:width - 1 if name == "l0" else width], None, src_ap,
                                                    bass.IndirectOffsetOnAxis(ap=gather_idx[k][:], axis=0)).then_inc(s(f"{fam}_gathered{k}"), 16)
                    for k in range(K):
                        pool.wait_ge(s(f"{fam}_comb_ready"), c1[k] + 2)
                        pool.sem_inc(s("pool_turn"), 1)
                        pool.indirect_dma_start(sums(j)[k], bass.IndirectOffsetOnAxis(ap=scatter_idx[k][:], axis=0),
                                                comb[k][:, 0:width], None, compute_op=ALU.add,
                                                bounds_check=NROW - 1).then_inc(s(f"{fam}_scattered{k}"), 16)

            pool.wait_ge(s("l3_go"), 1)
            edge_pass(7)
            pool.wait_ge(s("flag1_ready"), 1)
            flag1 = pool.value_load(flags[0:1, 0:1], min_val=0, max_val=1)
            pool.wait_ge(s("rel_ready"), 1)

            def gather_round(r, q, half):
                pool.wait_ge(s("summed"), r + (TG - AHEAD))
                pool.wait_ge(s(f"ring_in{q % 2}"), half * (16 * K))
                pool.tensor_copy(ring_idx[q % 2], rel_f[:, bass.ds(r * K, K)]).then_inc(s("ring_idx"), 1)
                pool.wait_ge(s("ring_idx"), r + 1)
                pool.sem_inc(s("pool_turn"), 1)
                for k in range(K):
                    pool.indirect_dma_start(ring[:, q * K + k, 0:2 * D], None, rel_table,
                                            bass.IndirectOffsetOnAxis(ap=ring_idx[q % 2][:, k:k + 1], axis=0)).then_inc(s(f"ring_in{q % 2}"), 16)

            with pool.If(flag1):
                pool.wait_ge(s("ring_ready"), 1)
                with pool.Fori(0, ROUNDS // TG) as b:
                    for q in range(TG):
                        gather_round(b * TG + q, q, b * (TG // 2) + q // 2)
                for r in range(ROUNDS // TG * TG, ROUNDS):
                    gather_round(r, r % TG, r // 2)
            with pool.Else():
                pool.wait_ge(s("l0_go"), 1)
                edge_pass(0)
            pool.wait_ge(s("flag2_ready"), 1)
            flag2 = pool.value_load(flags[0:1, 1:2], min_val=0, max_val=1)
            with pool.If(flag2):
                pool.sem_inc(s("pool_turn"), 1)
            with pool.Else():
                for a in range(6):
                    edge_pass(a + 1)

        @block.scalar
        def _(act):
            ch = Chain(act, s("act_chain"))
            for fam in ("l0", "agg", "l3"):
                act.sem_inc(s(f"{fam}_comb_ready"), 2)
            act.sem_inc(s("half_out"), 2)
            act.sem_inc(s("counts_read"), 1)
            act.wait_ge(s("memset_done"), 1)

            def rstd(n):
                act.wait_ge(s("var_ready"), n)
                act.activation(var[:], var[:], ACT.Sqrt, bias=eps[:], scale=1.0 / D).then_inc(s("std_ready"), 1)

            def edge_round(j, r, k0, count=None):
                name, width, key = PASSES[j]
                fam, b = FAMILY[j], BEFORE[j]
                idx = rel_f if name == "l0" else src_f
                first = dst_first if key == "dst" else src_first
                dma_free = r * 16 + b * ROUNDS * 16
                for k in range(K if name != "l3" else 0):
                    act.wait_ge(s(f"{fam}_gathered{k}"), dma_free)
                    act.copy(gather_idx[k][:], idx[:, bass.ds(k0 + k, 1)]).then_inc(s(f"{fam}_gather_idx"), 1)
                if name == "l3":
                    act.wait_ge(s("src_first_ready"), r + 1)
                for k in range(K):
                    act.wait_ge(s(f"{fam}_scattered{k}"), dma_free)
                    act.copy(scatter_idx[k][:], first[:, bass.ds(k0 + k, 1)])
                    act.wait_ge(s(f"{fam}_comb_done"), k0 + (k + 1 + b * NC + K))
                    act.copy(comb[k][:, 0:width], bank[2 + k % 2][:, 0:width]).then_inc(s(f"{fam}_comb_ready"), 1)
                    if k == 1 and count is not None:
                        count()

            def edge_pass(j):
                with act.Fori(0, ROUNDS) as i:
                    edge_round(j, i, i * K)

            def store_counts(g, q):
                act.wait_ge(s("summed"), g + (1 + TG))
                act.wait_ge(s("counts_stored"), g * 16)
                act.sem_inc(s("act_turn"), 1)
                w0 = A_SPLIT * GN
                b0, b1 = (bank[n] for n in count_bank[q % 2])
                act.copy(count_stage[:, 0:w0], b0[:, 0:w0], saturate=False)
                act.copy(count_stage[:, w0:GW], b1[:, 0:GW - w0], saturate=False)
                act.wait_ge(s("counts_read"), g + 1)
                act.activation(over_junk[:, 0:w0], b0[:, 0:w0], ACT.Relu, bias=minus_max[:], accum_out=over[:, bass.ds(g * 2, 1)])
                act.activation(over_junk[:, w0:GW], b1[:, 0:GW - w0], ACT.Relu, bias=minus_max[:],
                               accum_out=over[:, bass.ds(g * 2 + 1, 1)]).then_inc(s("counts_read"), 1)
                act.wait_ge(s("counts_read"), g + 2)
                act.dma_start(adjacency[bass.ds(g * P, P), :], count_words).then_inc(s("counts_stored"), 16)

            edge_pass(7)
            for k in range(K):
                act.wait_ge(s(f"l3_scattered{k}"), 16 * ROUNDS)
            rstd(1)
            with act.Fori(0, NB) as b:
                act.wait_ge(s("h_T"), b + 1)
                act.copy(hT[:], bank[0][0:D, :]).then_inc(s("hT_ready"), 1)
                for q in range(BT):
                    act.wait_ge(s("rel_mm"), b * BT + q + 1)
                    act.wait_ge(s(f"rel_stored{q % 2}"), (b * 2 + q // 2) * 16)
                    for half in range(2):
                        ins = act.copy(rel_stage[q % 2][:, half * 8:half * 8 + 8, D:2 * D],
                                       bank[1 + half][:, :].rearrange("p (r o) -> p r o", o=D))
                    ins.then_inc(s("rel_h"), 1)
            act.wait_ge(s("flag1_ready"), 1)
            flag1 = act.value_load(flags[0:1, 0:1], min_val=0, max_val=1)
            with act.If(flag1):
                def tile_out(t):
                    tile = bass.ds(t, 1)
                    act.copy(G[:, tile, :], bank[6][:, 0:D].unsqueeze(1))
                    act.copy(U[:, tile, :], bank[6][:, D:2 * D].unsqueeze(1))
                    act.copy(cnt[:, tile], bank[6][:, 2 * D:2 * D + 1]).then_inc(s("tile_out"), 1)

                with act.Fori(0, NG // TG) as b:
                    for q in range(TG):
                        store_counts(b * TG + q, q)
                    tile_out(b)
                for g in range(NG // TG * TG, NG):
                    store_counts(g, g)
                tile_out(NG // TG)
                act.wait_ge(s("tile_out"), NG // TG + 1)
                act.wait_ge(s("counts_stored"), NG * 16)
                act.sem_inc(s("adjacency_ready"), 1)
            with act.Else():
                act.wait_ge(s("dst_first_ready"), 1)
                edge_pass(0)
            act.wait_ge(s("flag2_ready"), 1)
            flag2 = act.value_load(flags[0:1, 1:2], min_val=0, max_val=1)

            def agg(a):
                with act.If(flag2):
                    def out(m, slot, tiles):
                        act.wait_ge(s("half_fin"), m + 3)
                        act.copy(G[:, tiles, :], bank[2 + slot][:, 0:2 * D].rearrange("p (t d) -> p t d", d=D)).then_inc(s("half_out"), 1)
                    with act.Fori(0, NH // 2) as i:
                        for q in range(2):
                            out(i * 2 + (q + NH * a), q, bass.ds(i * 4 + 2 * q, 2))
                    out(NH * a + NH - 1, 0, slice(2 * (NH - 1), 2 * NH))
                with act.Else():
                    edge_pass(a + 1)

            rstd(2)
            agg(0)
            agg(1)
            rstd(3)
            act.wait_ge(s("deg_ready"), 1)
            act.activation(dinv[:], cnt[:], ACT.Sqrt).then_inc(s("deg_sqrt"), 1)
            agg(2)

            def dense(n, bias):
                with act.Fori(0, NB) as b:
                    if True:
                        act.wait_ge(s("dense_T"), b + n * NB)
                    act.copy(stg[:], G[:, bass.ds(b * BT, BT), :]).then_inc(s("dense_staged"), 1)
                    act.wait_ge(s("dense_mm1"), b + 1 + n * NB)
                    act.activation(xs[:], bank[1][:], ACT.Relu, bias=bias[:]).then_inc(s("dense_relu"), 1)

            act.wait_ge(s("g_ready"), 1)
            dense(0, g_b1)
            agg(3)
            agg(4)
            act.wait_ge(s("g_ready"), 2)
            dense(1, g_b3)
            agg(5)
            rstd(4)
            act.wait_ge(s("u_bias_mm"), 1)
            act.activation(m_c1[:], bank[0][:, 0:1], ACT.Identity, bias=m_b1[:]).then_inc(s("c1_ready"), 1)
            act.wait_ge(s("c1_ready"), 1)
            act.wait_ge(s("ve_ready"), 1)
            with act.Fori(0, NB) as b:
                act.wait_ge(s("mlp_T"), b)
                act.copy(stg[:], h[:, bass.ds(b * BT, BT), :])
                act.copy(stg_e, ld[0][:, bass.ds(b * BT, BT), 0:D48]).then_inc(s("mlp_staged"), 1)
                act.wait_ge(s("mlp_mm1"), b + 1)
                act.activation(xs[:], bank[2][:], ACT.Relu, bias=m_c1[:]).then_inc(s("mlp_h1"), 1)
                act.wait_ge(s("mlp_mm2"), b + 1)
                act.activation(xs2, bank[3][:], ACT.Relu, bias=m_b2[:]).then_inc(s("mlp_h2"), 1)

        @block.vector
        def _(v):
            ch = Chain(v, s("dve_chain"))
            link = lambda ins: chains[-1].link(ins)
            chains = [ch]
            fast = Chain(v, s("dve_fast_chain"))
            slow = Chain(v, s("dve_slow_chain"))
            v.sem_inc(s("he_free"), 2)
            v.sem_inc(s("dup_done"), K)
            for fam in ("l0", "agg", "l3"):
                v.sem_inc(s(f"{fam}_same_ready"), 2)
            v.sem_inc(s("acc_read"), 2)
            v.memset(verdict[:], 0)
            for t in (zeros[:], x[:], z, dup["src"], dup["dst"], he[0], he[1], idx_stage):
                v.memset(t, 0)
            for k in range(K):
                v.memset(raw[k][:], 1.0)
                v.memset(raw3[k][:], 1.0)
            link(v.memset(eps[:], EPS))
            v.memset(idx_stage[:, ET - 1, :], PAD_NODE).then_inc(s("memset_done"), 1)

            groups = [(g, min(4, ET - g * 4)) for g in range(-(-ET // 4))]
            done = 0
            for n, (tab, pad) in enumerate(((src_f, None), (dst_f, None), (rel_f, None))):
                v.wait_ge(s("idx_loaded"), 48 * (n + 1))
                if n:
                    v.wait_ge(s("idx_T"), len(groups) * n)
                v.tensor_copy(idx_f, idx_stage).then_inc(s("idx_cast"), 1)
                if n == 1:
                    v.wait_ge(s("idx_cast"), 2)
                    smaller = ld_all[:, 0:ET * (P - 1)].rearrange("p (t c) -> p t c", t=ET)
                    link(v.tensor_tensor(smaller, idx_f[:, :, 1:P], idx_f[:, :, 0:P - 1], ALU.is_lt))
                    link(v.tensor_reduce(verdict[:, 0:1], smaller, axis=AX.XY, op=ALU.add))
                for g, w in groups:
                    v.wait_ge(s("idx_T"), len(groups) * n + g + 1)
                    link(v.tensor_copy(tab[:, g * 512:g * 512 + w * P], bank[g][:, 0:w * P]))
            link(v.tensor_scalar(rel_f, rel_f, float(R - 1), None, ALU.min))
            link(v.scalar_tensor_tensor(rel_f, src_f[:], float(R), rel_f, ALU.mult, ALU.add))
            for name, tab in (("src", src_f), ("dst", dst_f)):
                hi, lo = key16[name]
                tmp = idx_stage.rearrange("p t c -> p (t c)")
                tmpf = idx_f.rearrange("p t c -> p (t c)")
                link(v.tensor_copy(tmp, tab[:]))
                link(v.tensor_scalar(tmp, tmp, P - 1, None, ALU.bitwise_and))
                link(v.tensor_copy(tmpf, tmp))
                link(v.tensor_copy(lo[:], tmpf))
                link(v.tensor_tensor(hi[:], tab[:], tmpf, ALU.subtract))
            v.tensor_copy(scratch[0][:, 0:1], dst_f[:, 0:1]).then_inc(s("keys_ready"), 1)

            rows = [ld_all[:, NT * D + m * NCT:NT * D + (m + 1) * NCT] for m in range(2)]
            compared = ld_all[:, 0:NC]
            for m in range(2):
                v.wait_ge(s("edge_row"), m + 1)
                for g, w in groups:
                    ins = v.tensor_copy(rows[m][:, g * 512:g * 512 + w * P], bank[g][:, 0:w * P])
                link(ins)
                v.sem_inc(s("edge_row_read"), 1)
            link(v.tensor_tensor(compared[:, 0:NC - 1], rows[1][:, 1:NC], rows[0][:, 0:NC - 1], ALU.is_lt))
            link(v.tensor_reduce(verdict[:, 1:2], compared[:, 0:NC - 1], axis=AX.X, op=ALU.add))
            link(v.tensor_scalar(is_group[:], group_first[:], float(N) - 0.5, None, ALU.is_lt))
            for nodes, chunks in ((group_first, first_chunk), (group_past, last_chunk)):
                for t in range(4):
                    link(v.tensor_scalar(compared, rows[0][:, 0:NC], nodes[:, t:t + 1], 0.0, ALU.is_lt, ALU.add,
                                         accum_out=chunks[:, t:t + 1]))
            link(v.tensor_copy(first_chunk_i[:], first_chunk[:]))
            v.sem_inc(s("chunks_ready"), 1)
            link(v.tensor_tensor(last_chunk[:], last_chunk[:], first_chunk[:], ALU.subtract))
            link(v.tensor_scalar(last_chunk[:], last_chunk[:], CG - 0.5, None, ALU.is_gt))
            link(v.tensor_reduce(verdict[:, 2:3], last_chunk[:], axis=AX.X, op=ALU.add))
            link(v.scalar_tensor_tensor(last_chunk[:], group_first[:], -float(K) / GN, first_chunk[:], ALU.mult, ALU.add))
            link(v.tensor_scalar(first_chunk[:], last_chunk[:], K * (LAG + 1) - CG + 0.5, None, ALU.is_gt))
            link(v.tensor_scalar(last_chunk[:], last_chunk[:], K * AHEAD - RING + K - 0.5, None, ALU.is_lt))
            link(v.tensor_tensor(last_chunk[:], last_chunk[:], first_chunk[:], ALU.add))
            link(v.tensor_tensor(last_chunk[:], last_chunk[:], is_group[:], ALU.mult))
            link(v.tensor_reduce(verdict[:, 3:4], last_chunk[:], axis=AX.X, op=ALU.add))
            link(v.tensor_tensor(verdict[:, 2:3], verdict[:, 2:3], verdict[:, 3:4], ALU.add))
            link(v.tensor_reduce(verdict[:, 3:4], verdict[:, 0:3], axis=AX.X, op=ALU.add))
            v.sem_inc(s("verdict_ready"), 1)
            v.wait_ge(s("verdict_mm"), 1)
            link(v.tensor_scalar(flags[:, 0:1], bank[7][0:1, 0:1], 0.5, None, ALU.is_lt))
            v.sem_inc(s("flag1_ready"), 1)

            v.wait_ge(s("ve_mm"), 1)
            link(v.tensor_copy(ve_row[:], bank[5][:, 0:D]))
            v.tensor_copy(v_cols[:], bank[4][0:D, 0:3]).then_inc(s("v_cols_ready"), 1)

            def z_piece(n, q, cols, dst_ap):
                v.wait_ge(s("he_free"), n + 1)
                link(v.tensor_tensor(prod[q][:, 0:cols, :], he[q][:, 0:cols, :],
                                     ve_row[:].unsqueeze(1).to_broadcast([P, cols, D]), ALU.mult))
                v.reduce_sum(dst_ap, prod[q][:, 0:cols, :], axis=AX.X).then_inc(s("he_free"), 1)

            def rest_of_z():
                v.wait_ge(s("he_loaded0"), HE_ROUNDS * 16 + 16)
                z_piece(HE_ROUNDS * 2, 0, 8, z[:, HE_ROUNDS * 16:HE_ROUNDS * 16 + 8])
                v.wait_ge(s("he_loaded1"), HE_ROUNDS * 16 + 32)
                z_piece(HE_ROUNDS * 2 + 1, 1, HE_REST - 7, z[:, HE_ROUNDS * 16 + 8:FULL + 1])

            stat = lambda t: t[:].unsqueeze(2).to_broadcast([P, NT, D])

            def layernorm(n):
                link(v.reduce_sum(mean[:], x[:], axis=AX.X))
                link(v.tensor_scalar(mean[:], mean[:], 1.0 / D, None, ALU.mult))
                link(v.tensor_tensor(h[:], x[:], stat(mean), ALU.subtract))
                link(v.tensor_tensor(G[:], h[:], h[:], ALU.mult))
                v.reduce_sum(var[:], G[:], axis=AX.X).then_inc(s("var_ready"), 1)
                v.wait_ge(s("std_ready"), n)
                link(v.reciprocal(var[:], var[:]))
                link(v.tensor_tensor(h[:], h[:], stat(var), ALU.mult))
                ins = v.tensor_scalar(h[:], h[:], 0.0, None, ALU.max)
                return ins

            def edge_round(j, i, count=None):
                name, width, key = PASSES[j]
                fam, b = FAMILY[j], BEFORE[j]
                tab = {"src": src_f, "dst": dst_f}[key]
                c1 = [i * K + k + 1 + b * NC for k in range(K)]

                def same_rows(k):
                    v.wait_ge(s(f"{fam}_key_row"), c1[k])
                    v.wait_ge(s(f"{fam}_comb_done"), c1[k])
                    key = tab[:, bass.ds(i * K + k, 1)]
                    ins = v.tensor_scalar(same[k][:], bank[k % 2][:, 0:P], key, None, ALU.is_equal)
                    if name == "l3":
                        v.wait_ge(s("l3_same_ready"), c1[k])
                        ins = v.scalar_tensor_tensor(scratch[k % 2][:], bank[k % 2][:, 0:P], key, before[:],
                                                     ALU.is_equal, ALU.mult, accum_out=dup4[:, k:k + 1])
                    ins.then_inc(s(f"{fam}_same_ready"), 1)

                def message(k):
                    if name == "l0":
                        v.wait_ge(s(f"l0_gathered{k}"), i * 16 + 16)
                        v.scalar_tensor_tensor(raw[k][:, 0:D], raw[k][:, D:2 * D], z[:, bass.ds(i * K + k, 1)],
                                               raw[k][:, 0:D], ALU.mult, ALU.add).then_inc(s("message_ready"), 1)
                for op, k in ((same_rows, 0), (same_rows, 1), (message, 0), (same_rows, 2), (message, 1),
                              (same_rows, 3), (message, 2), (message, 3)):
                    op(k)
                if name == "l3":
                    four = bass.ds(i * K, K)
                    link(v.tensor_scalar(apart4[:], src_f[:, four], discard_row[:], None, ALU.subtract))
                    v.wait_ge(s("l3_same_ready"), c1[K - 1] + 2)
                    link(v.scalar_tensor_tensor(apart4[:], dup4[:], 1.0, apart4[:], ALU.min, ALU.mult))
                    v.tensor_tensor(src_first[:, four], src_f[:, four], apart4[:], ALU.subtract).then_inc(s("src_first_ready"), 1)

            def sum_tables(j):
                name, fam, b = PASSES[j][0], FAMILY[j], BEFORE[j]
                for k in range(K):
                    v.wait_ge(s(f"{fam}_loaded{k % 2}"), 16 * loads(j, k))
                    if name == "l0":
                        ops = [(G[:], ld[0]), (U[:], ld[1]), (cnt[:], ldc[:])]
                    elif name == "l3":
                        ops = [(G[:, :, 0:D48], ld[k % 2][:, :, 0:D48]), (cnt[:], ldc[:])]
                    else:
                        ops = [(G[:], ld[k % 2])]
                    for acc, part in ops:
                        link(v.tensor_copy(acc, part) if k == 0 else v.tensor_tensor(acc, acc, part, ALU.add))
                    v.sem_inc(s(f"{fam}_read"), 1)

            def edge_pass(j):
                with v.Fori(0, ROUNDS) as i:
                    edge_round(j, i)
                sum_tables(j)

            def one_hots(g, q):
                first = v.value_load(starts[0:1, bass.ds(g, 1)], min_val=0, max_val=NC)
                v.wait_ge(s("summed"), g + (TG - 1))
                six = bass.ds(first, CG)
                base = minus_base[:, bass.ds(g, 1)]
                v.scalar_tensor_tensor(dst_in[q % 2], minus_group[:, six], base, key16["dst"][1][:, six], ALU.is_equal, ALU.mult)
                link(v.scalar_tensor_tensor(lo_in[q % 2], minus_group[:, six], base, key16["src"][1][:, six], ALU.is_equal, ALU.mult))
                v.tensor_tensor(dst_hot[q % 2], io128f[:].unsqueeze(1).to_broadcast([P, CG, P]),
                                dst_in[q % 2].unsqueeze(2).to_broadcast([P, CG, P]), ALU.is_equal)
                v.tensor_tensor(lo_hot[q % 2], io128[:].unsqueeze(1).to_broadcast([P, CG, P]),
                                lo_in[q % 2].unsqueeze(2).to_broadcast([P, CG, P]), ALU.is_equal)
                for k in range(CG):
                    ins = v.tensor_scalar(pair_hot[q % 2][:, k, :], count_key[:].rearrange("p a b -> p (a b)"), pair_key[:, bass.ds(first + k, 1)],
                                          base, ALU.subtract, ALU.is_equal)
                ins.then_inc(s("hot_ready"), 1)

            def power_of_two(t):
                link(v.tensor_scalar(t, t, 1e-30, None, ALU.max))
                link(v.tensor_scalar(t.bitcast(i32), t.bitcast(i32), 0x7F800000, None, ALU.bitwise_and))

            def split_rows(a):
                link(v.tensor_reduce(top2[:, 0, :], U[:, 0:SRC_T, :].rearrange("p t d -> p d t"), axis=AX.X, op=ALU.max,
                                     apply_absolute_value=True))
                link(v.tensor_copy(top2[:, 1, :], top2[:, 0, :]))
                v.sem_inc(s("top_ready"), 1)
                v.wait_ge(s("top_T"), a + 1)
                link(v.tensor_reduce(feature_top[:], bank[7][:, 0:P], axis=AX.X, op=ALU.max))
                power_of_two(feature_top[:])
                link(v.tensor_scalar(feature_top[:], feature_top[:], 2.0 ** -14, None, ALU.mult))
                link(v.tensor_scalar(unscale[:], twice[:], feature_top[:], None, ALU.mult))
                link(v.reciprocal(feature_inv[:], feature_top[:]))
                link(v.tensor_scalar(diag[:], ident[:], feature_inv[:], None, ALU.mult))
                v.sem_inc(s("diag_ready"), 1)
                v.wait_ge(s("scale_row_mm"), a + 1)
                link(v.tensor_copy(scale_row[:], bank[7][:, 0:D]))
                scaled = G[:, 0:SRC_T, :]
                link(v.tensor_tensor(scaled, U[:, 0:SRC_T, :], scale_row[:].unsqueeze(1).to_broadcast([P, SRC_T, D]), ALU.mult))
                link(v.tensor_copy(x16[:, :, 0:D], scaled))
                link(v.tensor_tensor(x16[:, :, D:2 * D], scaled, x16[:, :, 0:D], ALU.subtract))
                link(v.memset(G[:, 2 * NH:NT, :], 0))
                v.sem_inc(s("x16_ready"), 1)

            def agg(a):
                with v.If(flag2):
                    chains.append(fast)
                    split_rows(a)

                    def acc_copy(m, slot):
                        v.wait_ge(s("half_mm"), m + 3)
                        v.wait_ge(s("half_fin"), m + 1)
                        return v.tensor_copy(accT[slot][:], bank[slot][:, 0:HG * GN])
                    with v.Fori(0, NH // 2) as i:
                        for q in range(2):
                            acc_copy(i * 2 + (q + NH * a), q).then_inc(s("acc_read"), 1)
                    m, n = NH * a + NH - 1, (NG - (NH - 1) * HG) * GN
                    v.wait_ge(s("half_mm"), m + 3)
                    v.wait_ge(s("half_fin"), m + 1)
                    v.memset(accT[0][:, n:HG * GN], 0)
                    v.tensor_copy(accT[0][:, 0:n], bank[0][:, 0:n]).then_inc(s("acc_read"), 1)
                    v.wait_ge(s("half_out"), NH * (a + 1) + 2)
                    chains.pop()
                with v.Else():
                    chains.append(slow)
                    edge_pass(a + 1)
                    chains.pop()

            with ch.over(HE_ROUNDS, 2 + 8) as i:
                for q in range(4):
                    edge_round(7, i * 4 + q)
                    if q % 2:
                        v.wait_ge(s(f"he_loaded{q // 2}"), i * 16 + 16)
                        z_piece(i * 2 + q // 2, q // 2, 8, z[:, bass.ds((i * 2 + q // 2) * 8, 8)])
            rest_of_z()
            for r in range(HE_ROUNDS * 4, ROUNDS):
                edge_round(7, r)
            v.wait_ge(s("src_first_ready"), ROUNDS)

            v.wait_ge(s("x_loaded"), 32)
            layernorm(1).then_inc(s("h_ready"), 1)
            v.wait_ge(s("small_loaded"), 16 * len(small))
            v.wait_ge(s("v_cols_ready"), 1)
            link(v.tensor_copy(v_sd[:, 0:1], v_cols[:, 0:1]))
            v.tensor_copy(v_sd[:, 1:2], v_cols[:, 2:3]).then_inc(s("v_sd_ready"), 1)
            v.wait_ge(s("h_ready"), 1)
            with ch.over(NB, 2 * BT) as b:
                v.wait_ge(s("h_T"), b)
                v.tensor_copy(stgh[:], h[:, bass.ds(b * BT, BT), :]).then_inc(s("h_staged"), 1)
                for q in range(BT):
                    v.wait_ge(s("rel_mm"), b * BT + q + 1)
                    v.wait_ge(s("rel_h"), b * BT + q + 1)
                    link(v.tensor_copy(s12[:, bass.ds(b * BT + q, 1), :], bank[3][:, 0:2].unsqueeze(1)))
                    link(v.tensor_tensor(rel_stage[q % 2][:, :, 0:D], rel_stage[q % 2][:, :, D:2 * D],
                                         s12[:, bass.ds(b * BT + q, 1), 0:1].to_broadcast([P, R, D]), ALU.mult))
                    v.sem_inc(s("rel_staged"), 1)

            v.wait_ge(s("starts_in"), 16)
            flag1 = v.value_load(flags[0:1, 0:1], min_val=0, max_val=1)
            with v.If(flag1):
                chains.append(fast)
                src_hi, src_lo = key16["src"]
                link(v.scalar_tensor_tensor(pair_key, src_hi[:], 512.0 / P, dst_f[:], ALU.mult, ALU.add))
                for lo in (src_lo, key16["dst"][1]):
                    link(v.tensor_scalar(lo[:], lo[:], 1.0, None, ALU.add))
                v.wait_ge(s("rel_ready"), 1)
                for t, value in ((ring, 1.0), (G[:, SRC_T:NT, :], 0.0), (U[:, SRC_T:NT, :], 0.0), (cnt[:, SRC_T:NT], 0.0)):
                    link(v.memset(t, value))
                v.sem_inc(s("ring_ready"), 1)
                node_i = flat3(G)[:, 0:NCT].bitcast(i32)
                link(v.tensor_copy(node_i, dst_f[:]))
                link(v.tensor_scalar(node_i, node_i, -GN, None, ALU.bitwise_and))
                link(v.tensor_copy(minus_group, node_i))
                link(v.tensor_scalar(minus_group, minus_group, -1.0, None, ALU.mult))
                def message_round(r, q, half):
                    v.wait_ge(s(f"ring_in{q % 2}"), half * (16 * K) + 16 * K)
                    for k in range(K):
                        row = ring[:, q * K + k, :]
                        v.scalar_tensor_tensor(row[:, 0:D], row[:, D:2 * D], z[:, bass.ds(r * K + k, 1)], row[:, 0:D], ALU.mult, ALU.add)

                for r in range(LAG):
                    message_round(r, r, r // 2)
                with fast.over(NG // TG, TG) as b:
                    for q in range(TG):
                        message_round(b * TG + (q + LAG), (q + LAG) % TG, b * (TG // 2) + (q + LAG) // 2)
                        one_hots(b * TG + q, q)
                for g in range(NG // TG * TG, NG):
                    if g + LAG < ROUNDS:
                        message_round(g + LAG, (g + LAG) % TG, (g + LAG) // 2)
                    one_hots(g, g)
                v.wait_ge(s("adjacency_ready"), 1)
                link(v.tensor_reduce(over_sum[:], over, axis=AX.X, op=ALU.add))
                for lo in (src_lo, key16["dst"][1]):
                    link(v.tensor_scalar(lo[:], lo[:], 1.0, None, ALU.subtract))
                v.sem_inc(s("over_ready"), 1)
                v.wait_ge(s("over_mm"), 1)
                link(v.tensor_scalar(flags[:, 1:2], bank[7][0:1, 0:1], 0.5, None, ALU.is_lt))
                chains.pop()
            with v.Else():
                chains.append(slow)
                dup_dst = dup["dst"]
                link(v.memset(dup_dst, 0))
                with v.Fori(0, ROUNDS) as i:
                    for k in range(K):
                        v.wait_ge(s("dup_row"), i * K + k + 1)
                        col = bass.ds(i * K + k, 1)
                        v.wait_ge(s("dup_done"), i * K + k + 3)
                        v.scalar_tensor_tensor(scratch[k % 2][:], bank[k][:, 0:P], dst_f[:, col], before[:],
                                               ALU.is_equal, ALU.mult, accum_out=dup_dst[:, col]).then_inc(s("dup_done"), 1)
                v.wait_ge(s("dup_done"), K + NC)
                tmpf = idx_f.rearrange("p t c -> p (t c)")
                link(v.tensor_scalar(tmpf, dst_f[:], discard_row[:], None, ALU.subtract))
                link(v.tensor_scalar(dup_dst, dup_dst, 1.0, None, ALU.min))
                link(v.tensor_tensor(tmpf, tmpf, dup_dst, ALU.mult))
                link(v.tensor_tensor(dst_first[:], dst_f[:], tmpf, ALU.subtract))
                v.sem_inc(s("dst_first_ready"), 1)
                with v.Fori(0, ROUNDS) as i:
                    edge_round(0, i)
                sum_tables(0)
                link(v.memset(flags[:, 1:2], 0))
                chains.pop()
            v.sem_inc(s("flag2_ready"), 1)
            flag2 = v.value_load(flags[0:1, 1:2], min_val=0, max_val=1)
            link(v.tensor_tensor(U[:], U[:], s12[:, :, 1:2].to_broadcast([P, NT, D]), ALU.mult))
            link(v.tensor_tensor(G[:], G[:], U[:], ALU.add))
            link(v.tensor_scalar(G[:], G[:], 0.0, None, ALU.max))
            link(v.tensor_tensor(x[:], x[:], G[:], ALU.add))
            link(v.tensor_scalar(cnt[:], cnt[:], 1.0, None, ALU.add))
            link(layernorm(2))
            v.tensor_copy(U[:], h[:]).then_inc(s("u_ready"), 1)
            v.wait_ge(s("u_ready"), 1)
            agg(0)
            v.tensor_scalar(U[:], G[:], 0.0, None, ALU.max).then_inc(s("u_ready"), 1)
            v.wait_ge(s("u_ready"), 2)
            agg(1)
            link(v.tensor_tensor(x[:], x[:], G[:], ALU.add))
            link(layernorm(3))
            v.sem_inc(s("deg_ready"), 1)
            v.wait_ge(s("deg_sqrt"), 1)
            link(v.reciprocal(dinv[:], dinv[:]))
            v.tensor_tensor(U[:], h[:], stat(dinv), ALU.mult).then_inc(s("u_ready"), 1)

            def gcn_sum(j):
                v.wait_ge(s("u_ready"), j)
                agg(j - 1)
                link(v.tensor_tensor(G[:], G[:], U[:], ALU.add))
                return v.tensor_tensor(G[:], G[:], stat(dinv), ALU.mult)

            def dense(n):
                with ch.over(NB, 1 - n) as b:
                    v.wait_ge(s("dense_T"), b + 1 + n * NB)
                    v.tensor_copy(vT[:], bank[0][0:D, :]).then_inc(s("dense_vT"), 1)
                    v.wait_ge(s("dense_relu"), b + 1 + n * NB)
                    blk = bass.ds(b * 512, 512)
                    if n == 0:
                        link(v.tensor_copy(hid_T[:, blk], xs[:]))
                        v.sem_inc(s("dense_x"), 1)
                    else:
                        v.tensor_tensor(xs[:], xs[:], hid_T[:, blk], ALU.add).then_inc(s("dense_x"), 1)
                    v.wait_ge(s("dense_mm2"), b + 1 + n * NB)
                    v.tensor_tensor(U[:, bass.ds(b * BT, BT), :], bank[2][:, 0:BT * D].rearrange("p (t d) -> p t d", d=D),
                                    dinv[:, bass.ds(b * BT, BT)].unsqueeze(2).to_broadcast([P, BT, D]),
                                    ALU.mult).then_inc(s("dense_u"), 1)
                v.wait_ge(s("dense_u"), (n + 1) * NB)
                v.sem_inc(s("u_ready"), 1)

            gcn_sum(3).then_inc(s("g_ready"), 1)
            dense(0)
            link(gcn_sum(4))
            link(v.tensor_tensor(G[:], G[:], g_b2[:].unsqueeze(1).to_broadcast([P, NT, D]), ALU.add))
            link(v.tensor_scalar(G[:], G[:], 0.0, None, ALU.max))
            v.tensor_tensor(U[:], G[:], stat(dinv), ALU.mult).then_inc(s("u_ready"), 1)
            gcn_sum(5).then_inc(s("g_ready"), 1)
            dense(1)
            link(gcn_sum(6))
            link(v.tensor_tensor(G[:], G[:], g_b4[:].unsqueeze(1).to_broadcast([P, NT, D]), ALU.add))
            link(v.tensor_scalar(G[:], G[:], 0.0, None, ALU.max))
            link(v.tensor_tensor(G[:], G[:], h[:], ALU.add))
            link(v.tensor_tensor(x[:], x[:], G[:], ALU.add))
            v.sem_inc(s("l3_sums_wanted"), 1)
            link(layernorm(4))
            sum_tables(7)
            link(v.tensor_scalar(cnt[:], cnt[:], 1.0, None, ALU.max))
            link(v.reciprocal(cnt[:], cnt[:]))
            v.tensor_tensor(ld[0][:, :, 0:D48], G[:, :, 0:D48], cnt[:].unsqueeze(2).to_broadcast([P, NT, D48]),
                            ALU.mult).then_inc(s("ve_ready"), 1)
            v.wait_ge(s("ve_ready"), 1)
            with ch.over(NB, 1) as b:
                v.wait_ge(s("mlp_T"), b + 1)
                link(v.tensor_copy(vT[:], bank[0][0:D, :]))
                v.tensor_copy(veT, bank[1][0:D48, :]).then_inc(s("mlp_vT"), 1)
                v.wait_ge(s("mlp_mm3"), b + 1)
                blk = bass.ds(b * BT, BT)
                v.tensor_tensor(G[:, blk, :], bank[4][:, 0:BT * D].rearrange("p (t d) -> p t d", d=D), x[:, blk, :],
                                ALU.add).then_inc(s("mlp_y"), 1)
            v.wait_ge(s("mlp_y"), NB)
            v.tensor_tensor(G[:], G[:], m_b3[:].unsqueeze(1).to_broadcast([P, NT, D]), ALU.add).then_inc(s("out_ready"), 1)

        @block.tensor
        def _(pe):
            for fam in ("l0", "agg", "l3"):
                pe.sem_inc(s(f"{fam}_comb_done"), K)
            pe.sem_inc(s("half_mm"), 2)
            pe.sem_inc(s("summed"), TG)
            pe.sem_inc(s("half_fin"), 2)
            pe.wait_ge(s("const_ready"), 1)
            pe.wait_ge(s("small_loaded"), 16 * len(small))
            pe.matmul(bank[4][0:D, 0:3], w_shared[:], w_attn[:], start=True, stop=True)
            pe.matmul(bank[5][:, 0:D], w_attn[:, 1:2].to_broadcast([D, P]), w_shared[:], start=True, stop=True).then_inc(s("ve_mm"), 1)
            groups = [(g, min(4, ET - g * 4)) for g in range(-(-ET // 4))]
            for n in range(3):
                pe.wait_ge(s("idx_cast"), n + 1)
                for g, w in groups:
                    for t in range(w):
                        ins = pe.transpose(bank[g][:, t * P:t * P + P], idx_f[:, g * 4 + t, :], ident[:])
                    ins.then_inc(s("idx_T"), 1)
            pe.wait_ge(s("keys_ready"), 1)
            for m, row in enumerate((P - 1, 0)):
                if m:
                    pe.wait_ge(s("edge_row_read"), m)
                for g, w in groups:
                    ins = pe.matmul(bank[g][:, 0:w * P], ident[:, row:row + 1].to_broadcast([P, P]), dst_f[:, g * 512:g * 512 + w * P],
                                    start=True, stop=True)
                ins.then_inc(s("edge_row"), 1)
            pe.wait_ge(s("verdict_ready"), 1)
            pe.matmul(bank[7][:, 0:1], ones[:], verdict[:, 3:4], start=True, stop=True).then_inc(s("verdict_mm"), 1)
            pe.wait_ge(s("v_cols_ready"), 1)

            def key_row(dst_bank, name, col):
                hi, lo = key16[name]
                pe.matmul(dst_bank[:, 0:P], hi[:, col].to_broadcast([P, P]), ident16[:], start=True, stop=False)
                return pe.matmul(dst_bank[:, 0:P], lo[:, col].to_broadcast([P, P]), ident16[:], start=False, stop=True)

            def edge_round(j, i):
                name, width, key = PASSES[j]
                fam, b = FAMILY[j], BEFORE[j]
                src_buf = raw3 if name == "l3" else raw
                c1 = [i * K + k + 1 + b * NC for k in range(K)]

                def row(k):
                    pe.wait_ge(s(f"{fam}_same_ready"), c1[k])
                    key_row(bank[k % 2], key, bass.ds(i * K + k, 1)).then_inc(s(f"{fam}_key_row"), 1)

                def combine(k):
                    pe.wait_ge(s(f"{fam}_same_ready"), c1[k] + 2)
                    if name == "l0":
                        pe.wait_ge(s("message_ready"), c1[k])
                    elif name == "l3":
                        pe.wait_ge(s(f"edges_loaded{k}"), i * 16 + 16)
                    else:
                        pe.wait_ge(s(f"agg_gathered{k}"), i * 16 + 16 * (1 + b * ROUNDS))
                    pe.wait_ge(s(f"{fam}_comb_ready"), c1[k])
                    pe.matmul(bank[2 + k % 2][:, 0:width], same[k][:], src_buf[k][:, 0:width],
                              start=True, stop=True).then_inc(s(f"{fam}_comb_done"), 1)
                for op, k in ((row, 0), (row, 1), (combine, 0), (row, 2), (combine, 1), (row, 3), (combine, 2), (combine, 3)):
                    op(k)

            def edge_pass(j):
                with pe.Fori(0, ROUNDS) as i:
                    edge_round(j, i)

            edge_pass(7)
            pe.wait_ge(s("l3_comb_ready"), NC + 2)

            pe.wait_ge(s("v_sd_ready"), 1)
            with pe.Fori(0, NB) as b:
                pe.wait_ge(s("h_staged"), b + 1)
                pe.wait_ge(s("hT_ready"), b)
                pe.sem_inc(s("pe_turn"), 1)
                for q in range(BT):
                    ins = pe.transpose(bank[0][0:D, q * P:q * P + P], stgh[:, q, :], ident[:])
                ins.then_inc(s("h_T"), 1)
                pe.wait_ge(s("hT_ready"), b + 1)
                for q in range(BT):
                    pe.wait_ge(s("rel_staged"), b * BT + q)
                    tile = hT[:, q * P:q * P + P]
                    pe.matmul(bank[1][:], tile, w_rel[:, 0:8, :].rearrange("i r o -> i (r o)"), start=True, stop=True)
                    pe.matmul(bank[2][:], tile, w_rel[:, 8:16, :].rearrange("i r o -> i (r o)"), start=True, stop=True)
                    pe.matmul(bank[3][:, 0:2], tile, v_sd[:], start=True, stop=True).then_inc(s("rel_mm"), 1)
            pe.wait_ge(s("rel_staged"), NT)

            def sum_group(g, q, last):
                first = pe.value_load(starts[0:1, bass.ds(g, 1)], min_val=0, max_val=NC)
                pe.wait_ge(s("hot_ready"), g + 1)
                pe.wait_ge(s("counts_read"), g)
                b0, b1 = (bank[n] for n in count_bank[q % 2])
                w0 = A_SPLIT * GN
                for k in range(CG):
                    pe.matmul(b0[:, 0:w0], lo_hot[q % 2][:, k, :], pair_hot[q % 2][:, k, 0:w0], start=k == 0, stop=k == CG - 1)
                    pe.matmul(b1[:, 0:GW - w0], lo_hot[q % 2][:, k, :], pair_hot[q % 2][:, k, w0:GW], start=k == 0, stop=k == CG - 1)
                for k in range(CG):
                    ins = pe.matmul(bank[6][:, 0:RW], dst_hot[q % 2][:, k, :], ring[:, bass.ds((first + k) & (RING - 1), 1), :].rearrange("p a w -> p (a w)"),
                                    start=q == 0 and k == 0, stop=last and k == CG - 1)
                ins.then_inc(s("summed"), 1)

            pe.wait_ge(s("flag1_ready"), 1)
            flag1 = pe.value_load(flags[0:1, 0:1], min_val=0, max_val=1)
            with pe.If(flag1):
                pe.wait_ge(s("starts_in"), 16)
                with pe.Fori(0, NG // TG) as b:
                    pe.wait_ge(s("tile_out"), b)
                    for q in range(TG):
                        sum_group(b * TG + q, q, q == TG - 1)
                pe.wait_ge(s("tile_out"), NG // TG)
                for g in range(NG // TG * TG, NG):
                    sum_group(g, g % TG, g == NG - 1)
                pe.wait_ge(s("over_ready"), 1)
                pe.matmul(bank[7][:, 0:1], ones[:], over_sum[:], start=True, stop=True).then_inc(s("over_mm"), 1)
            with pe.Else():
                with pe.Fori(0, ROUNDS) as i:
                    for k in range(K):
                        pe.wait_ge(s("dup_done"), i * K + k + 1)
                        key_row(bank[k], "dst", bass.ds(i * K + k, 1)).then_inc(s("dup_row"), 1)
                pe.wait_ge(s("dst_first_ready"), 1)
                edge_pass(0)
            pe.wait_ge(s("flag2_ready"), 1)
            flag2 = pe.value_load(flags[0:1, 1:2], min_val=0, max_val=1)

            def agg(a):
                with pe.If(flag2):
                    pe.wait_ge(s("top_ready"), a + 1)
                    pe.transpose(bank[7][:, 0:P], top2[:].rearrange("p m d -> p (m d)"), ident[:]).then_inc(s("top_T"), 1)
                    pe.wait_ge(s("diag_ready"), a + 1)
                    pe.matmul(bank[7][:, 0:D], ones[0:D, :], diag[0:D, 0:D], start=True, stop=True).then_inc(s("scale_row_mm"), 1)
                    pe.wait_ge(s("x16_ready"), a + 1)

                    def multiply(m, slot, loads, n=HG):
                        pe.wait_ge(s(f"half_in{slot}"), loads)
                        pe.wait_ge(s("acc_read"), m + 1)
                        pe.sem_inc(s("pe_turn"), 1)
                        for t in range(SRC_T):
                            ins = pe.matmul(bank[slot][:, 0:n * GN].rearrange("p (g d) -> p g d", d=GN), x16[:, t, :],
                                            a_half[slot][:, 0:n, t * GN:(t + 1) * GN], start=t == 0, stop=t == SRC_T - 1)
                        ins.then_inc(s("half_mm"), 1)

                    def finalize(m, slot):
                        pe.wait_ge(s("acc_read"), m + 3)
                        pe.wait_ge(s("half_out"), m + 1)
                        for q in range(2):
                            ins = pe.matmul(bank[2 + slot][:, q * D:(q + 1) * D], accT[slot][:, q * P:(q + 1) * P], unscale[:],
                                            start=True, stop=True)
                        ins.then_inc(s("half_fin"), 1)

                    m0, in0, in1 = NH * a, (NH // 2 + 1) * a, NH // 2 * a
                    multiply(m0, 0, 16 * (in0 + 1))
                    with pe.Fori(0, NH // 2 - 1) as i:
                        multiply(i * 2 + (m0 + 1), 1, i * 16 + 16 * (in1 + 1))
                        finalize(i * 2 + m0, 0)
                        multiply(i * 2 + (m0 + 2), 0, i * 16 + 16 * (in0 + 2))
                        finalize(i * 2 + (m0 + 1), 1)
                    multiply(m0 + NH - 2, 1, 16 * (in1 + NH // 2))
                    finalize(m0 + NH - 3, 0)
                    multiply(m0 + NH - 1, 0, 16 * (in0 + NH // 2 + 1), NG - (NH - 1) * HG)
                    finalize(m0 + NH - 2, 1)
                    finalize(m0 + NH - 1, 0)
                with pe.Else():
                    edge_pass(a + 1)

            for a in range(3):
                agg(a)

            def dense(n, wa, wb):
                with pe.Fori(0, NB) as b:
                    at = b + 1 + n * NB
                    pe.wait_ge(s("dense_staged"), at)
                    pe.wait_ge(s("dense_vT"), b + n * NB)
                    pe.sem_inc(s("pe_turn"), 1)
                    for q in range(BT):
                        ins = pe.transpose(bank[0][0:D, q * P:q * P + P], stg[:, q, :], ident[:])
                    ins.then_inc(s("dense_T"), 1)
                    pe.wait_ge(s("dense_vT"), at)
                    pe.matmul(bank[1][:], wa[:], vT[:], start=True, stop=True).then_inc(s("dense_mm1"), 1)
                    pe.wait_ge(s("dense_x"), at)
                    pe.wait_ge(s("dense_u"), b + n * NB)
                    for q in range(BT):
                        ins = pe.matmul(bank[2][:, q * D:q * D + D], xs[:, q * P:q * P + P], wb[:], start=True, stop=True)
                    ins.then_inc(s("dense_mm2"), 1)

            dense(0, g_w1, g_w2)
            agg(3)
            agg(4)
            dense(1, g_w3, g_w4)
            agg(5)
            pe.matmul(bank[0][:, 0:1], m_w1u[:], m_u[:], start=True, stop=True).then_inc(s("u_bias_mm"), 1)
            pe.wait_ge(s("c1_ready"), 1)
            with pe.Fori(0, NB) as b:
                pe.wait_ge(s("mlp_staged"), b + 1)
                pe.wait_ge(s("mlp_vT"), b)
                pe.sem_inc(s("pe_turn"), 1)
                for q in range(BT):
                    pe.transpose(bank[0][0:D, q * P:q * P + P], stg[:, q, :], ident[:])
                for q in range(BT):
                    ins = pe.transpose(bank[1][0:D48, q * P:q * P + P], stg_e[:, q, :], ident[:])
                ins.then_inc(s("mlp_T"), 1)
                pe.wait_ge(s("mlp_vT"), b + 1)
                pe.matmul(bank[2][:], m_w1x[:], vT[:], start=True, stop=False)
                pe.matmul(bank[2][:], m_w1e[:], veT, start=False, stop=True).then_inc(s("mlp_mm1"), 1)
                pe.wait_ge(s("mlp_h1"), b + 1)
                pe.matmul(bank[3][:], m_w2[:], xs[:], start=True, stop=True).then_inc(s("mlp_mm2"), 1)
                pe.wait_ge(s("mlp_h2"), b + 1)
                pe.wait_ge(s("mlp_y"), b)
                for q in range(BT):
                    ins = pe.matmul(bank[4][:, q * D:q * D + D], xs2[:, q * P:q * P + P], m_w3[:], start=True, stop=True)
                ins.then_inc(s("mlp_mm3"), 1)


_INS = ["x", "src", "dst", "edge_attr_48", "edge_attr_64", "edge_type_16", "L0_gnn_W_shared", "L0_gnn_W_attn", "L0_gnn_W_rel",
        "L2_gnn_W1", "L2_gnn_b1", "L2_gnn_W2", "L2_gnn_b2", "L2_gnn_W3", "L2_gnn_b3", "L2_gnn_W4", "L2_gnn_b4",
        "L3_gnn_u", "L3_gnn_W1", "L3_gnn_b1", "L3_gnn_W2", "L3_gnn_b2", "L3_gnn_W3", "L3_gnn_b3"]


def kernel(**inputs):
    import numpy as _np
    import concourse.bacc as _bacc
    from concourse import mybir as _mybir
    from concourse.bass_utils import run_bass_kernel_spmd as _run

    nc = _bacc.Bacc("TRN2", target_bir_lowering=False, num_devices=1)
    arrays, aps = {}, {}
    for name in _INS:
        a = _np.ascontiguousarray(inputs[name])
        arrays[f"in_{name}"] = a
        aps[name] = nc.dram_tensor(f"in_{name}", a.shape, _mybir.dt.from_np(a.dtype), kind="ExternalInput").ap()
    out = nc.dram_tensor("out_0", (N, D), _mybir.dt.float32, kind="ExternalOutput").ap()
    build(nc, aps, out)
    r = _run(nc, [arrays], core_ids=[0])
    return r.results[0]["out_0"]
```

```python
import concourse.bass as bass
from concourse import mybir
from contextlib import ExitStack, contextmanager

N = 6250
E = 200000
D = 64
D48 = 48
R = 16
HID = 128
P = 128
BT = 4
NB = -(-N // (BT * P))
NT = NB * BT
NP = NT * P
NROW = NP + P
PAD_NODE = N + 50
K = 4
K3 = 2 * K
NC = -(-E // (P * K)) * K
ROUNDS = NC // K
NC3 = -(-E // (P * K3)) * K3
ROUNDS3 = NC3 // K3
ET = -(-NC // P)
NCT = ET * P
FULL = E // P
TAIL = E - FULL * P
EPS = 1e-5
SRC_T = -(-N // P)
GN = 16
NG = -(-N // GN)
CG = 6
A_SPLIT = 25
GW = SRC_T * GN
HG = 16
NH = -(-NG // HG)
COUNT_MAX = 16.0
RING = 32
LAG = 3
AHEAD = 5
TG = P // GN
assert NG == ROUNDS and NH % 2 == 1 and RING == TG * K


class Chain:

    def __init__(self, eng, sem):
        self.eng, self.sem = eng, sem
        self.base, self.i, self.per, self.k = 0, None, 0, 0

    def link(self, ins):
        ins.then_inc(self.sem, 1)
        self.k += 1
        at = self.base + self.k
        self.eng.wait_ge(self.sem, at if self.i is None else self.i * self.per + at)

    @contextmanager
    def over(self, trips, per):
        self.base, self.k = self.base + self.k, 0
        with self.eng.Fori(0, trips) as i:
            self.i, self.per = i, per
            yield i
        assert self.k == per, (self.k, per)
        self.base, self.i, self.k = self.base + per * trips, None, 0


def build(nc, A, out):
    f32, f16, i32, i16, f8 = mybir.dt.float32, mybir.dt.float16, mybir.dt.int32, mybir.dt.int16, mybir.dt.float8e4
    ALU, ACT, AX = mybir.AluOpType, mybir.ActivationFunctionType, mybir.AxisListType
    ctx = ExitStack()
    with ctx:
        def sb(name, shape, dt=f32):
            return ctx.enter_context(nc.sbuf_tensor(name, shape, dt))

        def sem(name):
            return ctx.enter_context(nc.semaphore(name))

        def dram(name, shape, dt=f32):
            return nc.dram_tensor(name, shape, dt, kind="Internal").ap()

        bank = [ctx.enter_context(nc.psum_tensor(f"bank{i}", [P, 512], f32)) for i in range(8)]

        rel_table = dram("rel_table", [NP * R, 2 * D])
        x_table = dram("x_table", [NP, D])
        l0_sums = [dram(f"l0_sums{k}", [NROW, 2 * D + 1]) for k in range(K)]
        agg_sums = [[dram(f"agg_sums{s}_{k}", [NROW, D]) for k in range(K)] for s in range(2)]
        l3_sums = [dram(f"l3_sums{k}", [NROW, D48 + 1]) for k in range(K3)]

        adjacency = dram("adjacency", [NG * P, GW // 4])
        starts_dram = dram("starts_dram", [4 * P], i32)

        ident = sb("ident", [P, P])
        ident16 = sb("ident16", [P, P], f16)
        before = sb("before", [P, P])
        discard_row = sb("discard_row", [P, 1])
        zeros = sb("zeros", [P, 848])
        w_shared = sb("w_shared", [D, D])
        w_attn = sb("w_attn", [D, 3])
        w_rel = sb("w_rel", [D, R, D])
        v_cols = sb("v_cols", [D, 3])
        v_sd = sb("v_sd", [D, 2])
        ve_row = sb("ve_row", [P, D])
        g_w1, g_w2 = sb("g_w1", [D, HID]), sb("g_w2", [HID, D])
        g_w3, g_w4 = sb("g_w3", [D, HID]), sb("g_w4", [HID, D])
        g_b1, g_b3 = sb("g_b1", [HID, 1]), sb("g_b3", [HID, 1])
        g_b2, g_b4 = sb("g_b2", [P, D]), sb("g_b4", [P, D])
        m_w1x, m_w1e, m_w1u = sb("m_w1x", [D, HID]), sb("m_w1e", [D48, HID]), sb("m_w1u", [32, HID])
        m_u = sb("m_u", [32, 1])
        m_w2, m_w3 = sb("m_w2", [HID, HID]), sb("m_w3", [HID, D])
        m_b1, m_b2, m_b3 = sb("m_b1", [HID, 1]), sb("m_b2", [HID, 1]), sb("m_b3", [P, D])
        m_c1 = sb("m_c1", [HID, 1])
        x = sb("x", [P, NT, D])
        h = sb("h", [P, NT, D])
        U = sb("U", [P, NT, D])
        G = sb("G", [P, NT, D])
        ld_all = sb("ld_all", [P, 2 * NT * D])
        ld = [ld_all[:, i * NT * D:(i + 1) * NT * D].rearrange("p (t d) -> p t d", d=D) for i in range(2)]
        hid_T = sb("hid_T", [HID, NP])
        mean, var, dinv, cnt = (sb(n, [P, NT]) for n in ("mean", "var", "dinv", "cnt"))
        ldc = sb("ldc", [P, NT])
        s12 = sb("s12", [P, NT, 2])
        eps = sb("eps", [P, 1])
        early = [hid_T[:, q * NCT:(q + 1) * NCT] for q in range(4)]
        idx_stage = early[0].bitcast(i32).rearrange("p (t c) -> p t c", c=P)
        idx_f = early[1].rearrange("p (t c) -> p t c", c=P)
        rel_and_z = sb("rel_and_z", [P, 2 * NCT])
        rel_f, z = rel_and_z[:, 0:NCT], rel_and_z[:, NCT:2 * NCT]
        src_f, dst_f = (sb(n, [P, NCT]) for n in ("src_f", "dst_f"))
        dst_first = sb("dst_first", [P, NCT])
        key16 = {k: (sb(f"{k}_hi16", [P, NCT], f16), sb(f"{k}_lo16", [P, NCT], f16)) for k in ("src", "dst")}
        dup = {"src": early[2], "dst": early[3]}
        he_prod = sb("he_prod", [P, 4 * 8 * D])
        he, prod = ([he_prod[:, i * 8 * D:(i + 1) * 8 * D].rearrange("p (c d) -> p c d", d=D) for i in pair] for pair in ((0, 1), (2, 3)))
        dup3, apart3 = sb("dup3", [P, K3]), sb("apart3", [P, K3])
        scratch = [sb(f"scratch{i}", [P, P]) for i in range(2)]
        gather_idx4 = sb("gather_idx4", [P, 2 * K], i32)
        gather_idx = [gather_idx4[:, k:k + 1] for k in range(K)]
        scatter_idx = [sb(f"scatter_idx{k}", [P, 1], i32) for k in range(K)]
        raw = [sb(f"raw{k}", [P, 2 * D + 1]) for k in range(K)]
        W3 = D48 + 1
        raw3 = [ld_all[:, k * W3:(k + 1) * W3] for k in range(K3)]
        raw3_all = ld_all[:, 0:K3 * W3].rearrange("p (k w) -> p k w", w=W3)
        comb3 = [ld_all[:, (K3 + k) * W3:(K3 + k + 1) * W3] for k in range(K3)]
        same3 = [ld_all[:, 2 * K3 * W3 + k * P:2 * K3 * W3 + (k + 1) * P] for k in range(K3)]
        l3_idx = sb("l3_targets", [P, K3], i32)
        same = [sb(f"same{k}", [P, P]) for k in range(K)]
        comb = [sb(f"comb{k}", [P, 2 * D + 1]) for k in range(K)]
        hT = sb("hT", [D, 512])
        rel_stage = [ld_all[:, i * NT * D:i * NT * D + R * 2 * D].rearrange("p (r d) -> p r d", r=R) for i in range(2)]
        stg = sb("stg", [P, BT, D])
        stgh = stg
        stg_e = he[1].rearrange("p c d -> p (c d)")[:, 0:BT * D48].rearrange("p (t d) -> p t d", t=BT)
        veT = he[0][0:D48].rearrange("p c d -> p (c d)")
        xs2 = prod[0].rearrange("p c d -> p (c d)")
        vT, xs = sb("vT", [D, 512]), sb("xs", [HID, 512])

        ones = sb("ones", [P, P])
        twice = sb("twice", [P, D])
        count_key = sb("count_key", [P, SRC_T, GN], i16)
        io128 = sb("io128", [P, P], f16)
        io128f = sb("io128f", [P, P])
        is_group = sb("is_group", [P, 4])
        minus_base = sb("minus_base", [P, NG])
        group_first, group_past = sb("group_first", [P, 4]), sb("group_past", [P, 4])
        first_chunk, last_chunk = sb("first_chunk", [P, 4]), sb("last_chunk", [P, 4])
        first_chunk_i = sb("first_chunk_i", [P, 4], i32)
        starts = sb("starts", [1, 4 * P], i32)
        verdict = sb("verdict", [P, 4])
        flags = sb("flags", [1, 2], i32)
        minus_max = sb("minus_max", [P, 1])
        over_sum = sb("over_sum", [P, 1])
        flat3 = lambda t: t[:].rearrange("p t d -> p (t d)")
        pair_key = flat3(h)[:, 0:NCT]
        minus_group = flat3(h)[:, NCT:2 * NCT]
        RW = 2 * D + 1
        ring = ld_all[:, 0:RING * RW].rearrange("p (c w) -> p c w", w=RW)
        at = RING * RW
        over = ld_all[:, at:at + 2 * NG]
        at += 2 * NG
        count_words = ld_all[:, at:at + GW // 4]
        count_stage = count_words.bitcast(f8)
        at += GW // 4
        over_junk = ld_all[:, at:at + GW // 2].bitcast(f16)
        assert at + GW // 2 <= 2 * NT * D
        at, pair_hot, lo_hot, dst_hot, lo_in, dst_in, pair_in = 0, [], [], [], [], [], []
        for q in range(2):
            pair_hot.append(hid_T[:, at:at + CG * GW // 2].bitcast(f16).rearrange("p (c f) -> p c f", c=CG))
            at += CG * GW // 2
            lo_hot.append(hid_T[:, at:at + CG * P // 2].bitcast(f16).rearrange("p (c f) -> p c f", c=CG))
            at += CG * P // 2
            lo_in.append(hid_T[:, at:at + CG])
            dst_in.append(hid_T[:, at + CG:at + 2 * CG])
            pair_in.append(hid_T[:, at + 2 * CG:at + 3 * CG])
            at += 3 * CG
            dst_hot.append(he_prod[:, q * CG * P:(q + 1) * CG * P].rearrange("p (c f) -> p c f", c=CG))
        assert at <= NP
        count_bank = [(4, 5), (0, 1)]
        ring_idx = [gather_idx4[:, q * K:(q + 1) * K] for q in range(2)]
        x16 = ld_all[:, 0:SRC_T * P // 2].bitcast(f16).rearrange("p (t f) -> p t f", t=SRC_T)
        half_words = [t[:, 0:HG * GW // 4] for t in (ld_all[:, NT * D:2 * NT * D], rel_and_z[:, :])]
        a_half = [t.bitcast(f8).rearrange("p (g f) -> p g f", g=HG) for t in half_words]
        accT = [sb(f"accT{q}", [P, HG * GN]) for q in range(2)]
        top2, scale_row, unscale, diag = sb("top2", [P, 2, D]), sb("scale_row", [P, D]), sb("unscale", [P, D]), sb("diag", [P, P])
        feature_top, feature_inv = sb("feature_top", [P, 1]), sb("feature_inv", [P, 1])

        S = {}

        def s(name):
            if name not in S:
                S[name] = sem(name)
            return S[name]

        block = ctx.enter_context(nc.Block())

        col1 = lambda v: v.rearrange("(k a) -> k a", a=1)
        small = [(w_shared[:], A["L0_gnn_W_shared"]), (w_attn[:], A["L0_gnn_W_attn"].rearrange("a (k o) -> o (a k)", o=D)),
                 (w_rel[:], A["L0_gnn_W_rel"].rearrange("r i o -> i r o")),
                 (g_w1[:], A["L2_gnn_W1"]), (g_w2[:], A["L2_gnn_W2"]), (g_w3[:], A["L2_gnn_W3"]), (g_w4[:], A["L2_gnn_W4"]),
                 (g_b1[:], col1(A["L2_gnn_b1"])), (g_b3[:], col1(A["L2_gnn_b3"])),
                 (g_b2[:], A["L2_gnn_b2"].partition_broadcast(P)), (g_b4[:], A["L2_gnn_b4"].partition_broadcast(P)),
                 (m_w1x[:], A["L3_gnn_W1"][0:D, :]), (m_w1e[:], A["L3_gnn_W1"][D:D + D48, :]),
                 (m_w1u[:], A["L3_gnn_W1"][D + D48:D + D48 + 32, :]), (m_u[:], A["L3_gnn_u"][0:1, :].rearrange("a k -> k a")),
                 (m_w2[:], A["L3_gnn_W2"]), (m_w3[:], A["L3_gnn_W3"]),
                 (m_b1[:], col1(A["L3_gnn_b1"])), (m_b2[:], col1(A["L3_gnn_b2"])), (m_b3[:], A["L3_gnn_b3"].partition_broadcast(P))]

        def he_piece(c0, n):
            return A["edge_attr_64"][c0 * P:(c0 + n) * P, :].rearrange("(c p) d -> p c d", p=P)

        HE_ROUNDS = FULL // 16
        HE_REST = FULL - HE_ROUNDS * 16
        NODE_TAIL = N - (N // P) * P
        WHOLE = N // P

        def zero_table(eng, table, width, signal):
            flat = table.rearrange("(p a) d -> p (a d)", p=P)
            total, at, n = (NROW // P) * width, 0, 0
            while at < total:
                w = min(848, total - at)
                eng.dma_start(flat[:, at:at + w], zeros[:, 0:w]).then_inc(signal, 16)
                at, n = at + w, n + 1
            return n

        def node_rows(table):
            return table[0:NP, :].rearrange("(t p) d -> p t d", p=P)

        PASSES = [("l0", 2 * D + 1, "dst")] + [(f"agg{j}", D, "dst") for j in range(6)] + [("l3", D48 + 1, "src")]

        FAMILY = ["l0"] + ["agg"] * 6 + ["l3"]
        BEFORE = [0] + list(range(6)) + [0]
        DEPTH = [K] * 7 + [K3]
        COUNT = [NC] * 7 + [NC3]
        ROW_BANKS = [(0, 1)] * 7 + [(0, 1, 4, 5)]

        def sums(j):
            name = PASSES[j][0]
            return l0_sums if name == "l0" else l3_sums if name == "l3" else agg_sums[j % 2]

        def loads(j, k):
            per = {"l0": 3, "l3": 2, "agg": 1}[FAMILY[j]]
            return per * (BEFORE[j] * 2 + k // 2 + 1)

        @block.sync
        def _(sp):
            for dst_ap, src_ap in small:
                sp.dma_start(dst_ap, src_ap, allow_slow_non_contiguous=True).then_inc(s("small_loaded"), 16)
            sp.wait_ge(s("memset_done"), 1)
            sp.dma_start(x[:, 0:WHOLE, :], A["x"][0:WHOLE * P, :].rearrange("(t p) d -> p t d", p=P)).then_inc(s("x_loaded"), 16)
            sp.dma_start(x[0:NODE_TAIL, WHOLE, :], A["x"][WHOLE * P:N, :]).then_inc(s("x_loaded"), 16)
            for n, name in enumerate(("src", "dst", "edge_type_16")):
                if n:
                    sp.wait_ge(s("idx_cast"), n)
                a = A[name]
                whole = (ET - 1) * P * P
                rest = FULL - (ET - 1) * P
                sp.dma_start(idx_stage[:, 0:ET - 1, :], a[0:whole].rearrange("(t c p) -> c t p", c=P, p=P)).then_inc(s("idx_loaded"), 16)
                sp.dma_start(idx_stage[0:rest, ET - 1, :], a[whole:FULL * P].rearrange("(c p) -> c p", p=P)).then_inc(s("idx_loaded"), 16)
                sp.dma_start(idx_stage[rest:rest + 1, ET - 1, 0:TAIL], a[FULL * P:E].rearrange("(c p) -> c p", p=TAIL)).then_inc(s("idx_loaded"), 16)
            sp.wait_ge(s("chunks_ready"), 1)
            sp.dma_start(starts_dram.rearrange("(t p) -> p t", p=P), first_chunk_i[:], allow_slow_non_contiguous=True).then_inc(s("starts_out"), 16)
            sp.wait_ge(s("starts_out"), 16)
            sp.dma_start(starts[:], starts_dram.rearrange("(a n) -> a n", a=1)).then_inc(s("starts_in"), 16)
            nz = 0
            for t in l3_sums:
                nz += zero_table(sp, t, D48 + 1, s("l3_zeroed"))
            sp.wait_ge(s("l3_zeroed"), 16 * nz)
            sp.sem_inc(s("l3_go"), 1)
            sp.wait_ge(s("flag1_ready"), 1)

            def l3_edges(r, k):
                sp.wait_ge(s("l3_comb_done"), r * K3 + (k + K))
                sp.dma_start(raw3_all[:, k:k + K, 0:D48], A["edge_attr_48"][bass.ds((r * K3 + k) * P, K * P), :].rearrange("(c p) d -> p c d", p=P)) \
                    .then_inc(s(f"edges_loaded{k // K}"), 16)

            with sp.Fori(0, HE_ROUNDS) as i:
                for q in range(2):
                    sp.wait_ge(s("he_free"), i * 2 + q + 1)
                    sp.dma_start(he[q], A["edge_attr_64"][bass.ds((i * 2 + q) * 8 * P, 8 * P), :].rearrange("(c p) d -> p c d", p=P)).then_inc(s(f"he_loaded{q}"), 16)
                    for k in range(0, K3, K):
                        l3_edges(i * 2 + q, k)
            sp.wait_ge(s("he_free"), HE_ROUNDS * 2 + 1)
            sp.dma_start(he[0][:, 0:8, :], he_piece(HE_ROUNDS * 16, 8)).then_inc(s("he_loaded0"), 16)
            sp.wait_ge(s("he_free"), HE_ROUNDS * 2 + 2)
            rest2 = HE_REST - 8
            sp.dma_start(he[1][:, 0:rest2, :], he_piece(HE_ROUNDS * 16 + 8, rest2)).then_inc(s("he_loaded1"), 16)
            sp.dma_start(he[1][0:TAIL, rest2, :], A["edge_attr_64"][FULL * P:E, :]).then_inc(s("he_loaded1"), 16)
            for r in range(HE_ROUNDS * 2, ROUNDS3 - 1):
                for k in range(0, K3, K):
                    l3_edges(r, k)
            c = (ROUNDS3 - 1) * K3
            sp.wait_ge(s("l3_comb_done"), c + K)
            sp.dma_start(raw3_all[0:TAIL, FULL - c, 0:D48], A["edge_attr_48"][FULL * P:E, :]).then_inc(s("edges_tail"), 16)
            sp.wait_ge(s("edges_tail"), 16)
            sp.dma_start(raw3_all[:, 0:FULL - c, 0:D48], A["edge_attr_48"][c * P:FULL * P, :].rearrange("(c p) d -> p c d", p=P)) \
                .then_inc(s("edges_loaded0"), 16)
            sp.sem_inc(s("edges_loaded1"), 16)
            with sp.Fori(0, NB) as b:
                for q in range(BT):
                    sp.wait_ge(s("rel_staged"), b * BT + q + 2)
                    sp.dma_start(rel_table[bass.ds((b * BT + q) * P * R, P * R), :].rearrange("(p r) d -> p r d", r=R),
                                 rel_stage[q % 2]).then_inc(s(f"rel_stored{q % 2}"), 16)
            sp.wait_ge(s("rel_stored0"), 16 * NT // 2)
            sp.wait_ge(s("rel_stored1"), 16 * NT // 2)
            sp.sem_inc(s("rel_ready"), 1)

            def load_sums(j):
                name, fam, b = PASSES[j][0], FAMILY[j], BEFORE[j]
                for k in range(DEPTH[j]):
                    sp.wait_ge(s(f"{fam}_scattered{k}"), 16 * (COUNT[j] // DEPTH[j]) * (b + 1))
                for k in range(DEPTH[j]):
                    rows = node_rows(sums(j)[k])
                    if name == "l0":
                        pieces = [(ld[0], rows[:, :, 0:D]), (ld[1], rows[:, :, D:2 * D]), (ldc[:], rows[:, :, 2 * D])]
                    elif name == "l3":
                        pieces = [(ld[k % 2][:, :, 0:D48], rows[:, :, 0:D48]), (ldc[:], rows[:, :, D48])]
                    else:
                        pieces = [(ld[k % 2], rows)]
                    if fam in ("l0", "l3"):
                        sp.wait_ge(s(f"{fam}_read"), b * K + k)
                    elif k >= 2:
                        sp.wait_ge(s(f"{fam}_read"), b * K + k - 1)
                    for buf, view in pieces:
                        sp.dma_start(buf, view, allow_slow_non_contiguous=True).then_inc(s(f"{fam}_loaded{k % 2}"), 16)
                sp.wait_ge(s(f"{fam}_read"), b * K + DEPTH[j])

            sp.wait_ge(s("flag1_ready"), 1)
            flag1 = sp.value_load(flags[0:1, 0:1], min_val=0, max_val=1)
            with sp.If(flag1):
                sp.wait_ge(s("adjacency_ready"), 1)
            with sp.Else():
                n = 0
                for t in l0_sums:
                    n += zero_table(sp, t, 2 * D + 1, s("l0_zeroed"))
                sp.wait_ge(s("l0_zeroed"), 16 * n)
                sp.sem_inc(s("l0_go"), 1)
                load_sums(0)
            sp.wait_ge(s("flag2_ready"), 1)
            flag2 = sp.value_load(flags[0:1, 1:2], min_val=0, max_val=1)
            for a in range(6):
                sp.wait_ge(s("u_ready"), a + 1)
                with sp.If(flag2):
                    def half(at_row, slot, used, n=HG):
                        sp.wait_ge(s("half_mm"), used)
                        sp.dma_start(half_words[slot][:, 0:n * GW // 4].rearrange("p (g f) -> p g f", g=n), adjacency[bass.ds(at_row, n * P), :].rearrange("(g p) f -> p g f", p=P)) \
                            .then_inc(s(f"half_in{slot}"), 16)
                    if a == 0:
                        for q in range(2):
                            half(q * HG * P, q, q + 1)
                    with sp.Fori(0, NH // 2 - 1) as i:
                        for q in range(2):
                            half(i * (2 * HG * P) + (q + 2) * HG * P, q, i * 2 + (q + 3 + NH * a))
                    half((NH - 1) * HG * P, 0, NH * a + NH, n=NG - (NH - 1) * HG)
                    if a < 5:
                        half(HG * P, 1, NH * (a + 1) + 1)
                        half(0, 0, NH * (a + 1) + 2)
                with sp.Else():
                    sp.dma_start(node_rows(x_table), U[:]).then_inc(s("x_table_stored"), 16)
                    sp.wait_ge(s("x_table_stored"), 16 * (a + 1))
                    n = 0
                    for t in sums(a + 1):
                        n += zero_table(sp, t, D, s("agg_zeroed"))
                    sp.wait_ge(s("agg_zeroed"), 16 * n * (a + 1))
                    sp.sem_inc(s("table_ready"), 1)
                    load_sums(a + 1)
            sp.wait_ge(s("l3_sums_wanted"), 1)
            load_sums(7)
            sp.wait_ge(s("out_ready"), 1)
            sp.dma_start(out[0:WHOLE * P, :].rearrange("(t p) d -> p t d", p=P), G[:, 0:WHOLE, :]).then_inc(s("out_stored"), 16)
            sp.dma_start(out[WHOLE * P:N, :], G[0:NODE_TAIL, WHOLE, :]).then_inc(s("out_stored"), 16)
            sp.wait_ge(s("out_stored"), 32)

        @block.gpsimd
        def _(pool):
            ch = Chain(pool, s("pool_chain"))
            ch.link(pool.memset(ident[:], 0.0))
            ch.link(pool.memset(before[:], 1.0))
            ch.link(pool.affine_select(out=ident[:], in_=ident[:], compare_op=ALU.not_equal, fill=1.0, base=0,
                                       pattern=[[-1, P]], channel_multiplier=1))
            ch.link(pool.affine_select(out=before[:], in_=before[:], compare_op=ALU.is_gt, fill=0.0, base=0,
                                       pattern=[[-1, P]], channel_multiplier=1))
            ch.link(pool.iota(discard_row[:], pattern=[[0, 1]], base=NP, channel_multiplier=1, allow_small_or_imprecise_dtypes=True))
            exact = dict(allow_small_or_imprecise_dtypes=True)
            ch.link(pool.memset(ones[:], 1.0))
            ch.link(pool.memset(minus_max[:], -COUNT_MAX))
            ch.link(pool.iota(count_key[:], pattern=[[512, SRC_T], [1, GN]], base=0, channel_multiplier=0, **exact))
            ch.link(pool.iota(io128[:], pattern=[[1, P]], base=1, channel_multiplier=0, **exact))
            ch.link(pool.iota(io128f[:], pattern=[[1, P]], base=1, channel_multiplier=0, **exact))
            ch.link(pool.iota(minus_base[:], pattern=[[-GN, NG]], base=0, channel_multiplier=0, **exact))
            ch.link(pool.iota(group_first[:], pattern=[[GN * P, 4]], base=0, channel_multiplier=GN, **exact))
            ch.link(pool.iota(group_past[:], pattern=[[GN * P, 4]], base=GN, channel_multiplier=GN, **exact))
            ch.link(pool.tensor_tensor(twice[:], ident[:, 0:D], ident[:, D:2 * D], ALU.add))
            pool.tensor_copy(ident16[:], ident[:]).then_inc(s("const_ready"), 1)

            def edge_pass(j):
                name, width, key = PASSES[j]
                fam, b = FAMILY[j], BEFORE[j]
                if fam == "agg":
                    pool.wait_ge(s("table_ready"), b + 1)
                n = DEPTH[j]
                with pool.Fori(0, COUNT[j] // n) as i:
                    c1 = [i * n + k + 1 + b * NC for k in range(n)]
                    if name != "l3":
                        src_ap = rel_table if name == "l0" else x_table
                        for k in range(K):
                            pool.wait_ge(s(f"{fam}_gather_idx"), c1[k])
                            pool.wait_ge(s(f"{fam}_comb_done"), c1[k])
                            pool.sem_inc(s("pool_turn"), 1)
                            pool.indirect_dma_start(raw[k][:, 0:width - 1 if name == "l0" else width], None, src_ap,
                                                    bass.IndirectOffsetOnAxis(ap=gather_idx[k][:], axis=0)).then_inc(s(f"{fam}_gathered{k}"), 16)
                    for k in range(n):
                        if name == "l3" and k % K == 0:
                            pool.wait_ge(s("l3_idx_ready"), i * 2 + k // K + 1)
                        pool.wait_ge(s(f"{fam}_comb_ready"), c1[k] + 2)
                        pool.sem_inc(s("pool_turn"), 1)
                        pool.indirect_dma_start(sums(j)[k], bass.IndirectOffsetOnAxis(ap=l3_idx[:, k:k + 1] if name == "l3" else scatter_idx[k][:], axis=0),
                                                (comb3[k] if name == "l3" else comb[k])[:, 0:width], None, compute_op=ALU.add,
                                                bounds_check=NROW - 1).then_inc(s(f"{fam}_scattered{k}"), 16)

            pool.wait_ge(s("l3_go"), 1)
            edge_pass(7)
            pool.wait_ge(s("flag1_ready"), 1)
            flag1 = pool.value_load(flags[0:1, 0:1], min_val=0, max_val=1)
            pool.wait_ge(s("rel_ready"), 1)

            def gather_round(r, q, half):
                pool.wait_ge(s("summed"), r + (TG - AHEAD))
                pool.wait_ge(s(f"ring_in{q % 2}"), half * (16 * K))
                pool.tensor_copy(ring_idx[q % 2], rel_f[:, bass.ds(r * K, K)]).then_inc(s("ring_idx"), 1)
                pool.wait_ge(s("ring_idx"), r + 1)
                pool.sem_inc(s("pool_turn"), 1)
                for k in range(K):
                    pool.indirect_dma_start(ring[:, q * K + k, 0:2 * D], None, rel_table,
                                            bass.IndirectOffsetOnAxis(ap=ring_idx[q % 2][:, k:k + 1], axis=0)).then_inc(s(f"ring_in{q % 2}"), 16)

            with pool.If(flag1):
                pool.wait_ge(s("ring_ready"), 1)
                with pool.Fori(0, ROUNDS // TG) as b:
                    for q in range(TG):
                        gather_round(b * TG + q, q, b * (TG // 2) + q // 2)
                for r in range(ROUNDS // TG * TG, ROUNDS):
                    gather_round(r, r % TG, r // 2)
            with pool.Else():
                pool.wait_ge(s("l0_go"), 1)
                edge_pass(0)
            pool.wait_ge(s("flag2_ready"), 1)
            flag2 = pool.value_load(flags[0:1, 1:2], min_val=0, max_val=1)
            with pool.If(flag2):
                pool.sem_inc(s("pool_turn"), 1)
            with pool.Else():
                for a in range(6):
                    edge_pass(a + 1)

        @block.scalar
        def _(act):
            ch = Chain(act, s("act_chain"))
            for fam in ("l0", "agg", "l3"):
                act.sem_inc(s(f"{fam}_comb_ready"), 2)
            act.sem_inc(s("half_out"), 2)
            act.sem_inc(s("counts_read"), 1)
            act.wait_ge(s("memset_done"), 1)

            def rstd(n):
                act.wait_ge(s("var_ready"), n)
                act.activation(var[:], var[:], ACT.Sqrt, bias=eps[:], scale=1.0 / D).then_inc(s("std_ready"), 1)

            def edge_round(j, r, k0, count=None):
                name, width, key = PASSES[j]
                fam, b = FAMILY[j], BEFORE[j]
                idx = rel_f if name == "l0" else src_f
                n = DEPTH[j]
                dma_free = r * 16 + b * ROUNDS * 16
                for k in range(K if name != "l3" else 0):
                    act.wait_ge(s(f"{fam}_gathered{k}"), dma_free)
                    act.copy(gather_idx[k][:], idx[:, bass.ds(k0 + k, 1)]).then_inc(s(f"{fam}_gather_idx"), 1)
                for k in range(n):
                    act.wait_ge(s(f"{fam}_scattered{k}"), dma_free)
                    if name != "l3":
                        act.copy(scatter_idx[k][:], dst_first[:, bass.ds(k0 + k, 1)])
                    act.wait_ge(s(f"{fam}_comb_done"), k0 + (k + 1 + b * NC + n))
                    act.copy((comb3[k] if name == "l3" else comb[k])[:, 0:width], bank[2 + k % 2][:, 0:width]).then_inc(s(f"{fam}_comb_ready"), 1)
                    if k == 1 and count is not None:
                        count()

            def edge_pass(j):
                with act.Fori(0, COUNT[j] // DEPTH[j]) as i:
                    edge_round(j, i, i * DEPTH[j])

            def store_counts(g, q):
                act.wait_ge(s("summed"), g + (1 + TG))
                act.wait_ge(s("counts_stored"), g * 16)
                act.sem_inc(s("act_turn"), 1)
                w0 = A_SPLIT * GN
                b0, b1 = (bank[n] for n in count_bank[q % 2])
                act.copy(count_stage[:, 0:w0], b0[:, 0:w0], saturate=False)
                act.copy(count_stage[:, w0:GW], b1[:, 0:GW - w0], saturate=False)
                act.wait_ge(s("counts_read"), g + 1)
                act.activation(over_junk[:, 0:w0], b0[:, 0:w0], ACT.Relu, bias=minus_max[:], accum_out=over[:, bass.ds(g * 2, 1)])
                act.activation(over_junk[:, w0:GW], b1[:, 0:GW - w0], ACT.Relu, bias=minus_max[:],
                               accum_out=over[:, bass.ds(g * 2 + 1, 1)]).then_inc(s("counts_read"), 1)
                act.wait_ge(s("counts_read"), g + 2)
                act.dma_start(adjacency[bass.ds(g * P, P), :], count_words).then_inc(s("counts_stored"), 16)

            edge_pass(7)
            for k in range(K3):
                act.wait_ge(s(f"l3_scattered{k}"), 16 * ROUNDS3)
            rstd(1)
            with act.Fori(0, NB) as b:
                act.wait_ge(s("h_T"), b + 1)
                act.copy(hT[:], bank[0][0:D, :]).then_inc(s("hT_ready"), 1)
                for q in range(BT):
                    act.wait_ge(s("rel_mm"), b * BT + q + 1)
                    act.wait_ge(s(f"rel_stored{q % 2}"), (b * 2 + q // 2) * 16)
                    for half in range(2):
                        ins = act.copy(rel_stage[q % 2][:, half * 8:half * 8 + 8, D:2 * D],
                                       bank[1 + 3 * (q % 2) + half][:, :].rearrange("p (r o) -> p r o", o=D))
                    ins.then_inc(s("rel_h"), 1)
            act.wait_ge(s("flag1_ready"), 1)
            flag1 = act.value_load(flags[0:1, 0:1], min_val=0, max_val=1)
            with act.If(flag1):
                def tile_out(t, groups):
                    act.wait_ge(s("summed"), groups + TG)
                    tile = bass.ds(t, 1)
                    act.copy(G[:, tile, :], bank[6][:, 0:D].unsqueeze(1))
                    act.copy(U[:, tile, :], bank[6][:, D:2 * D].unsqueeze(1))
                    act.copy(cnt[:, tile], bank[6][:, 2 * D:2 * D + 1]).then_inc(s("tile_out"), 1)

                with act.Fori(0, NG // TG) as b:
                    for q in range(TG):
                        if q == TG - 1:
                            tile_out(b, b * TG + TG)
                        store_counts(b * TG + q, q)
                for g in range(NG // TG * TG, NG):
                    store_counts(g, g)
                tile_out(NG // TG, NG)
                act.wait_ge(s("tile_out"), NG // TG + 1)
                act.wait_ge(s("counts_stored"), NG * 16)
                act.sem_inc(s("adjacency_ready"), 1)
            with act.Else():
                act.wait_ge(s("dst_first_ready"), 1)
                edge_pass(0)
            act.wait_ge(s("flag2_ready"), 1)
            flag2 = act.value_load(flags[0:1, 1:2], min_val=0, max_val=1)

            def agg(a):
                with act.If(flag2):
                    def out(m, slot, tiles):
                        act.wait_ge(s("half_fin"), m + 3)
                        act.copy(G[:, tiles, :], bank[2 + slot][:, 0:2 * D].rearrange("p (t d) -> p t d", d=D)).then_inc(s("half_out"), 1)
                    with act.Fori(0, NH // 2) as i:
                        for q in range(2):
                            out(i * 2 + (q + NH * a), q, bass.ds(i * 4 + 2 * q, 2))
                    out(NH * a + NH - 1, 0, slice(2 * (NH - 1), 2 * NH))
                with act.Else():
                    edge_pass(a + 1)

            rstd(2)
            agg(0)
            agg(1)
            rstd(3)
            act.wait_ge(s("deg_ready"), 1)
            act.activation(dinv[:], cnt[:], ACT.Sqrt).then_inc(s("deg_sqrt"), 1)
            agg(2)

            def dense(n, bias):
                m0 = n * NB

                def stage(b):
                    act.copy(stg[:], G[:, bass.ds(b * BT, BT), :]).then_inc(s("dense_staged"), 1)

                def relu(b):
                    act.wait_ge(s("dense_mm1"), b + (1 + m0))
                    act.activation(xs[:], bank[1][:], ACT.Relu, bias=bias[:]).then_inc(s("dense_relu"), 1)
                stage(0)
                with act.Fori(0, NB - 1) as b:
                    act.wait_ge(s("dense_T"), b + (1 + m0))
                    stage(b + 1)
                    relu(b)
                relu(NB - 1)

            act.wait_ge(s("g_ready"), 1)
            dense(0, g_b1)
            agg(3)
            agg(4)
            act.wait_ge(s("g_ready"), 2)
            dense(1, g_b3)
            agg(5)
            rstd(4)
            act.wait_ge(s("u_bias_mm"), 1)
            act.activation(m_c1[:], bank[0][:, 0:1], ACT.Identity, bias=m_b1[:]).then_inc(s("c1_ready"), 1)
            act.wait_ge(s("c1_ready"), 1)
            act.wait_ge(s("ve_ready"), 1)
            def stage(b):
                act.copy(stg[:], h[:, bass.ds(b * BT, BT), :])
                act.copy(stg_e, ld[0][:, bass.ds(b * BT, BT), 0:D48]).then_inc(s("mlp_staged"), 1)

            def relus(b):
                act.wait_ge(s("mlp_mm1"), b + 1)
                act.activation(xs[:], bank[2][:], ACT.Relu, bias=m_c1[:]).then_inc(s("mlp_h1"), 1)
                act.wait_ge(s("mlp_mm2"), b + 1)
                act.activation(xs2, bank[3][:], ACT.Relu, bias=m_b2[:]).then_inc(s("mlp_h2"), 1)
            stage(0)
            with act.Fori(0, NB - 1) as b:
                act.wait_ge(s("mlp_T"), b + 1)
                stage(b + 1)
                relus(b)
            relus(NB - 1)

        @block.vector
        def _(v):
            ch = Chain(v, s("dve_chain"))
            link = lambda ins: chains[-1].link(ins)
            chains = [ch]
            fast = Chain(v, s("dve_fast_chain"))
            slow = Chain(v, s("dve_slow_chain"))
            v.sem_inc(s("he_free"), 2)
            v.sem_inc(s("dup_done"), K)
            for fam, banks in (("l0", ROW_BANKS[0]), ("agg", ROW_BANKS[1]), ("l3", ROW_BANKS[7])):
                v.sem_inc(s(f"{fam}_same_ready"), len(banks))
            v.sem_inc(s("acc_read"), 2)
            v.sem_inc(s("rel_staged"), 1)
            v.memset(verdict[:], 0)
            for t in (zeros[:], x[:], z, dup["src"], dup["dst"], he[0], he[1], idx_stage):
                v.memset(t, 0)
            for k in range(K):
                v.memset(raw[k][:], 1.0)
            link(v.memset(eps[:], EPS))
            v.memset(idx_stage[:, ET - 1, :], PAD_NODE).then_inc(s("memset_done"), 1)

            groups = [(g, min(4, ET - g * 4)) for g in range(-(-ET // 4))]
            done = 0
            for n, (tab, pad) in enumerate(((src_f, None), (dst_f, None), (rel_f, None))):
                v.wait_ge(s("idx_loaded"), 48 * (n + 1))
                if n:
                    v.wait_ge(s("idx_T"), len(groups) * n)
                v.tensor_copy(idx_f, idx_stage).then_inc(s("idx_cast"), 1)
                if n == 1:
                    v.wait_ge(s("idx_cast"), 2)
                    smaller = ld_all[:, 0:ET * (P - 1)].rearrange("p (t c) -> p t c", t=ET)
                    link(v.tensor_tensor(smaller, idx_f[:, :, 1:P], idx_f[:, :, 0:P - 1], ALU.is_lt))
                    link(v.tensor_reduce(verdict[:, 0:1], smaller, axis=AX.XY, op=ALU.add))
                for g, w in groups:
                    v.wait_ge(s("idx_T"), len(groups) * n + g + 1)
                    link(v.tensor_copy(tab[:, g * 512:g * 512 + w * P], bank[g][:, 0:w * P]))
            link(v.tensor_scalar(rel_f, rel_f, float(R - 1), None, ALU.min))
            link(v.scalar_tensor_tensor(rel_f, src_f[:], float(R), rel_f, ALU.mult, ALU.add))
            for name, tab in (("src", src_f), ("dst", dst_f)):
                hi, lo = key16[name]
                tmp = idx_stage.rearrange("p t c -> p (t c)")
                tmpf = idx_f.rearrange("p t c -> p (t c)")
                link(v.tensor_copy(tmp, tab[:]))
                link(v.tensor_scalar(tmp, tmp, P - 1, None, ALU.bitwise_and))
                link(v.tensor_copy(tmpf, tmp))
                link(v.tensor_copy(lo[:], tmpf))
                link(v.tensor_tensor(hi[:], tab[:], tmpf, ALU.subtract))
            v.tensor_copy(scratch[0][:, 0:1], dst_f[:, 0:1]).then_inc(s("keys_ready"), 1)

            rows = [ld_all[:, NT * D + m * NCT:NT * D + (m + 1) * NCT] for m in range(2)]
            compared = ld_all[:, 0:NC]
            for m in range(2):
                v.wait_ge(s("edge_row"), m + 1)
                for g, w in groups:
                    ins = v.tensor_copy(rows[m][:, g * 512:g * 512 + w * P], bank[g][:, 0:w * P])
                link(ins)
                v.sem_inc(s("edge_row_read"), 1)
            link(v.tensor_tensor(compared[:, 0:NC - 1], rows[1][:, 1:NC], rows[0][:, 0:NC - 1], ALU.is_lt))
            link(v.tensor_reduce(verdict[:, 1:2], compared[:, 0:NC - 1], axis=AX.X, op=ALU.add))
            link(v.tensor_scalar(is_group[:], group_first[:], float(N) - 0.5, None, ALU.is_lt))
            for nodes, chunks in ((group_first, first_chunk), (group_past, last_chunk)):
                for t in range(4):
                    link(v.tensor_scalar(compared, rows[0][:, 0:NC], nodes[:, t:t + 1], 0.0, ALU.is_lt, ALU.add,
                                         accum_out=chunks[:, t:t + 1]))
            link(v.tensor_copy(first_chunk_i[:], first_chunk[:]))
            v.sem_inc(s("chunks_ready"), 1)
            link(v.tensor_tensor(last_chunk[:], last_chunk[:], first_chunk[:], ALU.subtract))
            link(v.tensor_scalar(last_chunk[:], last_chunk[:], CG - 0.5, None, ALU.is_gt))
            link(v.tensor_reduce(verdict[:, 2:3], last_chunk[:], axis=AX.X, op=ALU.add))
            link(v.scalar_tensor_tensor(last_chunk[:], group_first[:], -float(K) / GN, first_chunk[:], ALU.mult, ALU.add))
            link(v.tensor_scalar(first_chunk[:], last_chunk[:], K * (LAG + 1) - CG + 0.5, None, ALU.is_gt))
            link(v.tensor_scalar(last_chunk[:], last_chunk[:], K * AHEAD - RING + K - 0.5, None, ALU.is_lt))
            link(v.tensor_tensor(last_chunk[:], last_chunk[:], first_chunk[:], ALU.add))
            link(v.tensor_tensor(last_chunk[:], last_chunk[:], is_group[:], ALU.mult))
            link(v.tensor_reduce(verdict[:, 3:4], last_chunk[:], axis=AX.X, op=ALU.add))
            link(v.tensor_tensor(verdict[:, 2:3], verdict[:, 2:3], verdict[:, 3:4], ALU.add))
            link(v.tensor_reduce(verdict[:, 3:4], verdict[:, 0:3], axis=AX.X, op=ALU.add))
            v.sem_inc(s("verdict_ready"), 1)
            v.wait_ge(s("verdict_mm"), 1)
            link(v.tensor_scalar(flags[:, 0:1], bank[7][0:1, 0:1], 0.5, None, ALU.is_lt))
            link(v.memset(ld_all[:, 0:K3 * W3], 1.0))
            v.sem_inc(s("flag1_ready"), 1)

            v.wait_ge(s("ve_mm"), 1)
            link(v.tensor_copy(ve_row[:], bank[5][:, 0:D]))
            v.tensor_copy(v_cols[:], bank[4][0:D, 0:3]).then_inc(s("v_cols_ready"), 1)

            def z_piece(n, q, cols, dst_ap):
                v.wait_ge(s("he_free"), n + 1)
                link(v.tensor_tensor(prod[q][:, 0:cols, :], he[q][:, 0:cols, :],
                                     ve_row[:].unsqueeze(1).to_broadcast([P, cols, D]), ALU.mult))
                v.reduce_sum(dst_ap, prod[q][:, 0:cols, :], axis=AX.X).then_inc(s("he_free"), 1)

            def rest_of_z():
                v.wait_ge(s("he_loaded0"), HE_ROUNDS * 16 + 16)
                z_piece(HE_ROUNDS * 2, 0, 8, z[:, HE_ROUNDS * 16:HE_ROUNDS * 16 + 8])
                v.wait_ge(s("he_loaded1"), HE_ROUNDS * 16 + 32)
                z_piece(HE_ROUNDS * 2 + 1, 1, HE_REST - 7, z[:, HE_ROUNDS * 16 + 8:FULL + 1])

            stat = lambda t: t[:].unsqueeze(2).to_broadcast([P, NT, D])

            def layernorm(n):
                link(v.reduce_sum(mean[:], x[:], axis=AX.X))
                link(v.tensor_scalar(mean[:], mean[:], 1.0 / D, None, ALU.mult))
                link(v.tensor_tensor(h[:], x[:], stat(mean), ALU.subtract))
                link(v.tensor_tensor(G[:], h[:], h[:], ALU.mult))
                v.reduce_sum(var[:], G[:], axis=AX.X).then_inc(s("var_ready"), 1)
                v.wait_ge(s("std_ready"), n)
                link(v.reciprocal(var[:], var[:]))
                link(v.tensor_tensor(h[:], h[:], stat(var), ALU.mult))
                ins = v.tensor_scalar(h[:], h[:], 0.0, None, ALU.max)
                return ins

            def edge_round(j, i):
                name, width, key = PASSES[j]
                fam, b, n = FAMILY[j], BEFORE[j], DEPTH[j]
                tab = {"src": src_f, "dst": dst_f}[key]
                banks = ROW_BANKS[j]
                c1 = [i * n + k + 1 + b * NC for k in range(n)]

                def same_rows(k):
                    v.wait_ge(s(f"{fam}_key_row"), c1[k])
                    v.wait_ge(s(f"{fam}_comb_done"), c1[k])
                    key = tab[:, bass.ds(i * n + k, 1)]
                    row = bank[banks[k % len(banks)]][:, 0:P]
                    ins = v.tensor_scalar(same3[k] if name == "l3" else same[k][:], row, key, None, ALU.is_equal)
                    if name == "l3":
                        v.wait_ge(s("l3_same_ready"), c1[k] + (len(banks) - 2))
                        ins = v.scalar_tensor_tensor(scratch[k % 2][:], row, key, before[:],
                                                     ALU.is_equal, ALU.mult, accum_out=dup3[:, k:k + 1])
                    ins.then_inc(s(f"{fam}_same_ready"), 1)

                def message(k):
                    v.wait_ge(s(f"l0_gathered{k}"), i * 16 + 16)
                    v.scalar_tensor_tensor(raw[k][:, 0:D], raw[k][:, D:2 * D], z[:, bass.ds(i * K + k, 1)],
                                           raw[k][:, 0:D], ALU.mult, ALU.add).then_inc(s("message_ready"), 1)

                def targets(k):
                    part = slice(k - K + 1, k + 1)
                    keys = src_f[:, bass.ds(i * n + (k - K + 1), K)]
                    link(v.tensor_scalar(apart3[:, part], keys, discard_row[:], None, ALU.subtract))
                    v.wait_ge(s("l3_same_ready"), c1[k] + len(banks))
                    link(v.scalar_tensor_tensor(apart3[:, part], dup3[:, part], 1.0, apart3[:, part], ALU.min, ALU.mult))
                    for m in range(k - K + 1, k + 1):
                        v.wait_ge(s(f"l3_scattered{m}"), i * 16)
                    v.tensor_tensor(l3_idx[:, part], keys, apart3[:, part], ALU.subtract).then_inc(s("l3_idx_ready"), 1)

                for k in range(n):
                    same_rows(k)
                    if name == "l0" and k:
                        message(k - 1)
                    if name == "l3" and k % K == K - 1:
                        targets(k)
                if name == "l0":
                    message(n - 1)

            def sum_tables(j):
                name, fam, b = PASSES[j][0], FAMILY[j], BEFORE[j]
                for k in range(DEPTH[j]):
                    v.wait_ge(s(f"{fam}_loaded{k % 2}"), 16 * loads(j, k))
                    if name == "l0":
                        ops = [(G[:], ld[0]), (U[:], ld[1]), (cnt[:], ldc[:])]
                    elif name == "l3":
                        ops = [(G[:, :, 0:D48], ld[k % 2][:, :, 0:D48]), (cnt[:], ldc[:])]
                    else:
                        ops = [(G[:], ld[k % 2])]
                    for acc, part in ops:
                        link(v.tensor_copy(acc, part) if k == 0 else v.tensor_tensor(acc, acc, part, ALU.add))
                    v.sem_inc(s(f"{fam}_read"), 1)

            def edge_pass(j):
                with v.Fori(0, ROUNDS) as i:
                    edge_round(j, i)
                sum_tables(j)

            def one_hots(g, q):
                first = v.value_load(starts[0:1, bass.ds(g, 1)], min_val=0, max_val=NC)
                v.wait_ge(s("summed"), g + (TG - 1))
                six = bass.ds(first, CG)
                base = minus_base[:, bass.ds(g, 1)]
                q = q % 2
                v.tensor_scalar(pair_in[q], pair_key[:, six], base, None, ALU.add)
                v.scalar_tensor_tensor(dst_in[q], minus_group[:, six], base, key16["dst"][1][:, six], ALU.is_equal, ALU.mult)
                link(v.scalar_tensor_tensor(lo_in[q], minus_group[:, six], base, key16["src"][1][:, six], ALU.is_equal, ALU.mult))
                for k in range(CG):
                    v.tensor_scalar(pair_hot[q][:, k, :], count_key[:].rearrange("p a b -> p (a b)"), pair_in[q][:, k:k + 1], None,
                                    ALU.is_equal)
                v.tensor_tensor(dst_hot[q], io128f[:].unsqueeze(1).to_broadcast([P, CG, P]),
                                dst_in[q].unsqueeze(2).to_broadcast([P, CG, P]), ALU.is_equal)
                return v.tensor_tensor(lo_hot[q], io128[:].unsqueeze(1).to_broadcast([P, CG, P]),
                                       lo_in[q].unsqueeze(2).to_broadcast([P, CG, P]), ALU.is_equal)

            def power_of_two(t):
                link(v.tensor_scalar(t, t, 1e-30, None, ALU.max))
                link(v.tensor_scalar(t.bitcast(i32), t.bitcast(i32), 0x7F800000, None, ALU.bitwise_and))

            def split_rows(a):
                link(v.tensor_reduce(top2[:, 0, :], U[:, 0:SRC_T, :].rearrange("p t d -> p d t"), axis=AX.X, op=ALU.max,
                                     apply_absolute_value=True))
                link(v.tensor_copy(top2[:, 1, :], top2[:, 0, :]))
                v.sem_inc(s("top_ready"), 1)
                v.wait_ge(s("top_T"), a + 1)
                link(v.tensor_reduce(feature_top[:], bank[7][:, 0:P], axis=AX.X, op=ALU.max))
                power_of_two(feature_top[:])
                link(v.tensor_scalar(feature_top[:], feature_top[:], 2.0 ** -14, None, ALU.mult))
                link(v.tensor_scalar(unscale[:], twice[:], feature_top[:], None, ALU.mult))
                link(v.reciprocal(feature_inv[:], feature_top[:]))
                link(v.tensor_scalar(diag[:], ident[:], feature_inv[:], None, ALU.mult))
                v.sem_inc(s("diag_ready"), 1)
                v.wait_ge(s("scale_row_mm"), a + 1)
                link(v.tensor_copy(scale_row[:], bank[7][:, 0:D]))
                scaled = G[:, 0:SRC_T, :]
                link(v.tensor_tensor(scaled, U[:, 0:SRC_T, :], scale_row[:].unsqueeze(1).to_broadcast([P, SRC_T, D]), ALU.mult))
                link(v.tensor_copy(x16[:, :, 0:D], scaled))
                link(v.tensor_tensor(x16[:, :, D:2 * D], scaled, x16[:, :, 0:D], ALU.subtract))
                link(v.memset(G[:, 2 * NH:NT, :], 0))
                v.sem_inc(s("x16_ready"), 1)

            def agg(a):
                with v.If(flag2):
                    chains.append(fast)
                    split_rows(a)

                    def acc_copy(m, slot):
                        v.wait_ge(s("half_mm"), m + 3)
                        v.wait_ge(s("half_fin"), m + 1)
                        return v.tensor_copy(accT[slot][:], bank[slot][:, 0:HG * GN])
                    with v.Fori(0, NH // 2) as i:
                        for q in range(2):
                            acc_copy(i * 2 + (q + NH * a), q).then_inc(s("acc_read"), 1)
                    m, n = NH * a + NH - 1, (NG - (NH - 1) * HG) * GN
                    v.wait_ge(s("half_mm"), m + 3)
                    v.wait_ge(s("half_fin"), m + 1)
                    v.memset(accT[0][:, n:HG * GN], 0)
                    v.tensor_copy(accT[0][:, 0:n], bank[0][:, 0:n]).then_inc(s("acc_read"), 1)
                    v.wait_ge(s("half_out"), NH * (a + 1) + 2)
                    chains.pop()
                with v.Else():
                    chains.append(slow)
                    edge_pass(a + 1)
                    chains.pop()

            with ch.over(HE_ROUNDS, 2 + 8) as i:
                for q in range(2):
                    edge_round(7, i * 2 + q)
                    v.wait_ge(s(f"he_loaded{q}"), i * 16 + 16)
                    z_piece(i * 2 + q, q, 8, z[:, bass.ds((i * 2 + q) * 8, 8)])
            rest_of_z()
            for r in range(HE_ROUNDS * 2, ROUNDS3):
                edge_round(7, r)
            v.wait_ge(s("l3_idx_ready"), 2 * ROUNDS3)

            v.wait_ge(s("x_loaded"), 32)
            layernorm(1).then_inc(s("h_ready"), 1)
            v.wait_ge(s("small_loaded"), 16 * len(small))
            v.wait_ge(s("v_cols_ready"), 1)
            link(v.tensor_copy(v_sd[:, 0:1], v_cols[:, 0:1]))
            v.tensor_copy(v_sd[:, 1:2], v_cols[:, 2:3]).then_inc(s("v_sd_ready"), 1)
            v.wait_ge(s("h_ready"), 1)
            with ch.over(NB, 2 * BT) as b:
                v.wait_ge(s("h_T"), b)
                v.tensor_copy(stgh[:], h[:, bass.ds(b * BT, BT), :]).then_inc(s("h_staged"), 1)
                for q in range(BT):
                    v.wait_ge(s("rel_mm"), b * BT + q + 1)
                    v.wait_ge(s("rel_h"), b * BT + q + 1)
                    link(v.tensor_copy(s12[:, bass.ds(b * BT + q, 1), :], bank[3 + 3 * (q % 2)][:, 0:2].unsqueeze(1)))
                    link(v.tensor_tensor(rel_stage[q % 2][:, :, 0:D], rel_stage[q % 2][:, :, D:2 * D],
                                         s12[:, bass.ds(b * BT + q, 1), 0:1].to_broadcast([P, R, D]), ALU.mult))
                    v.sem_inc(s("rel_staged"), 1)

            v.wait_ge(s("starts_in"), 16)
            flag1 = v.value_load(flags[0:1, 0:1], min_val=0, max_val=1)
            with v.If(flag1):
                chains.append(fast)
                src_hi, src_lo = key16["src"]
                link(v.scalar_tensor_tensor(pair_key, src_hi[:], 512.0 / P, dst_f[:], ALU.mult, ALU.add))
                for lo in (src_lo, key16["dst"][1]):
                    link(v.tensor_scalar(lo[:], lo[:], 1.0, None, ALU.add))
                v.wait_ge(s("rel_ready"), 1)
                for t, value in ((ring, 1.0), (G[:, SRC_T:NT, :], 0.0), (U[:, SRC_T:NT, :], 0.0), (cnt[:, SRC_T:NT], 0.0)):
                    link(v.memset(t, value))
                v.sem_inc(s("ring_ready"), 1)
                node_i = flat3(G)[:, 0:NCT].bitcast(i32)
                link(v.tensor_copy(node_i, dst_f[:]))
                link(v.tensor_scalar(node_i, node_i, -GN, None, ALU.bitwise_and))
                link(v.tensor_copy(minus_group, node_i))
                link(v.tensor_scalar(minus_group, minus_group, -1.0, None, ALU.mult))
                def message_round(r, q, half):
                    v.wait_ge(s(f"ring_in{q % 2}"), half * (16 * K) + 16 * K)
                    for k in range(K):
                        row = ring[:, q * K + k, :]
                        ins = v.scalar_tensor_tensor(row[:, 0:D], row[:, D:2 * D], z[:, bass.ds(r * K + k, 1)], row[:, 0:D], ALU.mult, ALU.add)
                    return ins

                for r in range(LAG):
                    message_round(r, r, r // 2)
                with fast.over(NG // TG, TG) as b:
                    for q in range(TG):
                        one_hots(b * TG + q, q)
                        message_round(b * TG + (q + LAG), (q + LAG) % TG, b * (TG // 2) + (q + LAG) // 2).then_inc(s("hot_ready"), 1)
                for g in range(NG // TG * TG, NG):
                    ins = one_hots(g, g)
                    if g + LAG < ROUNDS:
                        ins = message_round(g + LAG, (g + LAG) % TG, (g + LAG) // 2)
                    ins.then_inc(s("hot_ready"), 1)
                v.wait_ge(s("adjacency_ready"), 1)
                link(v.tensor_reduce(over_sum[:], over, axis=AX.X, op=ALU.add))
                for lo in (src_lo, key16["dst"][1]):
                    link(v.tensor_scalar(lo[:], lo[:], 1.0, None, ALU.subtract))
                v.sem_inc(s("over_ready"), 1)
                v.wait_ge(s("over_mm"), 1)
                link(v.tensor_scalar(flags[:, 1:2], bank[7][0:1, 0:1], 0.5, None, ALU.is_lt))
                chains.pop()
            with v.Else():
                chains.append(slow)
                dup_dst = dup["dst"]
                link(v.memset(dup_dst, 0))
                with v.Fori(0, ROUNDS) as i:
                    for k in range(K):
                        v.wait_ge(s("dup_row"), i * K + k + 1)
                        col = bass.ds(i * K + k, 1)
                        v.wait_ge(s("dup_done"), i * K + k + 3)
                        v.scalar_tensor_tensor(scratch[k % 2][:], bank[k][:, 0:P], dst_f[:, col], before[:],
                                               ALU.is_equal, ALU.mult, accum_out=dup_dst[:, col]).then_inc(s("dup_done"), 1)
                v.wait_ge(s("dup_done"), K + NC)
                tmpf = idx_f.rearrange("p t c -> p (t c)")
                link(v.tensor_scalar(tmpf, dst_f[:], discard_row[:], None, ALU.subtract))
                link(v.tensor_scalar(dup_dst, dup_dst, 1.0, None, ALU.min))
                link(v.tensor_tensor(tmpf, tmpf, dup_dst, ALU.mult))
                link(v.tensor_tensor(dst_first[:], dst_f[:], tmpf, ALU.subtract))
                v.sem_inc(s("dst_first_ready"), 1)
                with v.Fori(0, ROUNDS) as i:
                    edge_round(0, i)
                sum_tables(0)
                link(v.memset(flags[:, 1:2], 0))
                chains.pop()
            v.sem_inc(s("flag2_ready"), 1)
            flag2 = v.value_load(flags[0:1, 1:2], min_val=0, max_val=1)
            link(v.tensor_tensor(U[:], U[:], s12[:, :, 1:2].to_broadcast([P, NT, D]), ALU.mult))
            link(v.tensor_tensor(G[:], G[:], U[:], ALU.add))
            link(v.tensor_scalar(G[:], G[:], 0.0, None, ALU.max))
            link(v.tensor_tensor(x[:], x[:], G[:], ALU.add))
            link(v.tensor_scalar(cnt[:], cnt[:], 1.0, None, ALU.add))
            link(layernorm(2))
            v.tensor_copy(U[:], h[:]).then_inc(s("u_ready"), 1)
            v.wait_ge(s("u_ready"), 1)
            agg(0)
            v.tensor_scalar(U[:], G[:], 0.0, None, ALU.max).then_inc(s("u_ready"), 1)
            v.wait_ge(s("u_ready"), 2)
            agg(1)
            link(v.tensor_tensor(x[:], x[:], G[:], ALU.add))
            link(layernorm(3))
            v.sem_inc(s("deg_ready"), 1)
            v.wait_ge(s("deg_sqrt"), 1)
            link(v.reciprocal(dinv[:], dinv[:]))
            v.tensor_tensor(U[:], h[:], stat(dinv), ALU.mult).then_inc(s("u_ready"), 1)

            def gcn_sum(j):
                v.wait_ge(s("u_ready"), j)
                agg(j - 1)
                link(v.tensor_tensor(G[:], G[:], U[:], ALU.add))
                return v.tensor_tensor(G[:], G[:], stat(dinv), ALU.mult)

            def dense(n):
                m0 = n * NB

                def transposed(b):
                    v.wait_ge(s("dense_T"), b + (1 + m0))
                    v.tensor_copy(vT[:], bank[0][0:D, :]).then_inc(s("dense_vT"), 1)

                def hidden(b):
                    v.wait_ge(s("dense_relu"), b + (1 + m0))
                    blk = bass.ds(b * 512, 512)
                    if n == 0:
                        link(v.tensor_copy(hid_T[:, blk], xs[:]))
                        v.sem_inc(s("dense_x"), 1)
                    else:
                        v.tensor_tensor(xs[:], xs[:], hid_T[:, blk], ALU.add).then_inc(s("dense_x"), 1)

                def to_u(b):
                    v.wait_ge(s("dense_mm2"), b + (1 + m0))
                    v.tensor_tensor(U[:, bass.ds(b * BT, BT), :], bank[2][:, 0:BT * D].rearrange("p (t d) -> p t d", d=D),
                                    dinv[:, bass.ds(b * BT, BT)].unsqueeze(2).to_broadcast([P, BT, D]),
                                    ALU.mult).then_inc(s("dense_u"), 1)
                transposed(0)
                with ch.over(NB - 1, 1 - n) as b:
                    hidden(b)
                    transposed(b + 1)
                    to_u(b)
                hidden(NB - 1)
                to_u(NB - 1)
                v.wait_ge(s("dense_u"), (n + 1) * NB)
                v.sem_inc(s("u_ready"), 1)

            gcn_sum(3).then_inc(s("g_ready"), 1)
            dense(0)
            link(gcn_sum(4))
            link(v.tensor_tensor(G[:], G[:], g_b2[:].unsqueeze(1).to_broadcast([P, NT, D]), ALU.add))
            link(v.tensor_scalar(G[:], G[:], 0.0, None, ALU.max))
            v.tensor_tensor(U[:], G[:], stat(dinv), ALU.mult).then_inc(s("u_ready"), 1)
            gcn_sum(5).then_inc(s("g_ready"), 1)
            dense(1)
            link(gcn_sum(6))
            link(v.tensor_tensor(G[:], G[:], g_b4[:].unsqueeze(1).to_broadcast([P, NT, D]), ALU.add))
            link(v.tensor_scalar(G[:], G[:], 0.0, None, ALU.max))
            link(v.tensor_tensor(G[:], G[:], h[:], ALU.add))
            link(v.tensor_tensor(x[:], x[:], G[:], ALU.add))
            v.sem_inc(s("l3_sums_wanted"), 1)
            link(layernorm(4))
            sum_tables(7)
            link(v.tensor_scalar(cnt[:], cnt[:], 1.0, None, ALU.max))
            link(v.reciprocal(cnt[:], cnt[:]))
            v.tensor_tensor(ld[0][:, :, 0:D48], G[:, :, 0:D48], cnt[:].unsqueeze(2).to_broadcast([P, NT, D48]),
                            ALU.mult).then_inc(s("ve_ready"), 1)
            v.wait_ge(s("ve_ready"), 1)

            def transposed(b):
                v.wait_ge(s("mlp_T"), b + 1)
                link(v.tensor_copy(vT[:], bank[0][0:D, :]))
                v.tensor_copy(veT, bank[1][0:D48, :]).then_inc(s("mlp_vT"), 1)

            def result(b):
                v.wait_ge(s("mlp_mm3"), b + 1)
                blk = bass.ds(b * BT, BT)
                v.tensor_tensor(G[:, blk, :], bank[4][:, 0:BT * D].rearrange("p (t d) -> p t d", d=D), x[:, blk, :],
                                ALU.add).then_inc(s("mlp_y"), 1)
            transposed(0)
            with ch.over(NB - 1, 1) as b:
                transposed(b + 1)
                result(b)
            result(NB - 1)
            v.wait_ge(s("mlp_y"), NB)
            v.tensor_tensor(G[:], G[:], m_b3[:].unsqueeze(1).to_broadcast([P, NT, D]), ALU.add).then_inc(s("out_ready"), 1)

        @block.tensor
        def _(pe):
            for fam, n in (("l0", K), ("agg", K), ("l3", K3)):
                pe.sem_inc(s(f"{fam}_comb_done"), n)
            pe.sem_inc(s("half_mm"), 2)
            pe.sem_inc(s("summed"), TG)
            pe.sem_inc(s("half_fin"), 2)
            pe.wait_ge(s("const_ready"), 1)
            pe.wait_ge(s("small_loaded"), 16 * len(small))
            pe.matmul(bank[4][0:D, 0:3], w_shared[:], w_attn[:], start=True, stop=True)
            pe.matmul(bank[5][:, 0:D], w_attn[:, 1:2].to_broadcast([D, P]), w_shared[:], start=True, stop=True).then_inc(s("ve_mm"), 1)
            groups = [(g, min(4, ET - g * 4)) for g in range(-(-ET // 4))]
            for n in range(3):
                pe.wait_ge(s("idx_cast"), n + 1)
                for g, w in groups:
                    for t in range(w):
                        ins = pe.transpose(bank[g][:, t * P:t * P + P], idx_f[:, g * 4 + t, :], ident[:])
                    ins.then_inc(s("idx_T"), 1)
            pe.wait_ge(s("keys_ready"), 1)
            for m, row in enumerate((P - 1, 0)):
                if m:
                    pe.wait_ge(s("edge_row_read"), m)
                for g, w in groups:
                    ins = pe.matmul(bank[g][:, 0:w * P], ident[:, row:row + 1].to_broadcast([P, P]), dst_f[:, g * 512:g * 512 + w * P],
                                    start=True, stop=True)
                ins.then_inc(s("edge_row"), 1)
            pe.wait_ge(s("verdict_ready"), 1)
            pe.matmul(bank[7][:, 0:1], ones[:], verdict[:, 3:4], start=True, stop=True).then_inc(s("verdict_mm"), 1)
            pe.wait_ge(s("v_cols_ready"), 1)

            def key_row(dst_bank, name, col):
                hi, lo = key16[name]
                pe.matmul(dst_bank[:, 0:P], hi[:, col].to_broadcast([P, P]), ident16[:], start=True, stop=False)
                return pe.matmul(dst_bank[:, 0:P], lo[:, col].to_broadcast([P, P]), ident16[:], start=False, stop=True)

            def edge_round(j, i):
                name, width, key = PASSES[j]
                fam, b = FAMILY[j], BEFORE[j]
                src_buf = raw3 if name == "l3" else raw
                banks = ROW_BANKS[j]
                n = DEPTH[j]
                c1 = [i * n + k + 1 + b * NC for k in range(n)]

                def row(k):
                    pe.wait_ge(s(f"{fam}_same_ready"), c1[k])
                    key_row(bank[banks[k % len(banks)]], key, bass.ds(i * n + k, 1)).then_inc(s(f"{fam}_key_row"), 1)

                def combine(k):
                    pe.wait_ge(s(f"{fam}_same_ready"), c1[k] + len(banks))
                    if name == "l0":
                        pe.wait_ge(s("message_ready"), c1[k])
                    elif name == "l3":
                        if k % K == 0:
                            pe.wait_ge(s(f"edges_loaded{k // K}"), i * 16 + 16)
                    else:
                        pe.wait_ge(s(f"agg_gathered{k}"), i * 16 + 16 * (1 + b * ROUNDS))
                    pe.wait_ge(s(f"{fam}_comb_ready"), c1[k])
                    pe.matmul(bank[2 + k % 2][:, 0:width], same3[k] if name == "l3" else same[k][:], src_buf[k][:, 0:width],
                              start=True, stop=True).then_inc(s(f"{fam}_comb_done"), 1)
                for k in range(len(banks)):
                    row(k)
                for k in range(n):
                    combine(k)
                    if k + len(banks) < n:
                        row(k + len(banks))

            def edge_pass(j):
                with pe.Fori(0, COUNT[j] // DEPTH[j]) as i:
                    edge_round(j, i)

            edge_pass(7)
            pe.wait_ge(s("l3_comb_ready"), NC3 + 2)

            pe.wait_ge(s("v_sd_ready"), 1)
            with pe.Fori(0, NB) as b:
                pe.wait_ge(s("h_staged"), b + 1)
                pe.wait_ge(s("hT_ready"), b)
                pe.sem_inc(s("pe_turn"), 1)
                for q in range(BT):
                    ins = pe.transpose(bank[0][0:D, q * P:q * P + P], stgh[:, q, :], ident[:])
                ins.then_inc(s("h_T"), 1)
                pe.wait_ge(s("hT_ready"), b + 1)
                for q in range(BT):
                    pe.wait_ge(s("rel_staged"), b * BT + q)
                    tile = hT[:, q * P:q * P + P]
                    b1, b2, b3 = (bank[n + 3 * (q % 2)] for n in (1, 2, 3))
                    pe.matmul(b1[:], tile, w_rel[:, 0:8, :].rearrange("i r o -> i (r o)"), start=True, stop=True)
                    pe.matmul(b2[:], tile, w_rel[:, 8:16, :].rearrange("i r o -> i (r o)"), start=True, stop=True)
                    pe.matmul(b3[:, 0:2], tile, v_sd[:], start=True, stop=True).then_inc(s("rel_mm"), 1)
            pe.wait_ge(s("rel_staged"), NT + 1)

            def sum_group(g, q, last, tile):
                first = pe.value_load(starts[0:1, bass.ds(g, 1)], min_val=0, max_val=NC)
                pe.wait_ge(s("hot_ready"), g + 1)
                pe.wait_ge(s("counts_read"), g)
                b0, b1 = (bank[n] for n in count_bank[q % 2])
                w0 = A_SPLIT * GN
                for k in range(CG):
                    pe.matmul(b0[:, 0:w0], lo_hot[q % 2][:, k, :], pair_hot[q % 2][:, k, 0:w0], start=k == 0, stop=k == CG - 1)
                    pe.matmul(b1[:, 0:GW - w0], lo_hot[q % 2][:, k, :], pair_hot[q % 2][:, k, w0:GW], start=k == 0, stop=k == CG - 1)
                if q == 0:
                    pe.wait_ge(s("tile_out"), tile)
                for k in range(CG):
                    ins = pe.matmul(bank[6][:, 0:RW], dst_hot[q % 2][:, k, :], ring[:, bass.ds((first + k) & (RING - 1), 1), :].rearrange("p a w -> p (a w)"),
                                    start=q == 0 and k == 0, stop=last and k == CG - 1)
                ins.then_inc(s("summed"), 1)

            pe.wait_ge(s("flag1_ready"), 1)
            flag1 = pe.value_load(flags[0:1, 0:1], min_val=0, max_val=1)
            with pe.If(flag1):
                pe.wait_ge(s("starts_in"), 16)
                with pe.Fori(0, NG // TG) as b:
                    for q in range(TG):
                        sum_group(b * TG + q, q, q == TG - 1, b)
                for g in range(NG // TG * TG, NG):
                    sum_group(g, g % TG, g == NG - 1, NG // TG)
                pe.wait_ge(s("over_ready"), 1)
                pe.matmul(bank[7][:, 0:1], ones[:], over_sum[:], start=True, stop=True).then_inc(s("over_mm"), 1)
            with pe.Else():
                with pe.Fori(0, ROUNDS) as i:
                    for k in range(K):
                        pe.wait_ge(s("dup_done"), i * K + k + 1)
                        key_row(bank[k], "dst", bass.ds(i * K + k, 1)).then_inc(s("dup_row"), 1)
                pe.wait_ge(s("dst_first_ready"), 1)
                edge_pass(0)
            pe.wait_ge(s("flag2_ready"), 1)
            flag2 = pe.value_load(flags[0:1, 1:2], min_val=0, max_val=1)

            def agg(a):
                with pe.If(flag2):
                    pe.wait_ge(s("top_ready"), a + 1)
                    pe.transpose(bank[7][:, 0:P], top2[:].rearrange("p m d -> p (m d)"), ident[:]).then_inc(s("top_T"), 1)
                    pe.wait_ge(s("diag_ready"), a + 1)
                    pe.matmul(bank[7][:, 0:D], ones[0:D, :], diag[0:D, 0:D], start=True, stop=True).then_inc(s("scale_row_mm"), 1)
                    pe.wait_ge(s("x16_ready"), a + 1)

                    def multiply(m, slot, loads, n=HG):
                        pe.wait_ge(s(f"half_in{slot}"), loads)
                        pe.wait_ge(s("acc_read"), m + 1)
                        pe.sem_inc(s("pe_turn"), 1)
                        for t in range(SRC_T):
                            ins = pe.matmul(bank[slot][:, 0:n * GN].rearrange("p (g d) -> p g d", d=GN), x16[:, t, :],
                                            a_half[slot][:, 0:n, t * GN:(t + 1) * GN], start=t == 0, stop=t == SRC_T - 1)
                        ins.then_inc(s("half_mm"), 1)

                    def finalize(m, slot):
                        pe.wait_ge(s("acc_read"), m + 3)
                        pe.wait_ge(s("half_out"), m + 1)
                        for q in range(2):
                            ins = pe.matmul(bank[2 + slot][:, q * D:(q + 1) * D], accT[slot][:, q * P:(q + 1) * P], unscale[:],
                                            start=True, stop=True)
                        ins.then_inc(s("half_fin"), 1)

                    m0, in0, in1 = NH * a, (NH // 2 + 1) * a, NH // 2 * a
                    multiply(m0, 0, 16 * (in0 + 1))
                    with pe.Fori(0, NH // 2 - 1) as i:
                        multiply(i * 2 + (m0 + 1), 1, i * 16 + 16 * (in1 + 1))
                        finalize(i * 2 + m0, 0)
                        multiply(i * 2 + (m0 + 2), 0, i * 16 + 16 * (in0 + 2))
                        finalize(i * 2 + (m0 + 1), 1)
                    multiply(m0 + NH - 2, 1, 16 * (in1 + NH // 2))
                    finalize(m0 + NH - 3, 0)
                    multiply(m0 + NH - 1, 0, 16 * (in0 + NH // 2 + 1), NG - (NH - 1) * HG)
                    finalize(m0 + NH - 2, 1)
                    finalize(m0 + NH - 1, 0)
                with pe.Else():
                    edge_pass(a + 1)

            for a in range(3):
                agg(a)

            def dense(n, wa, wb):
                m0 = n * NB

                def transpose(b):
                    pe.wait_ge(s("dense_staged"), b + (1 + m0))
                    pe.sem_inc(s("pe_turn"), 1)
                    for q in range(BT):
                        ins = pe.transpose(bank[0][0:D, q * P:q * P + P], stg[:, q, :], ident[:])
                    ins.then_inc(s("dense_T"), 1)

                def first(b):
                    pe.wait_ge(s("dense_vT"), b + (1 + m0))
                    pe.matmul(bank[1][:], wa[:], vT[:], start=True, stop=True).then_inc(s("dense_mm1"), 1)

                def second(b):
                    pe.wait_ge(s("dense_x"), b + (1 + m0))
                    pe.wait_ge(s("dense_u"), b + m0)
                    for q in range(BT):
                        ins = pe.matmul(bank[2][:, q * D:q * D + D], xs[:, q * P:q * P + P], wb[:], start=True, stop=True)
                    ins.then_inc(s("dense_mm2"), 1)
                transpose(0)
                with pe.Fori(0, NB - 1) as b:
                    first(b)
                    transpose(b + 1)
                    second(b)
                first(NB - 1)
                second(NB - 1)

            dense(0, g_w1, g_w2)
            agg(3)
            agg(4)
            dense(1, g_w3, g_w4)
            agg(5)
            pe.matmul(bank[0][:, 0:1], m_w1u[:], m_u[:], start=True, stop=True).then_inc(s("u_bias_mm"), 1)
            pe.wait_ge(s("c1_ready"), 1)

            def transpose(b):
                pe.wait_ge(s("mlp_staged"), b + 1)
                pe.sem_inc(s("pe_turn"), 1)
                for q in range(BT):
                    pe.transpose(bank[0][0:D, q * P:q * P + P], stg[:, q, :], ident[:])
                for q in range(BT):
                    ins = pe.transpose(bank[1][0:D48, q * P:q * P + P], stg_e[:, q, :], ident[:])
                ins.then_inc(s("mlp_T"), 1)

            def first(b):
                pe.wait_ge(s("mlp_vT"), b + 1)
                pe.matmul(bank[2][:], m_w1x[:], vT[:], start=True, stop=False)
                pe.matmul(bank[2][:], m_w1e[:], veT, start=False, stop=True).then_inc(s("mlp_mm1"), 1)

            def rest(b):
                pe.wait_ge(s("mlp_h1"), b + 1)
                pe.matmul(bank[3][:], m_w2[:], xs[:], start=True, stop=True).then_inc(s("mlp_mm2"), 1)
                pe.wait_ge(s("mlp_h2"), b + 1)
                pe.wait_ge(s("mlp_y"), b)
                for q in range(BT):
                    ins = pe.matmul(bank[4][:, q * D:q * D + D], xs2[:, q * P:q * P + P], m_w3[:], start=True, stop=True)
                ins.then_inc(s("mlp_mm3"), 1)
            transpose(0)
            with pe.Fori(0, NB - 1) as b:
                first(b)
                transpose(b + 1)
                rest(b)
            first(NB - 1)
            rest(NB - 1)


_INS = ["x", "src", "dst", "edge_attr_48", "edge_attr_64", "edge_type_16", "L0_gnn_W_shared", "L0_gnn_W_attn", "L0_gnn_W_rel",
        "L2_gnn_W1", "L2_gnn_b1", "L2_gnn_W2", "L2_gnn_b2", "L2_gnn_W3", "L2_gnn_b3", "L2_gnn_W4", "L2_gnn_b4",
        "L3_gnn_u", "L3_gnn_W1", "L3_gnn_b1", "L3_gnn_W2", "L3_gnn_b2", "L3_gnn_W3", "L3_gnn_b3"]


def kernel(**inputs):
    import numpy as _np
    import concourse.bacc as _bacc
    from concourse import mybir as _mybir
    from concourse.bass_utils import run_bass_kernel_spmd as _run

    nc = _bacc.Bacc("TRN2", target_bir_lowering=False, num_devices=1)
    arrays, aps = {}, {}
    for name in _INS:
        a = _np.ascontiguousarray(inputs[name])
        arrays[f"in_{name}"] = a
        aps[name] = nc.dram_tensor(f"in_{name}", a.shape, _mybir.dt.from_np(a.dtype), kind="ExternalInput").ap()
    out = nc.dram_tensor("out_0", (N, D), _mybir.dt.float32, kind="ExternalOutput").ap()
    build(nc, aps, out)
    r = _run(nc, [arrays], core_ids=[0])
    return r.results[0]["out_0"]
```
